# Optimizing a Trainium2 kernel written in Bass

```python
import numpy as np
import jax
import jax.numpy as jnp

def _softmax(x, axis=-1):
    return jax.nn.softmax(x, axis=axis)

def _gelu(x):
    return jax.nn.gelu(x, approximate=True)

def _silu(x):
    return jax.nn.silu(x)

def _sigmoid(x):
    return jax.nn.sigmoid(x)

def _layernorm(x, axis=-1, eps=1e-05):
    m = jnp.mean(x, axis=axis, keepdims=True)
    v = jnp.var(x, axis=axis, keepdims=True)
    return (x - m) / jnp.sqrt(v + eps)

def _scatter_add(tgt, idx, src, axis=0):
    return tgt.at[idx].add(src)

def _segment_sum(src, seg, n):
    return jax.ops.segment_sum(src, seg, n)
kernel_name = 'mk_prb_d1_jaxref_r4_2a484f'

def setup_inputs(seed: int=0):
    np.random.seed(seed)
    _w = jnp.asarray

    def _L0_attn_setup():
        import jax, jax.numpy as jnp
        import numpy as np
        N_HEADS = 16
        D_MODEL = 256
        SEQ_LEN = 512
        BATCH = 4
        key = jax.random.key(seed)
        k1, k2, k3 = jax.random.split(key, 3)
        std = 1.0 / np.sqrt(D_MODEL)
        x = jax.random.normal(k1, (BATCH, SEQ_LEN, D_MODEL), dtype=jnp.float32)
        w_qkv = std * jax.random.normal(k2, (D_MODEL, 3 * D_MODEL), dtype=jnp.float32)
        w_o = std * jax.random.normal(k3, (D_MODEL, D_MODEL), dtype=jnp.float32)
        return {'x': x, 'w_qkv': w_qkv, 'w_o': w_o}
    _L0_attn_in = _L0_attn_setup()

    def _L0_ffn_setup():
        import jax, jax.numpy as jnp
        import numpy as np
        B, T, C, E, K, CAP, H = (8, 512, 256, 8, 2, 1024, 1024)
        key = jax.random.key(seed)
        ks = jax.random.split(key, 6)
        s = 0.02
        return {'x': jax.random.normal(ks[0], (B, T, C), jnp.float32), 'rw1': s * jax.random.normal(ks[1], (C, H), jnp.float32), 'rb1': jnp.zeros((H,), jnp.float32), 'rw2': s * jax.random.normal(ks[2], (H, E), jnp.float32), 'rb2': jnp.zeros((E,), jnp.float32), 'ew1': s * jax.random.normal(ks[3], (E, C, H), jnp.float32), 'eb1': jnp.zeros((E, H), jnp.float32), 'ew2': s * jax.random.normal(ks[4], (E, H, C), jnp.float32), 'eb2': jnp.zeros((E, C), jnp.float32)}
    _L0_ffn_in = _L0_ffn_setup()
    _d = {'L0_attn_x': _L0_attn_in['x'], 'L0_attn_w_qkv': _L0_attn_in['w_qkv'], 'L0_attn_w_o': _L0_attn_in['w_o'], 'L0_ffn_rw1': _L0_ffn_in['rw1'], 'L0_ffn_rb1': _L0_ffn_in['rb1'], 'L0_ffn_rw2': _L0_ffn_in['rw2'], 'L0_ffn_rb2': _L0_ffn_in['rb2'], 'L0_ffn_ew1': _L0_ffn_in['ew1'], 'L0_ffn_eb1': _L0_ffn_in['eb1'], 'L0_ffn_ew2': _L0_ffn_in['ew2'], 'L0_ffn_eb2': _L0_ffn_in['eb2']}
    _x0 = _d['L0_attn_x']
    _d['L0_attn_x'] = jax.random.normal(jax.random.fold_in(jax.random.key(seed), 1), (8, 1024, 256), dtype=_x0.dtype)
    del _x0
    return _d

def reference(L0_attn_x, L0_attn_w_qkv, L0_attn_w_o, L0_ffn_rw1, L0_ffn_rb1, L0_ffn_rw2, L0_ffn_rb2, L0_ffn_ew1, L0_ffn_eb1, L0_ffn_ew2, L0_ffn_eb2):

    def _L0_attn_ref(x, w_qkv, w_o):
        import jax, jax.numpy as jnp
        import numpy as np
        N_HEADS = 16
        D_MODEL = 256
        SEQ_LEN = 512
        BATCH = 4
        *lead, seq_len, d_model = x.shape
        head_dim = d_model // N_HEADS
        qkv = x @ w_qkv
        qkv = qkv.reshape(*qkv.shape[:-1], N_HEADS, 3 * head_dim)
        qkv = jnp.einsum('...Thd->...hTd', qkv)
        q, k, v = jnp.split(qkv, 3, axis=-1)
        scores = jnp.einsum('...hqd,...hkd->...hqk', q, k) / np.sqrt(d_model).astype(x.dtype)
        causal = jnp.tri(seq_len, dtype=bool)
        scores = jnp.where(causal, scores, jnp.asarray(-1e+30, dtype=scores.dtype))
        attn = jax.nn.softmax(scores, axis=-1)
        out = jnp.einsum('...hqk,...hkd->...qhd', attn, v)
        out = out.reshape(*out.shape[:-2], d_model)
        return out @ w_o

    def _L0_ffn_ref(x, rw1, rb1, rw2, rb2, ew1, eb1, ew2, eb2):
        import jax, jax.numpy as jnp
        import numpy as np
        B, T, C, E, K, CAP, H = (8, 512, 256, 8, 2, 1024, 1024)
        Bx, Tx, Cx = x.shape
        N = Bx * Tx
        logits = jax.nn.relu(x @ rw1 + rb1) @ rw2 + rb2
        vals, ids = jax.lax.top_k(logits, K)
        probs = jax.nn.softmax(vals, axis=-1)
        ids_f = ids.reshape(N * K)
        probs_f = probs.reshape(N * K)
        xr = jnp.repeat(x.reshape(N, Cx), K, axis=0)
        m = jax.nn.one_hot(ids_f, E, dtype=jnp.int32)
        pos = jnp.cumsum(m, axis=0) - 1
        pos_tok = jnp.take_along_axis(pos, ids_f[:, None], axis=1)[:, 0]
        keep = (pos_tok < CAP).astype(x.dtype)
        pos_c = jnp.clip(pos_tok, 0, CAP - 1)
        disp = jnp.zeros((E, CAP, Cx), x.dtype).at[ids_f, pos_c].add(xr * keep[:, None])
        h = jax.nn.relu(jnp.einsum('enc,ech->enh', disp, ew1) + eb1[:, None, :])
        eo = jnp.einsum('enh,ehc->enc', h, ew2) + eb2[:, None, :]
        y = eo[ids_f, pos_c] * (probs_f * keep)[:, None]
        return y.reshape(Bx, Tx, K, Cx).sum(axis=2)
    x = L0_attn_x
    xn = _layernorm(x, axis=-1)
    x = x + _L0_attn_ref(xn, L0_attn_w_qkv, L0_attn_w_o) + _L0_ffn_ref(xn, L0_ffn_rw1, L0_ffn_rb1, L0_ffn_rw2, L0_ffn_rb2, L0_ffn_ew1, L0_ffn_eb1, L0_ffn_ew2, L0_ffn_eb2)
    return x

_drawn_inputs = setup_inputs


def setup_inputs(seed=0):
    import zlib

    import numpy as np

    out = dict(_drawn_inputs(seed))
    spreads = {'L0_ffn_rb1': (0.0, 0.1),
     'L0_ffn_rb2': (0.0, 0.1),
     'L0_ffn_eb1': (0.0, 0.423),
     'L0_ffn_eb2': (0.0, 0.1)}
    factors = {}
    for name, (base, spread) in spreads.items():
        noise = np.random.default_rng([zlib.crc32(name.encode()), seed]).standard_normal(out[name].shape)
        drawn = base * np.exp(spread * noise) if base else spread * noise
        out[name] = jnp.asarray(drawn.astype(out[name].dtype))
    for name, factor in factors.items():
        out[name] = (out[name] * factor).astype(out[name].dtype)
    return out
```

```python
from contextlib import ExitStack

import concourse.bass as bass
from concourse import mybir

F32 = mybir.dt.float32
F32R = mybir.dt.float32r
BF16 = mybir.dt.bfloat16
U32 = mybir.dt.uint32
I32 = mybir.dt.int32
ALU = mybir.AluOpType
ACT = mybir.ActivationFunctionType
AX = mybir.AxisListType.X

P = 128
BIG = 1.0e30
EPS = 1e-5
PARTS = 3
TERMS_Q = (0, 0, 0, 1, 1, 2)
TERMS_K = (0, 1, 2, 0, 1, 0)


def layer_kernel(nc, x, w_qkv, w_o, rw1, rb1, rw2, rb2, ew1, eb1, ew2, eb2, out):
    B, T, C = x.shape
    N = B * T
    H = rw1.shape[1]
    E = rw2.shape[1]
    CAP = 1024
    NH, DH = 16, 16
    KC = C // P
    MH = H // P
    BLK = 512
    TB = BLK // P
    HG = 4
    NG = NH // HG
    U = B * NG
    KT = T // P
    NT = len(TERMS_Q)
    KR = NT * DH
    ROW = 272
    TOKC, PVC = C, C + 4
    CH = 256
    assert (C, H, E, T, B) == (256, 1024, 8, 1024, 8) and N // BLK == 2 * B

    acc = nc.dram_tensor("acc", (N + P, C), F32).ap()
    disp = nc.dram_tensor("disp", (E * CAP, ROW), F32).ap()
    qkd = nc.dram_tensor("qk_parts", (B, 2, PARTS, 2, C, 512), BF16).ap()
    vhd = nc.dram_tensor("v_ones", (B, NG, P, KT, HG * 32), F32).ap()

    ctx = ExitStack()
    with ctx:
        def sb(name, shape, dt=F32, stack=ctx):
            return stack.enter_context(nc.sbuf_tensor(name, shape, dt))

        def sem(name):
            return ctx.enter_context(nc.semaphore(name))

        ident = sb("ident", [P, P])
        identb = sb("identb", [P, P], BF16)
        mask_qk = sb("mask_qk", [P, P], BF16)
        mask_kq = sb("mask_kq", [P, P], BF16)
        before = sb("before", [P, P], BF16)
        onesb = sb("onesb", [P, P], BF16)
        sum4 = sb("sum4", [P, E])
        wo = sb("wo", [P, NG, C])
        biasT = sb("biasT", [P, 9 * MH])
        RB = 8 * MH
        phase = sem("phase")

        banks = [ctx.enter_context(nc.psum_tensor(f"bank{i}", [P, 512], F32)) for i in range(8)]

        p1 = ExitStack()
        stage = sb("stage", [P, KC, H], stack=p1)
        wqs = sb("wqs", [P, KC, 3 * C], stack=p1)
        brow = sb("brow", [9 * MH, P], stack=p1)
        rw1h = sb("rw1h", [P, KC, H], F32R, p1)
        rw1l = sb("rw1l", [P, KC, H], F32R, p1)
        wqh = sb("wqh", [P, KC, 3 * C], F32R, p1)
        wql = sb("wql", [P, KC, 3 * C], F32R, p1)
        rw2p = sb("rw2p", [P, MH, 32], F32, p1)
        rb2b = sb("rb2b", [P, E], F32, p1)
        fill = sb("fill", [P, 8, ROW], F32, p1)
        xb = [sb(f"xb{i}", [P, TB, C], F32, p1) for i in range(2)]
        xn = [sb(f"xn{i}", [P, TB, ROW], F32, p1) for i in range(2)]
        xTh = [sb(f"xTh{i}", [P, KC, BLK], F32R, p1) for i in range(2)]
        xTl = [sb(f"xTl{i}", [P, KC, BLK], F32R, p1) for i in range(2)]
        hT = sb("hT", [P, MH, BLK], F32, p1)
        ltp = sb("ltp", [P, BLK], F32, p1)
        qst = [sb(f"qst{i}", [P, PARTS, BLK], BF16, p1) for i in range(4)]
        res = [sb(f"res{i}", [P, BLK], F32, p1) for i in range(4)]
        vst = sb("vst", [P, TB, NH, 32], F32, p1)
        stats = sb("stats", [P, TB, 6], F32, p1)
        mv = sb("mv", [P, TB, 2], F32, p1)
        veps = sb("veps", [P, TB], F32, p1)
        rstd = sb("rstd", [P, TB], F32, p1)
        minus_half = sb("minus_half", [P, TB], F32, p1)
        small = {n: sb(n, [P, TB, E], F32, p1) for n in
                 ("lg", "lg2", "eq", "oh0", "oh1", "cand", "pv0", "pv1", "iota8", "slotbase", "place", "over", "sel0", "sel1")}
        one = {n: sb(n, [P, TB], F32, p1) for n in
               ("top0", "top1", "f0", "f1", "gap", "egap", "den2", "w0", "w1", "tokf")}
        m8 = sb("m8", [P, TB, E], BF16, p1)
        msum = sb("msum", [P, E], F32, p1)
        carry = sb("carry", [P, E], BF16, p1)
        slotf = [sb(f"slotf{i}", [P, 2, TB], F32, p1) for i in range(2)]
        slot = [sb(f"slot{i}", [P, 2 * TB], U32, p1) for i in range(2)]
        p1.close()

        p2 = ctx
        qs = [sb(f"qs{i}", [P, 2, HG, 512], BF16, p2) for i in range(4)]
        ks = [sb(f"ks{i}", [P, 2, HG, 512], BF16, p2) for i in range(4)]
        vh = [sb(f"vh{i}", [P, KT, HG, 32], F32, p2) for i in range(2)]
        pt = [sb(f"pt{i}", [P, HG, 512], F32, p2) for i in range(2)]
        attT = sb("attT", [P, NG, T], F32, p2)
        den = sb("den", [P, 512], F32, p2)
        rden = sb("rden", [P, 512], F32, p2)
        rsum = sb("rsum", [P, 16], F32, p2)
        mxA = [sb(f"mxA{i}", [P, HG, 4], F32, p2) for i in range(2)]
        mxB = [sb(f"mxB{i}", [P, HG, 4, 2], F32, p2) for i in range(2)]
        mxBr = sb("mxBr", [P, HG * 4], F32, p2)
        nm = sb("nm", [16, P], F32, p2)
        nmr = sb("nmr", [16, P], F32, p2)
        mparts = [sb(f"mparts{i}", [16, PARTS, P], BF16, p2) for i in range(2)]
        wstage = sb("wstage", [P, 2048], F32, p2)
        w1h = sb("w1h", [P, 2048], F32R, p2)
        w1l = sb("w1l", [P, 2048], F32R, p2)
        w2h = sb("w2h", [P, 2048], F32R, p2)
        w2l = sb("w2l", [P, 2048], F32R, p2)
        ebias = sb("ebias", [P, MH], F32, p2)
        eb2b = sb("eb2b", [P, C], F32, p2)
        xd = [sb(f"xd{i}", [P, 2, ROW], F32, p2) for i in range(2)]
        dTh = sb("dTh", [P, KC, CH], F32R, p2)
        dTl = sb("dTl", [P, KC, CH], F32R, p2)
        hf = [sb(f"hf{i}", [P, 2, CH], F32, p2) for i in range(2)]
        hh = sb("hh", [P, MH, CH], F32R, p2)
        hl = sb("hl", [P, MH, CH], F32R, p2)
        eo = [sb(f"eo{i}", [P, C], F32, p2) for i in range(2)]
        wob = [sb(f"wob{i}", [P, 2, C], F32, p2) for i in range(2)]
        tok = [sb(f"tok{i}", [P, 2], U32, p2) for i in range(2)]
        wgt = [sb(f"wgt{i}", [P, 2], F32, p2) for i in range(2)]

        s_load = sem("small_loads")
        s_rw1 = sem("rw1_loaded")
        s_wq = sem("wqkv_loaded")
        s_accx = sem("acc_holds_x")
        s_fill = sem("disp_filled")
        c_pool = sem("constants_by_pool")
        sum4_step = sem("sum4_step")
        c_dve = sem("constants_by_dve")
        c_bias = sem("bias_transposed")
        x_ready = [sem(f"x_ready{i}") for i in range(2)]
        var_ready = sem("variance_ready")
        rstd_ready = sem("rstd_ready")
        ln_done = sem("ln_done")
        xT_ready = sem("xT_ready")
        hi_done = sem("hi_done")
        lo_done = sem("lo_done")
        g_ready = sem("g_ready")
        g_act = sem("g_act")
        g_dve = sem("g_dve")
        b1_done = sem("first_part_done")
        b2_done = sem("second_part_done")
        split_done = sem("parts_done")
        q_stored = [sem(f"q_stored{i}") for i in range(4)]
        v_stored = sem("v_stored")
        l_ready = sem("logit_parts_ready")
        lt_done = sem("logit_parts_read")
        s_ready = sem("logits_ready")
        m_ready = sem("choice_ready")
        p_ready = sem("places_ready")
        p_read = sem("places_read")
        gap_ready = sem("gap_ready")
        e_done = sem("gap_exp_done")
        slot_ready = sem("slot_ready")
        scat = [sem(f"scattered{i}") for i in range(2)]
        dstep = sem("dve_step")
        pool_passed, dve_passed = sem("pool_passed"), sem("dve_passed")
        qk_ready = [sem(f"qk_ready{i}") for i in range(4)]
        v_ready = [sem(f"v_ready{i}") for i in range(2)]
        s1_ready = sem("s1_ready")
        s1_max = sem("s1_max")
        mb_ready = sem("max_of_late_queries")
        mt_ready = sem("max_transposed")
        mn_ready = sem("max_negated")
        mp_step = sem("max_parts_step")
        mp_ready = sem("max_parts_ready")
        m_rows = [sem("max_rows_early"), sem("max_rows_late")]
        s2_ready = sem("s2_ready")
        exp_done = sem("exp_done")
        av_done = sem("av_done")
        den_ready = sem("den_ready")
        att_done = sem("att_done")
        f_ready = sem("f_ready")
        f_act = sem("f_act")
        f_dve = sem("f_dve")
        dhi_done = sem("dispatched_hi_done")
        tok_done = sem("token_rows_copied")
        h_hi = sem("h_hi_done")
        h_split = sem("h_split")
        w1_ld, w2_ld = sem("w1_loaded"), sem("w2_loaded")
        w1_hi, w2_hi = sem("w1_hi"), sem("w2_hi")
        w1_split, w2_split = sem("w1_split"), sem("w2_split")
        eb_ready = sem("expert_bias_ready")
        eb2_ld = sem("eb2_loaded")
        xd_ready = [sem(f"xd_ready{i}") for i in range(2)]
        eo_ready = sem("expert_rows_ready")
        added = sem("rows_added")
        s_out = sem("out_written")

        ringG = banks[0:4]
        bT = banks[4:6]
        bL, bR = banks[6], banks[7]
        GA, GD = 6, 8

        def g_end(g):
            if g < 8:
                return ("A", g // 2) if g % 2 == 0 else ("D", g // 2)
            return ("A", 4 + g - 8) if g < 10 else ("D", 4 + g - 10)

        def g_value(n, g):
            if g < 0:
                n, g = n - 1, g + 14
            who, k = g_end(g)
            return (g_act, (n + 2) * GA + k + 1) if who == "A" else (g_dve, (n + 2) * GD + k + 1)

        USES = []
        for g in range(NG):
            USES += [(g, "T", "D"), (g, "H0", "A"), (g, "H1", "D"), (g, "H2", "A"), (g, "H3", "D")]
            if g == NG - 1:
                USES += [(g, "W0", "A"), (g, "W1", "A")]
            USES += [(g, "S0", "D"), (g, "S1", "D")]
            if g == NG - 1:
                USES += [(g, "W2", "A"), (g, "W3", "A")]
        FU = len(USES)
        FA = sum(e == "A" for _, _, e in USES)
        FD = FU - FA
        USE = {(g, k): n for n, (g, k, _) in enumerate(USES)}
        assert FU % 2 == 0

        def f_end(b, n):
            if n < 0:
                b, n = b - 1, n + FU
            who = USES[n][2]
            k = sum(USES[i][2] == who for i in range(n))
            return (f_act, (b + 1) * FA + k + 1) if who == "A" else (f_dve, (b + 1) * FD + k + 1)

        def f_full(b, g, k):
            return b * FU + USE[(g, k)] + 1

        ringF = banks[6:8]
        bS1 = banks[0:2]
        bS2 = banks[2:4]
        bAV = banks[4]
        bM = banks[5]

        def f_bank(g, k):
            return ringF[USE[(g, k)] % 2]

        ADDS = [(g, k) for g, k, _ in USES if k[0] in "SW"]
        ADD = {gk: n for n, gk in enumerate(ADDS)}
        NA = len(ADDS)

        def add_done(b, n):
            return 16 + b * NA * 16 + 16 * (n + 1)

        STEP2 = [(0, k) for k in range(4)] + [(1, k) for k in range(8)]
        STEP1 = [(q, 0) for q in range(4)] + [(4 + i // 2, i % 2) for i in range(8)]
        NS = 12
        APART = 1000
        AFTER = {1: "T", 3: "H0", 4: "H1", 5: "H2", 6: "H3", 7: "W0", 8: "W1", 9: "S0", 10: "S1"}

        def part_after(g, s):
            k = AFTER.get(s)
            return k if k and (k[0] != "W" or g == NG - 1) else None

        def next_blk(i, p):
            return (1, i) if p == 0 else (0, i + 1)

        block = ctx.enter_context(nc.Block())

        @block.sync
        def _(sp):
            for i in range(4):
                sp.sem_inc(q_stored[i], 16)
            sp.sem_inc(v_stored, 16)
            x_blk = x.rearrange("b (c t p) d -> (b c) p t d", t=TB, p=P)

            def load_x(blk, p):
                sp.dma_start(xb[p][:, :, :], x_blk[blk, :, :, :]).then_inc(x_ready[p], 16)

            load_x(0, 0)
            sp.dma_start(stage[:, :, :], rw1.rearrange("(k p) n -> p k n", p=P)).then_inc(s_rw1, 16)
            sp.dma_start(wqs[:, :, :], w_qkv.rearrange("(k p) n -> p k n", p=P)).then_inc(s_wq, 16)
            sp.dma_start(brow[0:8 * MH, :], eb1.rearrange("e (m p) -> (e m) p", p=P)).then_inc(s_load, 16)
            sp.dma_start(brow[8 * MH:9 * MH, :], rb1.rearrange("(m p) -> m p", p=P)).then_inc(s_load, 16)
            sp.dma_start(rb2b[:, :], rb2.rearrange("(a e) -> a e", a=1).to_broadcast([P, E])).then_inc(s_load, 16)
            sp.wait_ge(c_dve, 1)
            sp.dma_start(rw2p[:, :, 0:E], rw2.rearrange("(m p) e -> p m e", p=P)).then_inc(s_load, 16)
            for j in range(HG):
                sp.dma_start(wo[32 * j:32 * j + DH, :, :],
                             w_o.rearrange("(g j d) n -> j d g n", j=HG, d=DH)[j, :, :, :]).then_inc(s_load, 16)
            sp.wait_ge(c_pool, 2)
            for a in range(E):
                sp.dma_start(disp[a * CAP:(a + 1) * CAP, :].rearrange("(n p) r -> p n r", p=P),
                             fill[:, :, :]).then_inc(s_fill, 16)
            with sp.Fori(0, B) as i:
                for p in range(2):
                    n = 2 * i + p
                    q, iq = next_blk(i, p)
                    sp.wait_ge(ln_done, n + 1)
                    load_x((n + 1) % (2 * B), q)
                    if p == 0:
                        sp.dma_start(acc[0:N, :].rearrange("(b t) d -> b t d", t=T)[i, :, :], x[i, :, :]
                                     ).then_inc(s_accx, 16)
                    s, v = g_value(n, 9)
                    sp.wait_ge(s, v)
                    for g in range(NG):
                        sp.dma_start(vhd[i, g, :, TB * p:TB * (p + 1), :],
                                     vst[:, :, HG * g:HG * (g + 1), :].rearrange("p t j e -> p t (j e)")
                                     ).then_inc(v_stored, 16)
                    for k in range(4):
                        sp.wait_ge(split_done, 4 + 4 * n + k + 1)
                        sp.dma_start(qkd[i, k // 2, :, p, P * (k % 2):P * (k % 2 + 1), :]
                                     .rearrange("a r t -> r a t"), qst[k][:, :, :]).then_inc(q_stored[k], 16)
            for i in range(4):
                sp.wait_ge(q_stored[i], 16 + 16 * 2 * B)
            sp.wait_ge(v_stored, 16 + 16 * 4 * 2 * B)
            sp.wait_ge(x_ready[0], 16 * (B + 1))
            sp.wait_ge(s_accx, 16 * B)
            for i in range(2):
                sp.wait_ge(scat[i], 16 + 128 * B)
            sp.sem_inc(phase, 1)
            sp.wait_ge(phase, 5)

            def load_stack(dst, which, terms, b, g, ready):
                for t, part in enumerate(terms):
                    sp.dma_start(dst[DH * t:DH * (t + 1), :, :, :].rearrange("r c j t -> r c (j t)"),
                                 qkd[b, which, part, :, HG * DH * g:HG * DH * (g + 1), :]
                                 .rearrange("c (d j) t -> d c (j t)", d=DH)).then_inc(ready, 16)

            def load_v(b, g, buf):
                sp.dma_start(vh[buf][:, :, :, :], vhd[b, g, :, :, :]).then_inc(v_ready[buf], 16)

            def load_disp(c, buf):
                sp.dma_start(xd[buf][:, :, :], disp.rearrange("(c s p) r -> c p s r", s=2, p=P)[c, :, :, :]
                             ).then_inc(xd_ready[buf], 16)

            def load_w1(e):
                sp.dma_start(wstage[:, :].rearrange("p (k n) -> p k n", k=KC),
                             ew1.rearrange("e (k p) n -> e p k n", p=P)[e, :, :, :]).then_inc(w1_ld, 16)

            def load_w2(e):
                sp.dma_start(wstage[:, :].rearrange("p (m n) -> p m n", m=MH),
                             ew2.rearrange("e (m p) n -> e p m n", p=P)[e, :, :, :]).then_inc(w2_ld, 16)

            def store_max(u, h, g):
                sp.wait_ge(mp_ready, 1 + 2 * u + h + 1)
                for r in range(PARTS):
                    sp.dma_start(qs[g][KR + r:KR + r + 1, h, :, :]
                                 .rearrange("a j (t q) -> a (j t) q", q=P),
                                 mparts[h][:, r, :]).then_inc(m_rows[h], 16)

            load_stack(ks[0], 1, TERMS_K, 0, 0, qk_ready[0])
            load_stack(qs[0], 0, TERMS_Q, 0, 0, qk_ready[0])
            load_v(0, 0, 0)
            load_w1(0)
            load_stack(ks[1], 1, TERMS_K, 0, 1, qk_ready[1])
            load_stack(qs[1], 0, TERMS_Q, 0, 1, qk_ready[1])
            load_disp(0, 0)
            sp.wait_ge(w1_split, 1)
            load_w2(0)
            store_max(0, 0, 0)
            with sp.Fori(0, B) as b:
                for g in range(NG):
                    u = NG * b + g
                    sp.wait_ge(av_done, 2 + NS * u)
                    load_v((b + (g + 1) // NG) % B, (g + 1) % NG, (g + 1) % 2)
                    g2 = (g + 2) % NG
                    b2 = (b + (g + 2) // NG) % B
                    load_stack(ks[g2], 1, TERMS_K, b2, g2, qk_ready[g2])
                    store_max(u, 1, g)
                    load_stack(qs[g2], 0, TERMS_Q, b2, g2, qk_ready[g2])
                    s, v = f_end(b, USE[(g - 1, "T")]) if g else f_end(b - 1, USE[(NG - 1, "T")])
                    sp.wait_ge(s, v)
                    load_disp((u + 1) % U, (g + 1) % 2)
                    if g == 0:
                        s, v = f_end(b - 1, USE[(NG - 1, "S1")])
                        sp.wait_ge(s, v)
                        sp.dma_start(eb2b[:, :], eb2[b, :].rearrange("(a n) -> a n", a=1).to_broadcast([P, C])
                                     ).then_inc(eb2_ld, 16)
                    if g == 1:
                        sp.wait_ge(w2_split, b + 1)
                        load_w1((b + 1) % E)
                    store_max(u + 1, 0, (g + 1) % NG)
                    if g == NG - 1:
                        sp.wait_ge(w1_split, b + 2)
                        load_w2((b + 1) % E)
            sp.wait_ge(added, 16 + NA * 16 * B)
            outf = out.rearrange("b t d -> (b t) d")
            for b in range(B):
                sp.dma_start(outf[T * b:T * (b + 1), :], acc[T * b:T * (b + 1), :]).then_inc(s_out, 16)
            sp.wait_ge(s_out, 16 * B)
            for i in range(4):
                sp.wait_ge(qk_ready[i], 192 * (B + (1 if i < 2 else 0)))
            sp.wait_ge(v_ready[0], 16 * (2 * B + 1))
            sp.wait_ge(xd_ready[0], 16 * (2 * B + 1))
            sp.wait_ge(w2_ld, 16 * (B + 1))
            sp.wait_ge(m_rows[0], 48 * (U + 2))

        @block.gpsimd
        def _(pool):
            pool.sem_inc(split_done, 4)
            fi = fill[:, :, :].bitcast(I32)
            nc.gpsimd.memset(fill[:, :, :], 0.0).then_inc(c_pool, 1)
            pool.wait_ge(c_pool, 1)
            nc.gpsimd.iota(fi[:, :, TOKC:TOKC + 1], pattern=[[0, 8], [0, 1]], base=N, channel_multiplier=1
                           ).then_inc(c_pool, 1)
            nc.gpsimd.memset(ident[:, :], 0.0)
            nc.gpsimd.memset(identb[:, :], 0.0)
            nc.gpsimd.memset(mask_qk[:, :], 0.0)
            nc.gpsimd.memset(mask_kq[:, :], 0.0)
            nc.gpsimd.memset(before[:, :], 1.0)
            nc.gpsimd.memset(onesb[:, :], 1.0)
            nc.gpsimd.memset(sum4[:, :], 0.0)
            nc.gpsimd.memset(minus_half[:, :], -0.5)
            nc.gpsimd.iota(small["iota8"][:, :, :], pattern=[[0, TB], [1, E]], base=-E, channel_multiplier=0,
                           allow_small_or_imprecise_dtypes=True)
            nc.gpsimd.iota(small["slotbase"][:, :, :], pattern=[[0, TB], [CAP, E]], base=0, channel_multiplier=0,
                           allow_small_or_imprecise_dtypes=True)
            nc.gpsimd.iota(one["tokf"][:, :], pattern=[[P, TB]], base=0, channel_multiplier=1,
                           allow_small_or_imprecise_dtypes=True).then_inc(c_pool, 1)
            pool.wait_ge(c_pool, 3)
            for t in (ident, identb):
                nc.gpsimd.affine_select(out=t[:, :], in_=t[:, :], compare_op=ALU.not_equal, fill=1.0, base=0,
                                        pattern=[[-1, P]], channel_multiplier=1)
            nc.gpsimd.affine_select(out=mask_qk[:, :], in_=mask_qk[:, :], compare_op=ALU.is_ge, fill=-BIG, base=0,
                                    pattern=[[-1, P]], channel_multiplier=1)
            nc.gpsimd.affine_select(out=mask_kq[:, :], in_=mask_kq[:, :], compare_op=ALU.is_ge, fill=-BIG, base=0,
                                    pattern=[[1, P]], channel_multiplier=-1)
            nc.gpsimd.affine_select(out=before[:, :], in_=before[:, :], compare_op=ALU.is_gt, fill=0.0, base=0,
                                    pattern=[[1, P]], channel_multiplier=-1)
            for j in range(4):
                nc.gpsimd.affine_select(out=sum4[:, :], in_=sum4[:, :], compare_op=ALU.not_equal, fill=1.0,
                                        base=-32 * j, pattern=[[-1, E]], channel_multiplier=1).then_inc(sum4_step, 1)
                pool.wait_ge(sum4_step, j + 1)
            pool.sem_inc(c_pool, 1)
            pool.wait_ge(c_pool, 4)

            def inverse_deviation(n):
                pool.wait_ge(var_ready, n + 1)
                nc.gpsimd.tensor_tensor(rstd[:, :], veps[:, :], minus_half[:, :], ALU.pow).then_inc(rstd_ready, 1)

            for a, (lo, hi) in zip((scat[0], scat[1], added), ((0, 32), (32, 64), (64, 128))):
                pool.dma_start(acc[N + lo:N + hi, :], fill[lo:hi, 0, 0:C]).then_inc(a, 16)
            inverse_deviation(0)
            pool.wait_ge(s_fill, 16 * E)
            def settled():
                pool.sem_inc(pool_passed, 1)

            with pool.Fori(0, B) as i:
                for p in range(2):
                    n = 2 * i + p
                    inverse_deviation(n + 1)
                    for k in range(4):
                        pool.wait_ge(b2_done, 4 * n + k + 1)
                        nc.gpsimd.tensor_tensor(qst[k][:, 2, :], res[k][:, :], qst[k][:, 1, :],
                                                ALU.subtract).then_inc(split_done, 1)
                    pool.wait_ge(slot_ready, n + 1)
                    settled()
                    for k in range(2):
                        for t in range(TB):
                            nc.gpsimd.indirect_dma_start(
                                out=disp, out_offset=bass.IndirectOffsetOnAxis(
                                    ap=slot[p][:, TB * k + t:TB * k + t + 1], axis=0),
                                in_=xn[p][:, t, :], in_offset=None,
                                bounds_check=E * CAP - 1, oob_is_err=False).then_inc(scat[p], 16)
            for i in range(2):
                pool.wait_ge(scat[i], 16 + 128 * B)
            pool.wait_ge(added, 16)
            pool.drain().then_inc(phase, 1)
            pool.wait_ge(phase, 5)

            pool.sem_inc(mp_ready, 1)
            pool.sem_inc(h_split, 2)
            for h in range(2):
                pool.sem_inc(m_rows[h], 48)

            def low_w(e, hi_sem, done, wh, wl):
                pool.wait_ge(hi_sem, e + 1)
                nc.gpsimd.tensor_tensor(wl[:, :], wstage[:, :], wh[:, :].bitcast(F32), ALU.subtract).then_inc(done, 1)

            def max_parts(u, h):
                M = 2 * u + h
                pool.wait_ge(mn_ready, 1 + M + 1)
                pool.wait_ge(m_rows[h], 48 * (u + 1))
                settled()
                nc.gpsimd.tensor_copy(mparts[h][:, 0, :], nm[:, :]).then_inc(mp_step, 1)
                pool.wait_ge(mp_step, 3 * M + 1)
                nc.gpsimd.tensor_tensor(nmr[:, :], nm[:, :], mparts[h][:, 0, :], ALU.subtract).then_inc(mp_step, 1)
                pool.wait_ge(mp_step, 3 * M + 2)
                settled()
                nc.gpsimd.tensor_copy(mparts[h][:, 1, :], nmr[:, :]).then_inc(mp_step, 1)
                pool.wait_ge(mp_step, 3 * M + 3)
                nc.gpsimd.tensor_tensor(mparts[h][:, 2, :], nmr[:, :], mparts[h][:, 1, :], ALU.subtract
                                        ).then_inc(mp_ready, 1)

            def part(b, g, k):
                u = NG * b + g
                if k[0] == "H":
                    r = int(k[1])
                    pool.wait_ge(h_hi, 4 * u + r + 1)
                    nc.gpsimd.tensor_tensor(hl[:, 2 * r:2 * r + 2, :], hf[r % 2][:, :, :],
                                            hh[:, 2 * r:2 * r + 2, :].bitcast(F32), ALU.subtract).then_inc(h_split, 1)
                if k[0] in "SW":
                    n = ADD[(g, k)]
                    pool.wait_ge(added, add_done(b, n - 1))
                if k[0] == "S":
                    r = int(k[1])
                    pool.wait_ge(eo_ready, 2 * u + r + 1)
                    settled()
                    nc.gpsimd.indirect_dma_start(
                        out=acc, out_offset=bass.IndirectOffsetOnAxis(ap=tok[g % 2][:, r:r + 1], axis=0),
                        in_=eo[r][:, :], in_offset=None, bounds_check=N + P - 1, oob_is_err=True,
                        compute_op=ALU.add).then_inc(added, 16)
                if k[0] == "W":
                    r = int(k[1])
                    s, v = f_end(b, USE[(g, k)])
                    pool.wait_ge(s, v)
                    settled()
                    pool.dma_start(acc[0:N, :].rearrange("(b k t p) c -> b k p t c", k=4, t=2, p=P)[b, r, :, :, :],
                                   wob[r % 2][:, :, :], accum_op=ALU.add).then_inc(added, 16)

            low_w(0, w1_hi, w1_split, w1h, w1l)
            max_parts(0, 0)
            low_w(0, w2_hi, w2_split, w2h, w2l)
            with pool.Fori(0, B) as b:
                for g in range(NG):
                    u = NG * b + g
                    for s in range(NS):
                        if s == 1:
                            max_parts(u, 1)
                        if s == 5:
                            max_parts(u + 1, 0)
                        k = part_after(g, s)
                        if k:
                            part(b, g, k)
                        if g == NG - 1 and s == 7:
                            low_w(b + 1, w1_hi, w1_split, w1h, w1l)
                        if g == NG - 1 and s == 11:
                            low_w(b + 1, w2_hi, w2_split, w2h, w2l)
                    if g == NG - 1:
                        part(b, g, "W2")
                        part(b, g, "W3")
            pool.wait_ge(added, 16 + NA * 16 * B)

        @block.scalar
        def _(act):
            act.sem_inc(g_act, 2 * GA)

            def high(k, n, q):
                act.wait_ge(xT_ready, n + 1)
                nc.scalar.activation(xTh[q][:, k, :], bT[k][:, :], ACT.Copy).then_inc(hi_done, 1)

            act.wait_ge(c_bias, 2)
            act.wait_ge(c_dve, 2)
            for k in range(KC):
                high(k, 0, 0)
            with act.Fori(0, B) as i:
                for p in range(2):
                    n = 2 * i + p
                    q, iq = next_blk(i, p)
                    for m in range(0, 8, 2):
                        act.wait_ge(g_ready, 14 * n + m + 1)
                        nc.scalar.activation(hT[:, m, :], ringG[(14 * p + m) % 4][:, :], ACT.Relu,
                                             bias=biasT[:, RB + m:RB + m + 1]).then_inc(g_act, 1)
                    act.wait_ge(v_stored, 16 + 64 * n)
                    for k in range(2):
                        act.wait_ge(g_ready, 14 * n + 8 + k + 1)
                        nc.scalar.activation(vst[:, 2 * k:2 * k + 2, :, 0:DH],
                                             ringG[(14 * p + 8 + k) % 4][:, :].rearrange("p (t h d) -> p t h d", t=2, d=DH),
                                             ACT.Copy).then_inc(g_act, 1)
                    def second(k):
                        s, v = g_value(n, 10 + k)
                        act.wait_ge(s, v)
                        nc.scalar.activation(qst[k][:, 1, :], res[k][:, :], ACT.Copy).then_inc(b2_done, 1)

                    for k in range(4):
                        if k == 2:
                            second(0)
                            second(1)
                            act.wait_ge(gap_ready, n + 1)
                            nc.scalar.activation(one["egap"][:, :], one["gap"][:, :], ACT.Exp).then_inc(e_done, 1)
                            for c in range(KC):
                                high(c, n + 1, q)
                        act.wait_ge(q_stored[k], 16 * (n + 1))
                        act.wait_ge(g_ready, 14 * n + 10 + k + 1)
                        nc.scalar.activation(qst[k][:, 0, :], ringG[(14 * p + 10 + k) % 4][:, :], ACT.Copy
                                             ).then_inc(b1_done, 1)
                    second(2)
                    second(3)
            act.drain().then_inc(phase, 1)
            act.wait_ge(phase, 5)

            act.sem_inc(f_act, FA)
            act.sem_inc(exp_done, 2)
            RS = 1.0 / float(C) ** 0.5

            def exps(u, s):
                c, kt = STEP2[s]
                nq = 512 * (c + 1) - max(P * kt, 512 * c)
                act.wait_ge(av_done, NS * u + s + 1)
                for j in range(HG):
                    act.wait_ge(s2_ready, 48 * u + 4 * s + j + 1)
                    nc.scalar.activation(pt[s % 2][:, j, 0:nq], bS2[j % 2][:, 0:nq], ACT.Exp, scale=RS
                                         ).then_inc(exp_done, 1)

            def part(b, g, k):
                u = NG * b + g
                if k == "T":
                    act.wait_ge(f_ready, f_full(b, g, k))
                    nc.scalar.activation(dTh[:, :, :], f_bank(g, k)[:, :].rearrange("p (k n) -> p k n", k=KC),
                                         ACT.Copy).then_inc(dhi_done, 1)
                if k in ("H0", "H2"):
                    r = int(k[1])
                    act.wait_ge(eb_ready, b + 1)
                    act.wait_ge(h_split, 4 * u + r + 1)
                    act.wait_ge(f_ready, f_full(b, g, k))
                    for m in range(2):
                        o = nc.scalar.activation(hf[r % 2][:, m, :], f_bank(g, k)[:, CH * m:CH * (m + 1)], ACT.Relu,
                                                 bias=ebias[:, 2 * r + m:2 * r + m + 1])
                    o.then_inc(f_act, 1)
                if k[0] == "H":
                    r = int(k[1])
                    s, v = f_end(b, USE[(g, k)])
                    act.wait_ge(s, v)
                    nc.scalar.activation(hh[:, 2 * r:2 * r + 2, :], hf[r % 2][:, :, :], ACT.Copy).then_inc(h_hi, 1)
                if k[0] == "W":
                    r = int(k[1])
                    prev = ADD[(NG - 1, f"W{(r + 2) % 4}")]
                    act.wait_ge(added, add_done(b, prev) if r >= 2 else add_done(b, -1))
                    act.wait_ge(f_ready, f_full(b, g, k))
                    nc.scalar.activation(wob[r % 2][:, :, :], f_bank(g, k)[:, :].rearrange("p (t c) -> p t c", t=2),
                                         ACT.Copy).then_inc(f_act, 1)

            def high_w(e, ld, hi_sem, wh):
                act.wait_ge(ld, 16 * (e + 1))
                nc.scalar.activation(wh[:, :], wstage[:, :], ACT.Copy).then_inc(hi_sem, 1)

            high_w(0, w1_ld, w1_hi, w1h)
            high_w(0, w2_ld, w2_hi, w2h)
            with act.Fori(0, B) as b:
                for g in range(NG):
                    for s in range(NS):
                        exps(NG * b + g, s)
                        k = part_after(g, s)
                        if k:
                            part(b, g, k)
                        if g == NG - 1 and s == 7:
                            act.wait_ge(f_ready, f_full(b, g, "H3"))
                            high_w(b + 1, w1_ld, w1_hi, w1h)
                        if g == NG - 1 and s == 11:
                            act.wait_ge(f_ready, f_full(b, g, "S1"))
                            high_w(b + 1, w2_ld, w2_hi, w2h)
                    if g == NG - 1:
                        part(b, g, "W2")
                        part(b, g, "W3")

        @block.vector
        def _(dve):
            chain = {"base": 0, "n": 0}

            def link(ins):
                chain["n"] += 1
                ins.then_inc(dstep, 1)
                dve.wait_ge(dstep, chain["base"] + chain["n"])

            dve.sem_inc(g_dve, 2 * GD)
            dve.sem_inc(ln_done, 1)
            dve.sem_inc(lt_done, 1)
            dve.sem_inc(p_read, 1)
            nc.vector.memset(rw2p[:, :, :], 0.0)
            nc.vector.memset(vst[:, :, :, :], 1.0)
            nc.vector.memset(carry[:, :], 0.0)
            for i in range(2):
                nc.vector.memset(xn[i][:, :, C:ROW], 0.0)
            nc.vector.memset(wo[:, :, :], 0.0).then_inc(c_dve, 1)
            dve.wait_ge(c_dve, 1)
            dve.wait_ge(s_rw1, 16)
            link(nc.vector.tensor_copy(rw1h[:, :, :], stage[:, :, :]))
            nc.vector.tensor_tensor(rw1l[:, :, :], stage[:, :, :], rw1h[:, :, :].bitcast(F32), ALU.subtract
                                    ).then_inc(c_dve, 2)

            def layer_norm(n, q, iq):
                dve.wait_ge(x_ready[q], 16 * (iq + 1))
                for t in range(TB):
                    o = nc.vector.bn_stats(stats[:, t, :], xb[q][:, t, :])
                link(o)
                dve.sem_inc(dve_passed, 1)
                for t in range(TB):
                    o = nc.vector.bn_aggr(mv[:, t, :], stats[:, t, :])
                link(o)
                nc.vector.tensor_scalar(veps[:, :], mv[:, :, 1], EPS, None, ALU.add).then_inc(var_ready, 1)
                dve.wait_ge(rstd_ready, n + 1)
                dve.wait_ge(scat[q], 16 + 128 * iq)
                for t in range(TB):
                    o = nc.vector.tensor_scalar(xn[q][:, t, 0:C], xb[q][:, t, :], mv[:, t, 0:1], rstd[:, t:t + 1],
                                                ALU.subtract, ALU.mult)
                o.then_inc(ln_done, 1)

            def low(k, n, q):
                dve.wait_ge(hi_done, 2 * n + k + 1)
                nc.vector.tensor_tensor(xTl[q][:, k, :], bT[k][:, :], xTh[q][:, k, :].bitcast(F32), ALU.subtract
                                        ).then_inc(lo_done, 1)

            layer_norm(0, 0, 0)
            dve.wait_ge(c_bias, 1)
            nc.vector.tensor_copy(biasT[:, :], bL[:, 0:9 * MH]).then_inc(c_bias, 1)
            dve.wait_ge(s_wq, 16)
            dve.wait_ge(c_pool, 4)
            for k in range(KC):
                src = wqs[:, k, :].rearrange("p (g j s d) -> p s g d j", s=3, d=DH, j=HG)
                dh = wqh[:, k, 0:2 * C].rearrange("p (s g d j) -> p s g d j", s=2, d=DH, j=HG)
                dl = wql[:, k, 0:2 * C].rearrange("p (s g d j) -> p s g d j", s=2, d=DH, j=HG)
                vsrc = wqs[:, k, :].rearrange("p (h s d) -> p h s d", s=3, d=DH)[:, :, 2, :]
                vdh = wqh[:, k, 2 * C:3 * C].rearrange("p (h d) -> p h d", d=DH)
                vdl = wql[:, k, 2 * C:3 * C].rearrange("p (h d) -> p h d", d=DH)
                for s in range(2):
                    for g in range(NG):
                        nc.vector.tensor_copy(dh[:, s, g, :, :], src[:, s, g, :, :])
                link(nc.vector.tensor_copy(vdh, vsrc))
                for s in range(2):
                    for g in range(NG):
                        nc.vector.tensor_tensor(dl[:, s, g, :, :], src[:, s, g, :, :],
                                                dh[:, s, g, :, :].bitcast(F32), ALU.subtract)
                o = nc.vector.tensor_tensor(vdl, vsrc, vdh.bitcast(F32), ALU.subtract)
            o.then_inc(c_dve, 1)
            for k in range(KC):
                low(k, 0, 0)
            dve.wait_ge(s_load, 16 * 8)
            start = chain["n"]

            def bc(ap):
                return ap.rearrange("p (t a) -> p t a", a=1).to_broadcast([P, TB, E])

            with dve.Fori(0, B) as i:
                S_ = small
                chain["base"] = start + i * CHAIN1
                chain["n"] = 0
                for p in range(2):
                    n = 2 * i + p
                    q, iq = next_blk(i, p)
                    for m in range(1, 8, 2):
                        dve.wait_ge(g_ready, 14 * n + m + 1)
                        nc.vector.tensor_scalar(hT[:, m, :], ringG[(14 * p + m) % 4][:, :],
                                                biasT[:, RB + m:RB + m + 1], 0.0, ALU.add, ALU.max).then_inc(g_dve, 1)
                    layer_norm(n + 1, q, iq)
                    dve.wait_ge(l_ready, n + 1)
                    nc.vector.tensor_copy(ltp[:, :], bL[:, :]).then_inc(lt_done, 1)

                    def rest(k):
                        dve.wait_ge(b1_done, 4 * n + k + 1)
                        dve.wait_ge(split_done, 4 * n + k + 1)
                        nc.vector.tensor_tensor(res[k][:, :], ringG[(14 * p + 10 + k) % 4][:, :],
                                                qst[k][:, 0, :], ALU.subtract).then_inc(g_dve, 1)

                    rest(0)
                    rest(1)
                    dve.wait_ge(s_ready, n + 1)
                    link(nc.vector.tensor_tensor(S_["lg"][:, :, :], bR[:, 0:TB * E].rearrange("p (t e) -> p t e", e=E),
                                                 rb2b[:, :].rearrange("p (a e) -> p a e", a=1).to_broadcast([P, TB, E]),
                                                 ALU.add))
                    for k, (lg, top, f, oh) in enumerate((("lg", "top0", "f0", "oh0"), ("lg2", "top1", "f1", "oh1"))):
                        if k == 1:
                            link(nc.vector.scalar_tensor_tensor(S_["lg2"][:, :, :], S_["oh0"][:, :, :], -3.0e38,
                                                                S_["lg"][:, :, :], ALU.mult, ALU.add))
                        link(nc.vector.tensor_reduce(one[top][:, :], S_[lg][:, :, :], AX, ALU.max))
                        link(nc.vector.tensor_tensor(S_["eq"][:, :, :], S_[lg][:, :, :], bc(one[top][:, :]), ALU.is_equal))
                        link(nc.vector.tensor_tensor(S_["cand"][:, :, :], S_["eq"][:, :, :], S_["iota8"][:, :, :], ALU.mult))
                        link(nc.vector.tensor_reduce(one[f][:, :], S_["cand"][:, :, :], AX, ALU.min))
                        link(nc.vector.tensor_tensor(S_[oh][:, :, :], S_["iota8"][:, :, :], bc(one[f][:, :]), ALU.is_equal))
                    nc.vector.tensor_tensor(m8[:, :, :], S_["oh0"][:, :, :], S_["oh1"][:, :, :], ALU.add
                                            ).then_inc(m_ready, 1)
                    nc.vector.tensor_tensor(one["gap"][:, :], one["top1"][:, :], one["top0"][:, :], ALU.subtract
                                            ).then_inc(gap_ready, 1)
                    for c in range(KC):
                        low(c, n + 1, q)
                    rest(2)
                    rest(3)
                    dve.wait_ge(e_done, n + 1)
                    link(nc.vector.tensor_scalar(one["den2"][:, :], one["egap"][:, :], 1.0, None, ALU.add))
                    link(nc.vector.reciprocal(one["w0"][:, :], one["den2"][:, :]))
                    nc.vector.tensor_tensor(S_["pv0"][:, :, :], S_["oh0"][:, :, :], bc(one["w0"][:, :]), ALU.mult)
                    link(nc.vector.tensor_tensor(one["w1"][:, :], one["w0"][:, :], one["egap"][:, :], ALU.mult))
                    link(nc.vector.tensor_tensor(S_["pv1"][:, :, :], S_["oh1"][:, :, :], bc(one["w1"][:, :]), ALU.mult))
                    nc.vector.tensor_tensor(xn[p][:, :, PVC:PVC + E], S_["pv0"][:, :, :], S_["pv1"][:, :, :], ALU.add)
                    link(nc.vector.tensor_copy(xn[p][:, :, TOKC:TOKC + 1].bitcast(U32),
                                               one["tokf"][:, :].rearrange("p (t a) -> p t a", a=1)))
                    link(nc.vector.tensor_scalar(one["tokf"][:, :], one["tokf"][:, :], float(BLK), None, ALU.add))
                    dve.wait_ge(p_ready, n + 1)
                    pos = bR[:, 64:64 + TB * E].rearrange("p (t e) -> p t e", e=E)
                    link(nc.vector.tensor_reduce(msum[:, :], m8[:, :, :].rearrange("p t e -> p e t"), AX, ALU.add))
                    nc.vector.tensor_tensor(carry[:, :], carry[:, :], msum[:, :], ALU.add)
                    nc.vector.tensor_scalar(S_["over"][:, :, :], pos, float(CAP), float(1 << 20), ALU.is_ge, ALU.mult)
                    link(nc.vector.tensor_tensor(S_["place"][:, :, :], pos, S_["slotbase"][:, :, :], ALU.add))
                    nc.vector.tensor_tensor(S_["cand"][:, :, :], S_["place"][:, :, :], S_["over"][:, :, :], ALU.add
                                            ).then_inc(p_read, 1)
                    dve.wait_ge(p_read, n + 2)
                    for k in range(2):
                        o = nc.vector.tensor_tensor(S_[f"sel{k}"][:, :, :], S_[f"oh{k}"][:, :, :], S_["cand"][:, :, :], ALU.mult)
                        if k == 1:
                            link(o)
                    for k in range(2):
                        o = nc.vector.tensor_reduce(slotf[p][:, k, :], S_[f"sel{k}"][:, :, :], AX, ALU.add)
                    link(o)
                    nc.vector.tensor_copy(slot[p][:, :], slotf[p][:, :, :].rearrange("p k t -> p (k t)")
                                          ).then_inc(slot_ready, 1)
                assert chain["n"] == CHAIN1, chain["n"]
            dve.drain().then_inc(phase, 1)
            dve.wait_ge(phase, 5)

            dve.sem_inc(f_dve, FD)
            dve.sem_inc(s1_max, APART + 2)
            dve.sem_inc(mn_ready, 1)
            dve.sem_inc(att_done, 1)
            for i in range(4):
                o = nc.vector.memset(ks[i][KR:KR + PARTS, :, :, :], 1.0)
            o.then_inc(c_dve, 1)

            def reduce_step(u, s, par):
                qt, kc = STEP1[s]
                nk = 512 if kc < qt // 4 else P * (qt % 4 + 1)
                for j in range(HG):
                    dve.wait_ge(s1_ready, 48 * u + 4 * s + j + 1)
                    dst = mxA[par][:, j, qt:qt + 1] if qt < 4 else mxB[par][:, j, qt - 4, kc:kc + 1]
                    nc.vector.tensor_reduce(dst, bS1[j % 2][:, 0:nk], AX, ALU.max).then_inc(s1_max, 1)

            def late_max(u, par):
                dve.wait_ge(s1_max, APART + 2 + 48 * (u + 1))
                dve.wait_ge(mt_ready, 2 * u + 1)
                nc.vector.tensor_reduce(mxBr[:, :], mxB[par][:, :, :, :].rearrange("p j t k -> p (j t) k"), AX, ALU.max
                                        ).then_inc(mb_ready, 1)

            def negate(u, h):
                M = 2 * u + h
                dve.wait_ge(mt_ready, M + 1)
                dve.wait_ge(mp_ready, M + 1)
                nc.vector.tensor_scalar(nm[:, :], bM[0:16, 0:P], -1.0, None, ALU.mult).then_inc(mn_ready, 1)

            def attend(u, g, c):
                dve.wait_ge(av_done, 2 + NS * u + (4 if c == 0 else 12))
                dve.wait_ge(att_done, 2 * u + c + 1)
                D = 3 * (2 * u + c)
                nc.vector.transpose(den[:, :], bAV[:, :]).then_inc(den_ready, 1)
                dve.wait_ge(den_ready, D + 1)
                nc.vector.reciprocal(rsum[:, :], den[:, :].rearrange("p (n r) -> p n r", r=32)[:, :, DH]
                                     ).then_inc(den_ready, 1)
                dve.wait_ge(den_ready, D + 2)
                nc.vector.transpose(rden[:, :].rearrange("p (n r) -> p n r", r=32),
                                    rsum[:, :].rearrange("p (n a) -> p n a", a=1).to_broadcast([P, 16, 32])
                                    ).then_inc(den_ready, 1)
                dve.wait_ge(den_ready, D + 3)
                nc.vector.tensor_tensor(attT[:, g, 512 * c:512 * (c + 1)], bAV[:, :], rden[:, :], ALU.mult
                                        ).then_inc(att_done, 1)

            def part(b, g, k):
                u = NG * b + g
                if k == "T":
                    dve.wait_ge(xd_ready[g % 2], 16 * (2 * b + g // 2 + 1))
                    nc.vector.tensor_copy(tok[g % 2][:, :], xd[g % 2][:, :, TOKC].bitcast(U32))
                    nc.vector.tensor_copy(wgt[g % 2][:, :].rearrange("p (s a) -> p s a", a=1),
                                          xd[g % 2][:, :, bass.ds(b + PVC, 1)]).then_inc(tok_done, 1)
                    dve.wait_ge(dhi_done, u + 1)
                    nc.vector.tensor_tensor(dTl[:, :, :], f_bank(g, k)[:, :].rearrange("p (k n) -> p k n", k=KC),
                                            dTh[:, :, :].bitcast(F32), ALU.subtract).then_inc(f_dve, 1)
                if k in ("H1", "H3"):
                    r = int(k[1])
                    dve.wait_ge(h_split, 4 * u + r + 1)
                    dve.wait_ge(f_ready, f_full(b, g, k))
                    for m in range(2):
                        o = nc.vector.tensor_scalar(hf[r % 2][:, m, :], f_bank(g, k)[:, CH * m:CH * (m + 1)],
                                                    ebias[:, 2 * r + m:2 * r + m + 1], 0.0, ALU.add, ALU.max)
                    o.then_inc(f_dve, 1)
                if k[0] == "S":
                    r = int(k[1])
                    n = ADD[(g, k)]
                    dve.wait_ge(added, add_done(b, ADD[(g - 1, k)]) if g else add_done(b, -1))
                    dve.wait_ge(eb2_ld, 16 * (b + 1))
                    dve.wait_ge(f_ready, f_full(b, g, k))
                    nc.vector.tensor_tensor(eo[r][:, :], f_bank(g, k)[:, 0:C], eb2b[:, :], ALU.add).then_inc(f_dve, 1)
                    s, v = f_end(b, USE[(g, k)])
                    dve.wait_ge(s, v)
                    nc.vector.tensor_scalar(eo[r][:, :], eo[r][:, :], wgt[g % 2][:, r:r + 1], None, ALU.mult
                                            ).then_inc(eo_ready, 1)

            dve.wait_ge(c_dve, 5)
            for s in range(NS):
                reduce_step(0, s, 0)
            dve.wait_ge(s1_max, APART + 2 + 48)
            nc.vector.tensor_reduce(mxBr[:, :], mxB[0][:, :, :, :].rearrange("p j t k -> p (j t) k"), AX, ALU.max
                                    ).then_inc(mb_ready, 1)
            negate(0, 0)
            with dve.Fori(0, B) as b:
                for g in range(NG):
                    u = NG * b + g
                    if g == 0:
                        nc.vector.tensor_copy(ebias[:, :], biasT[:, bass.ds(b * MH, MH)]).then_inc(eb_ready, 1)
                        dve.wait_ge(eb_ready, b + 1)
                    for s in range(NS):
                        reduce_step(u + 1, s, (g + 1) % 2)
                        if s == 1:
                            negate(u, 1)
                        if s == 4:
                            attend(u, g, 0)
                        if s == 5:
                            negate(u + 1, 0)
                        k = part_after(g, s)
                        if k:
                            part(b, g, k)
                    late_max(u + 1, (g + 1) % 2)
                    attend(u, g, 1)

        @block.tensor
        def _(pe):
            mm = nc.tensor.matmul

            def mm3(dst, ah, al, bh, bl, first, last):
                mm(dst, ah, bh, start=first, stop=False)
                mm(dst, ah, bl, start=False, stop=False)
                return mm(dst, al, bh, start=False, stop=last)

            pe.wait_ge(c_pool, 4)
            pe.wait_ge(s_load, 16 * 8)
            pe.wait_ge(c_dve, 1)
            nc.tensor.transpose(bL[:, 0:9 * MH], brow[:, :], ident[0:9 * MH, 0:9 * MH]).then_inc(c_bias, 1)
            pe.wait_ge(c_bias, 2)

            def transposes(n, q):
                pe.wait_ge(ln_done, n + 2)
                for k in range(KC):
                    for t in range(TB):
                        o = nc.tensor.transpose(bT[k][:, P * t:P * (t + 1)], xn[q][:, t, P * k:P * (k + 1)], ident[:, :])
                o.then_inc(xT_ready, 1)

            transposes(0, 0)
            pe.wait_ge(c_dve, 4)
            with pe.Fori(0, B) as i:
                for p in range(2):
                    n = 2 * i + p
                    q, iq = next_blk(i, p)
                    xh, xl = xTh[p], xTl[p]

                    def free(g):
                        s, v = g_value(n, g - 4)
                        pe.wait_ge(s, v)
                        return ringG[(14 * p + g) % 4]

                    pe.wait_ge(lo_done, 2 * n + 2)
                    for m in range(MH):
                        dst = free(m)
                        for k in range(KC):
                            o = mm3(dst[:, :], rw1h[:, k, P * m:P * (m + 1)], rw1l[:, k, P * m:P * (m + 1)],
                                    xh[:, k, :], xl[:, k, :], k == 0, k == KC - 1)
                        o.then_inc(g_ready, 1)
                    for h in range(2):
                        dst = free(8 + h)
                        for t in range(2):
                            ts = slice(P * (2 * h + t), P * (2 * h + t + 1))
                            for k in range(KC):
                                o = mm3(dst[:, C * t:C * (t + 1)], xh[:, k, ts], xl[:, k, ts],
                                        wqh[:, k, 2 * C:3 * C], wql[:, k, 2 * C:3 * C], k == 0, k == KC - 1)
                        o.then_inc(g_ready, 1)
                    for g in (6, 7):
                        s, v = g_value(n, g)
                        pe.wait_ge(s, v)
                    pe.wait_ge(lt_done, n + 1)
                    for r in range(2):
                        for j in range(4):
                            o = mm(bL[32 * j:32 * j + 32, :], rw2p[:, 4 * r + j, :], hT[:, 4 * r + j, :],
                                   start=(r == 0), stop=(r == 1), tile_position=(0, 32 * j), skip_group_check=True)
                    o.then_inc(l_ready, 1)

                    def qk_tile(k):
                        dst = free(10 + k)
                        for c in range(KC):
                            o = mm3(dst[:, :], wqh[:, c, P * k:P * (k + 1)], wql[:, c, P * k:P * (k + 1)],
                                    xh[:, c, :], xl[:, c, :], c == 0, c == KC - 1)
                        o.then_inc(g_ready, 1)

                    qk_tile(0)
                    qk_tile(1)
                    pe.wait_ge(lt_done, n + 2)
                    pe.wait_ge(p_read, n + 1)
                    for t in range(TB):
                        o = mm(bR[:, E * t:E * (t + 1)], ltp[:, P * t:P * (t + 1)], sum4[:, :], start=True, stop=True)
                    o.then_inc(s_ready, 1)
                    transposes(n + 1, q)
                    qk_tile(2)
                    qk_tile(3)
                    pe.wait_ge(m_ready, n + 1)
                    pos = bR[:, 64:64 + TB * E]
                    for t in range(TB):
                        d = pos[:, E * t:E * (t + 1)]
                        mm(d, before[:, :], m8[:, t, :], start=True, stop=False)
                        for tt in range(t):
                            mm(d, onesb[:, :], m8[:, tt, :], start=False, stop=False)
                        o = mm(d, onesb[:, :], carry[:, :], start=False, stop=True)
                    o.then_inc(p_ready, 1)
            pe.drain().then_inc(phase, 1)
            pe.wait_ge(phase, 5)

            pe.sem_inc(av_done, 2)

            def s1_chunk(u, s, j, g):
                qt, kc = STEP1[s]
                diag = kc == qt // 4
                nk = P * (qt % 4 + 1) if diag else 512
                pe.wait_ge(s1_max, APART + 48 * u + 4 * s + j + 1)
                bank = bS1[j % 2]
                o = mm(bank[:, 0:nk], qs[g][0:KR, qt // 4, j, P * (qt % 4):P * (qt % 4 + 1)], ks[g][0:KR, kc, j, 0:nk],
                       start=True, stop=True)
                if diag:
                    o = mm(bank[:, nk - P:nk], identb[:, :], mask_qk[:, :], start=False, stop=True, skip_group_check=True)
                o.then_inc(s1_ready, 1)

            def s2_chunk(u, s, j, g):
                c, kt = STEP2[s]
                q0 = max(P * kt, 512 * c)
                nq = 512 * (c + 1) - q0
                diag = P * kt >= 512 * c
                pe.wait_ge(exp_done, 48 * u + 4 * s + j + 1)
                bank = bS2[j % 2]
                o = mm(bank[:, 0:nq], ks[g][0:KR + PARTS, kt // 4, j, P * (kt % 4):P * (kt % 4 + 1)],
                       qs[g][0:KR + PARTS, c, j, q0 - 512 * c:512],
                       start=True, stop=True)
                if diag:
                    o = mm(bank[:, 0:P], identb[:, :], mask_kq[:, :], start=False, stop=True, skip_group_check=True)
                o.then_inc(s2_ready, 1)

            def av_step(u, s, g):
                c, kt = STEP2[s]
                q0 = max(P * kt, 512 * c)
                nq = 512 * (c + 1) - q0
                pe.wait_ge(exp_done, 2 + 48 * u + 4 * s + 4)
                if kt == 0:
                    pe.wait_ge(att_done, 2 * u + c + 1)
                for j in range(HG):
                    o = mm(bAV[32 * j:32 * j + 32, q0 - 512 * c:512], vh[g % 2][:, kt, j, :], pt[s % 2][:, j, 0:nq],
                           start=(kt == 0), stop=True, tile_position=(0, 32 * j), skip_group_check=True)
                o.then_inc(av_done, 1)

            def max_transpose(u, h, par):
                M = 2 * u + h
                if h == 0:
                    pe.wait_ge(s1_max, APART + 2 + 48 * u + 16)
                    src = mxA[par][:, :, :].rearrange("p j t -> p (j t)")
                else:
                    pe.wait_ge(mb_ready, u + 1)
                    src = mxBr[:, :]
                pe.wait_ge(mn_ready, M + 1)
                nc.tensor.transpose(bM[0:16, 0:P], src, ident[:, :]).then_inc(mt_ready, 1)

            def part(b, g, k):
                u = NG * b + g
                n = USE[(g, k)]
                dst = f_bank(g, k)
                if k == "T":
                    pe.wait_ge(xd_ready[g % 2], 16 * (2 * b + g // 2 + 1))
                if k == "H0":
                    if g == 0:
                        pe.wait_ge(w1_split, b + 1)
                    s, v = f_end(b, USE[(g, "T")])
                    pe.wait_ge(s, v)
                if k == "S0":
                    if g == 0:
                        pe.wait_ge(w2_split, b + 1)
                    pe.wait_ge(h_split, 2 + 4 * u + 4)
                if k in ("W0", "W2"):
                    pe.wait_ge(att_done, 1 + 2 * (NG * b + NG - 1) + (2 if k == "W2" else 1))
                s, v = f_end(b, n - 2)
                pe.wait_ge(s, v)
                r = int(k[1]) if len(k) > 1 else 0
                if k == "T":
                    for c in range(KC):
                        for st in range(2):
                            o = nc.tensor.transpose(dst[:, CH * c + P * st:CH * c + P * (st + 1)],
                                                    xd[g % 2][:, st, P * c:P * (c + 1)], ident[:, :])
                elif k[0] == "H":
                    for i in range(2):
                        m = 2 * r + i
                        for c in range(KC):
                            w = slice(H * c + P * m, H * c + P * (m + 1))
                            o = mm3(dst[:, CH * i:CH * (i + 1)], w1h[:, w], w1l[:, w], dTh[:, c, :], dTl[:, c, :],
                                    c == 0, c == KC - 1)
                elif k[0] == "S":
                    for m in range(MH):
                        ss = slice(P * r, P * (r + 1))
                        w = slice(C * m, C * (m + 1))
                        o = mm3(dst[:, 0:C], hh[:, m, ss], hl[:, m, ss], w2h[:, w], w2l[:, w], m == 0, m == MH - 1)
                else:
                    for t in range(2):
                        ts = slice(P * (2 * r + t), P * (2 * r + t + 1))
                        for gg in range(NG):
                            o = mm(dst[:, C * t:C * (t + 1)], attT[:, gg, ts], wo[:, gg, :],
                                   start=(gg == 0), stop=(gg == NG - 1))
                o.then_inc(f_ready, 1)

            pe.wait_ge(c_dve, 5)
            pe.wait_ge(qk_ready[0], 192)
            for s in range(NS):
                for j in range(HG):
                    s1_chunk(0, s, j, 0)
            max_transpose(0, 0, 0)
            with pe.Fori(0, B) as b:
                for g in range(NG):
                    u = NG * b + g
                    g1 = (g + 1) % NG
                    pe.wait_ge(qk_ready[g1], 192 * (b + 1 + (g + 1) // NG))
                    pe.wait_ge(v_ready[g % 2], 16 * (2 * b + g // 2 + 1))
                    pe.wait_ge(m_rows[0], 48 * (u + 2))
                    for s in range(NS):
                        if s == 4:
                            pe.wait_ge(m_rows[1], 48 * (u + 2))
                        for j in range(HG):
                            s2_chunk(u, s, j, g)
                            s1_chunk(u + 1, s, j, g1)
                            if j == 1 and s > 0:
                                av_step(u, s - 1, g)
                        if s == 1:
                            max_transpose(u, 1, g % 2)
                        if s == 5:
                            max_transpose(u + 1, 0, g1 % 2)
                        k = part_after(g, s)
                        if k:
                            part(b, g, k)
                    av_step(u, NS - 1, g)
                    if g == NG - 1:
                        part(b, g, "W2")
                        part(b, g, "W3")


CHAIN1 = 48

_INS = ['L0_attn_x', 'L0_attn_w_qkv', 'L0_attn_w_o', 'L0_ffn_rw1', 'L0_ffn_rb1', 'L0_ffn_rw2', 'L0_ffn_rb2',
        'L0_ffn_ew1', 'L0_ffn_eb1', 'L0_ffn_ew2', 'L0_ffn_eb2']
_OUTS = [((8, 1024, 256), 'float32')]


def kernel(**inputs):
    import numpy as _np
    import concourse.bacc as _bacc
    from concourse import mybir as _mybir
    from concourse.bass_utils import run_bass_kernel_spmd as _run

    nc = _bacc.Bacc("TRN2", target_bir_lowering=False, num_devices=1)
    arrays, args = {}, []
    for name in _INS:
        a = _np.ascontiguousarray(inputs[name])
        arrays[f"in_{name}_dram"] = a
        args.append(nc.dram_tensor(f"in_{name}_dram", a.shape, _mybir.dt.from_np(a.dtype), kind="ExternalInput").ap())
    for i, (shape, dtype) in enumerate(_OUTS):
        dt = _mybir.dt.from_np(_np.dtype(dtype))
        args.append(nc.dram_tensor(f"out_{i}_dram", shape, dt, kind="ExternalOutput").ap())
    layer_kernel(nc, *args)
    r = _run(nc, [arrays], core_ids=[0])
    got = tuple(r.results[0][f"out_{i}_dram"] for i in range(len(_OUTS)))
    return got[0]
```

```python
from contextlib import ExitStack

import concourse.bass as bass
from concourse import mybir

F32 = mybir.dt.float32
F32R = mybir.dt.float32r
BF16 = mybir.dt.bfloat16
U32 = mybir.dt.uint32
I32 = mybir.dt.int32
ALU = mybir.AluOpType
ACT = mybir.ActivationFunctionType
AX = mybir.AxisListType.X

P = 128
BIG = 1.0e30
EPS = 1e-5
PARTS = 3
TERMS_Q = (0, 0, 0, 1, 1, 2)
TERMS_K = (0, 1, 2, 0, 1, 0)


def layer_kernel(nc, x, w_qkv, w_o, rw1, rb1, rw2, rb2, ew1, eb1, ew2, eb2, out):
    B, T, C = x.shape
    N = B * T
    H = rw1.shape[1]
    E = rw2.shape[1]
    CAP = 1024
    NH, DH = 16, 16
    KC = C // P
    MH = H // P
    BLK = 512
    TB = BLK // P
    HG = 4
    NG = NH // HG
    U = B * NG
    KT = T // P
    NT = len(TERMS_Q)
    KR = NT * DH
    ROW = 272
    TOKC, PVC = C, C + 4
    CH = 256
    assert (C, H, E, T, B) == (256, 1024, 8, 1024, 8) and N // BLK == 2 * B

    acc = nc.dram_tensor("acc", (N + P, C), F32).ap()
    disp = nc.dram_tensor("disp", (E * CAP, ROW), F32).ap()
    qkd = nc.dram_tensor("qk_parts", (B, 2, PARTS, 2, C, 512), BF16).ap()
    vhd = nc.dram_tensor("v_ones", (B, NG, P, KT, HG * 32), F32).ap()

    ctx = ExitStack()
    with ctx:
        def sb(name, shape, dt=F32, stack=ctx):
            return stack.enter_context(nc.sbuf_tensor(name, shape, dt))

        def sem(name):
            return ctx.enter_context(nc.semaphore(name))

        ident = sb("ident", [P, P])
        identb = sb("identb", [P, P], BF16)
        mask_qk = sb("mask_qk", [P, P], BF16)
        mask_kq = sb("mask_kq", [P, P], BF16)
        before = sb("before", [P, P], BF16)
        onesb = sb("onesb", [P, P], BF16)
        sum4 = sb("sum4", [P, E])
        woh = sb("woh", [P, KC, C], F32R)
        wol = sb("wol", [P, KC, C], F32R)
        biasT = sb("biasT", [P, 9 * MH])
        RB = 8 * MH
        phase = sem("phase")
        qs = [sb(f"qs{i}", [P, 2, HG, 512], BF16) for i in range(2)]
        ks = [sb(f"ks{i}", [P, 2, HG, 512], BF16) for i in range(4)]
        wstage = sb("wstage", [P, 2048])
        mxA = [sb(f"mxA{i}", [P, HG, 4]) for i in range(2)]
        mxB = [sb(f"mxB{i}", [P, HG, 4, 2]) for i in range(2)]
        mxBr = sb("mxBr", [P, HG * 4])
        nm = sb("nm", [16, P])

        banks = [ctx.enter_context(nc.psum_tensor(f"bank{i}", [P, 512], F32)) for i in range(8)]

        p1 = ExitStack()
        stage = sb("stage", [P, KC, H], stack=p1)
        wqs = sb("wqs", [P, KC, 3 * C], stack=p1)
        wos = sb("wos", [P, KC, C], stack=p1)
        brow = sb("brow", [9 * MH, P], stack=p1)
        rw1h = sb("rw1h", [P, KC, H], F32R, p1)
        rw1l = sb("rw1l", [P, KC, H], F32R, p1)
        wqh = sb("wqh", [P, KC, 3 * C], F32R, p1)
        wql = sb("wql", [P, KC, 3 * C], F32R, p1)
        rw2p = sb("rw2p", [P, MH, 32], F32, p1)
        rb2b = sb("rb2b", [P, E], F32, p1)
        fill = sb("fill", [P, 8, ROW], F32, p1)
        xb = [sb(f"xb{i}", [P, TB, C], F32, p1) for i in range(2)]
        xn = [sb(f"xn{i}", [P, TB, ROW], F32, p1) for i in range(2)]
        xTh = [sb(f"xTh{i}", [P, KC, BLK], F32R, p1) for i in range(2)]
        xTl = [sb(f"xTl{i}", [P, KC, BLK], F32R, p1) for i in range(2)]
        hT = sb("hT", [P, MH, BLK], F32, p1)
        ltp = sb("ltp", [P, BLK], F32, p1)
        qst = [sb(f"qst{i}", [P, PARTS, BLK], BF16, p1) for i in range(4)]
        res = [sb(f"res{i}", [P, BLK], F32, p1) for i in range(4)]
        vst = sb("vst", [P, TB, NH, 32], F32, p1)
        stats = sb("stats", [P, TB, 6], F32, p1)
        mv = sb("mv", [P, TB, 2], F32, p1)
        veps = sb("veps", [P, TB], F32, p1)
        rstd = sb("rstd", [P, TB], F32, p1)
        minus_half = sb("minus_half", [P, TB], F32, p1)
        small = {n: sb(n, [P, TB, E], F32, p1) for n in
                 ("lg", "lg2", "eq", "oh0", "oh1", "cand", "pv0", "pv1", "iota8", "slotbase", "place", "over", "sel0", "sel1")}
        one = {n: sb(n, [P, TB], F32, p1) for n in
               ("top0", "top1", "f0", "f1", "gap", "egap", "den2", "w0", "w1", "tokf")}
        m8 = sb("m8", [P, TB, E], BF16, p1)
        msum = sb("msum", [P, E], F32, p1)
        carry = sb("carry", [P, E], BF16, p1)
        slotf = [sb(f"slotf{i}", [P, 2, TB], F32, p1) for i in range(2)]
        slots = [sb(f"slot{i}", [P, 2 * TB], U32, p1) for i in range(2)]
        p1.close()

        p2 = ctx
        qs += [sb(f"qs{i}", [P, 2, HG, 512], BF16, p2) for i in (2, 3)]
        vh = [sb(f"vh{i}", [P, KT, HG, 32], F32, p2) for i in range(2)]
        pt = [sb(f"pt{i}", [P, HG, 512], F32, p2) for i in range(2)]
        att = [sb(f"att{i}", [P, 512], F32, p2) for i in range(2)]
        attc = sb("attc", [P, KC, T], F32, p2)
        atth = sb("atth", [P, KC, T], F32R, p2)
        attl = sb("attl", [P, KC, T], F32R, p2)
        den = sb("den", [P, 512], F32, p2)
        rden = sb("rden", [P, 512], F32, p2)
        rsum = sb("rsum", [P, 16], F32, p2)
        nmr = sb("nmr", [16, P], F32, p2)
        mparts = [sb(f"mparts{i}", [16, PARTS, P], BF16, p2) for i in range(2)]
        w1h = sb("w1h", [P, 2048], F32R, p2)
        w1l = sb("w1l", [P, 2048], F32R, p2)
        w2h = sb("w2h", [P, 2048], F32R, p2)
        w2l = sb("w2l", [P, 2048], F32R, p2)
        ebias = sb("ebias", [P, MH], F32, p2)
        eb2b = sb("eb2b", [P, C], F32, p2)
        xd = [sb(f"xd{i}", [P, 2, ROW], F32, p2) for i in range(2)]
        dTh = sb("dTh", [P, KC, CH], F32R, p2)
        dTl = sb("dTl", [P, KC, CH], F32R, p2)
        hf = [sb(f"hf{i}", [P, 2, CH], F32, p2) for i in range(2)]
        hh = sb("hh", [P, MH, CH], F32R, p2)
        hl = sb("hl", [P, MH, CH], F32R, p2)
        eo = [sb(f"eo{i}", [P, C], F32, p2) for i in range(2)]
        wob = [sb(f"wob{i}", [P, 2, C], F32, p2) for i in range(2)]
        tok = [sb(f"tok{i}", [P, 2], U32, p2) for i in range(2)]
        wgt = [sb(f"wgt{i}", [P, 2], F32, p2) for i in range(2)]

        s_load = sem("small_loads")
        s_rw1 = sem("rw1_loaded")
        s_wq = sem("wqkv_loaded")
        s_accx = sem("acc_holds_x")
        s_fill = sem("disp_filled")
        c_pool = sem("constants_by_pool")
        sum4_step = sem("sum4_step")
        k_ones = sem("ones_rows_of_k")
        c_dve = sem("constants_by_dve")
        c_bias = sem("bias_transposed")
        x_ready = [sem(f"x_ready{i}") for i in range(2)]
        var_ready = sem("variance_ready")
        rstd_ready = sem("rstd_ready")
        ln_done = sem("ln_done")
        xT_ready = sem("xT_ready")
        hi_done = sem("hi_done")
        lo_done = sem("lo_done")
        g_ready = sem("g_ready")
        g_act = sem("g_act")
        g_dve = sem("g_dve")
        b1_done = sem("first_part_done")
        b2_done = sem("second_part_done")
        split_done = sem("parts_done")
        q_stored = [sem(f"q_stored{i}") for i in range(4)]
        v_stored = sem("v_stored")
        l_ready = sem("logit_parts_ready")
        lt_done = sem("logit_parts_read")
        s_ready = sem("logits_ready")
        m_ready = sem("choice_ready")
        p_ready = sem("places_ready")
        p_read = sem("places_read")
        gap_ready = sem("gap_ready")
        e_done = sem("gap_exp_done")
        slot_ready = sem("slot_ready")
        scat = [sem(f"scattered{i}") for i in range(2)]
        dstep = sem("dve_step")
        pool_passed, dve_passed, sp_passed = sem("pool_passed"), sem("dve_passed"), sem("sp_passed")
        qk_ready = [sem(f"qk_ready{i}") for i in range(4)]
        v_ready = [sem(f"v_ready{i}") for i in range(2)]
        s1_ready = sem("s1_ready")
        s1_max = sem("s1_max")
        mb_ready = sem("max_of_late_queries")
        mt_ready = sem("max_transposed")
        mn_ready = sem("max_negated")
        mp_step = sem("max_parts_step")
        mp_ready = sem("max_parts_ready")
        m_rows = [sem("max_rows_early"), sem("max_rows_late")]
        s2_ready = sem("s2_ready")
        exp_done = sem("exp_done")
        av_done = sem("av_done")
        den_ready = sem("den_ready")
        att_done = sem("att_done")
        att_moved = [sem(f"att_moved{i}") for i in range(2)]
        att_zero = sem("att_zeroed")
        att_hi = sem("att_hi")
        att_split = sem("att_split")
        f_ready = sem("f_ready")
        f_act = sem("f_act")
        f_dve = sem("f_dve")
        t_ready = sem("first_chunk_transposed")
        t_done = sem("first_chunk_split")
        dhi_done = sem("dispatched_hi_done")
        tok_done = sem("token_rows_copied")
        h_hi = sem("h_hi_done")
        h_split = sem("h_split")
        w1_ld, w2_ld = sem("w1_loaded"), sem("w2_loaded")
        w1_hi, w2_hi = sem("w1_hi"), sem("w2_hi")
        w1_split, w2_split = sem("w1_split"), sem("w2_split")
        eb_ready = sem("expert_bias_ready")
        eb2_ld = sem("eb2_loaded")
        xd_ready = [sem(f"xd_ready{i}") for i in range(2)]
        eo_ready = sem("expert_rows_ready")
        added = sem("rows_added")
        s_out = sem("out_written")

        ringG = banks[0:4]
        bT = banks[4:6]
        bL, bR = banks[6], banks[7]
        GA, GD = 6, 8

        def g_end(g):
            if g < 8:
                return ("A", g // 2) if g % 2 == 0 else ("D", g // 2)
            return ("A", 4 + g - 8) if g < 10 else ("D", 4 + g - 10)

        def g_value(n, g):
            if g < 0:
                n, g = n - 1, g + 14
            who, k = g_end(g)
            return (g_act, (n + 2) * GA + k + 1) if who == "A" else (g_dve, (n + 2) * GD + k + 1)

        USES = []
        for g in range(NG):
            USES += [(g, "H0", "A"), (g, "H1", "A"), (g, "H2", "A"), (g, "H3", "A")]
            if g < 2:
                USES += [(g, f"W{2 * g}", "A"), (g, f"W{2 * g + 1}", "A")]
            USES += [(g, "S0", "D"), (g, "T", "D"), (g, "S1", "D")]
        FU = len(USES)
        FA = sum(e == "A" for _, _, e in USES)
        FD = FU - FA
        USE = {(g, k): n for n, (g, k, _) in enumerate(USES)}
        assert FU % 2 == 0

        def f_end(b, n):
            if n < 0:
                b, n = b - 1, n + FU
            who = USES[n][2]
            k = sum(USES[i][2] == who for i in range(n))
            return (f_act, (b + 1) * FA + k + 1) if who == "A" else (f_dve, (b + 1) * FD + k + 1)

        def f_full(b, g, k):
            return b * FU + USE[(g, k)] + 1

        ringF = banks[6:8]
        bS1 = banks[0:2]
        bS2 = banks[2:4]
        bAV = banks[4:6]

        def f_bank(g, k):
            return ringF[USE[(g, k)] % 2]

        ADDS = [(g, k) for g, k, _ in USES if k[0] in "SW"]
        ADD = {gk: n for n, gk in enumerate(ADDS)}
        NA = len(ADDS)

        def add_done(b, n):
            return 16 + b * NA * 16 + 16 * (n + 1)

        STEP2 = [(0, k) for k in range(4)] + [(1, k) for k in range(8)]
        STEP1 = [(q, 0) for q in range(4)] + [(4, 0), (4, 1), (5, 0), (6, 0), (6, 1), (7, 0), (7, 1), (5, 1)]
        NS = 12
        APART = 1000
        BASE = {"M1": (1, 1), "M0": (24, 24)}
        LONG = {**BASE, "H0": (0, 5), "H1": (6, 11), "H2": (12, 17), "H3": (18, 23)}
        SHORT = {**BASE, "H0": (0, 4), "H1": (5, 9), "H2": (10, 14), "H3": (15, 19)}
        SLOTS_G = [{**SHORT, "W0": (20, 23), "W1": (24, 27), "S0": (28, 37), "T": (38, 39), "S1": (40, 47)},
                   {**SHORT, "W2": (20, 23), "W3": (24, 27), "S0": (28, 37), "T": (38, 39), "S1": (40, 47)},
                   {**LONG, "S0": (24, 34), "T": (35, 36), "S1": (37, 47)},
                   {**LONG, "S0": (24, 42), "T": (43, 44)}]
        WORK = {"T": 4, "M": 1, "H": 12, "S": 24, "W": 12}

        def slices(g, slot):
            got = []
            for k, (a, z) in SLOTS_G[g].items():
                if a <= slot <= z:
                    w, n = WORK[k[0]], z - a + 1
                    got.append((k, (slot - a) * w // n, (slot - a + 1) * w // n))
            return got

        def after(g, slot, kinds, lag):
            return [k for k, (a, z) in SLOTS_G[g].items() if k[0] in kinds and slot == z + lag]

        def att_value(b, gg, c):
            return 4 + 4 * b + {(0, 0): 2, (0, 1): 3, (1, 0): 4, (1, 1): 5}[gg, c]

        def next_blk(i, p):
            return (1, i) if p == 0 else (0, i + 1)

        block = ctx.enter_context(nc.Block())

        @block.sync
        def _(sp):
            for i in range(4):
                sp.sem_inc(q_stored[i], 16)
            sp.sem_inc(v_stored, 16)
            x_blk = x.rearrange("b (c t p) d -> (b c) p t d", t=TB, p=P)

            def load_x(blk, p):
                sp.dma_start(xb[p][:, :, :], x_blk[blk, :, :, :]).then_inc(x_ready[p], 16)

            load_x(0, 0)
            sp.dma_start(stage[:, :, :], rw1.rearrange("(k p) n -> p k n", p=P)).then_inc(s_rw1, 16)
            sp.dma_start(wqs[:, :, :], w_qkv.rearrange("(k p) n -> p k n", p=P)).then_inc(s_wq, 16)
            sp.dma_start(brow[0:8 * MH, :], eb1.rearrange("e (m p) -> (e m) p", p=P)).then_inc(s_load, 16)
            sp.dma_start(brow[8 * MH:9 * MH, :], rb1.rearrange("(m p) -> m p", p=P)).then_inc(s_load, 16)
            sp.dma_start(rb2b[:, :], rb2.rearrange("(a e) -> a e", a=1).to_broadcast([P, E])).then_inc(s_load, 16)
            sp.wait_ge(c_dve, 1)
            sp.dma_start(rw2p[:, :, 0:E], rw2.rearrange("(m p) e -> p m e", p=P)).then_inc(s_load, 16)
            sp.dma_start(wos[:, :, :], w_o.rearrange("(k p) n -> p k n", p=P)).then_inc(s_load, 16)
            for i in range(2):
                sp.wait_ge(scat[i], 16)
            sp.wait_ge(c_pool, 2)
            for a in range(E):
                sp.dma_start(disp[a * CAP:(a + 1) * CAP, :].rearrange("(n p) r -> p n r", p=P),
                             fill[:, :, :]).then_inc(s_fill, 16)
            with sp.Fori(0, B) as i:
                for p in range(2):
                    n = 2 * i + p
                    q, iq = next_blk(i, p)
                    sp.wait_ge(ln_done, n + 1)
                    load_x((n + 1) % (2 * B), q)
                    if p == 0:
                        sp.dma_start(acc[0:N, :].rearrange("(b t) d -> b t d", t=T)[i, :, :], x[i, :, :]
                                     ).then_inc(s_accx, 16)
                    s, v = g_value(n, 9)
                    sp.wait_ge(s, v)
                    for g in range(NG):
                        sp.dma_start(vhd[i, g, :, TB * p:TB * (p + 1), :],
                                     vst[:, :, HG * g:HG * (g + 1), :].rearrange("p t j e -> p t (j e)")
                                     ).then_inc(v_stored, 16)
                    for k in range(4):
                        sp.wait_ge(split_done, 4 + 4 * n + k + 1)
                        sp.dma_start(qkd[i, k // 2, :, p, P * (k % 2):P * (k % 2 + 1), :]
                                     .rearrange("a r t -> r a t"), qst[k][:, :, :]).then_inc(q_stored[k], 16)
            def load_stack(dst, which, terms, b, g, ready):
                for t, part in enumerate(terms):
                    sp.dma_start(dst[DH * t:DH * (t + 1), :, :, :].rearrange("r c j t -> r c (j t)"),
                                 qkd[b, which, part, :, HG * DH * g:HG * DH * (g + 1), :]
                                 .rearrange("c (d j) t -> d c (j t)", d=DH)).then_inc(ready, 16)

            def load_v(b, g, buf):
                sp.dma_start(vh[buf][:, :, :, :], vhd[b, g, :, :, :]).then_inc(v_ready[buf], 16)

            def load_disp(c, buf):
                sp.dma_start(xd[buf][:, :, :], disp.rearrange("(c s p) r -> c p s r", s=2, p=P)[c, :, :, :]
                             ).then_inc(xd_ready[buf], 16)

            def load_w1(e):
                sp.dma_start(wstage[:, :].rearrange("p (k n) -> p k n", k=KC),
                             ew1.rearrange("e (k p) n -> e p k n", p=P)[e, :, :, :]).then_inc(w1_ld, 16)

            def load_w2(e):
                sp.dma_start(wstage[:, :].rearrange("p (m n) -> p m n", m=MH),
                             ew2.rearrange("e (m p) n -> e p m n", p=P)[e, :, :, :]).then_inc(w2_ld, 16)

            for i in range(4):
                sp.wait_ge(q_stored[i], 16 + 16 * 2 * B)
            sp.wait_ge(k_ones, 1)
            load_stack(ks[0], 1, TERMS_K, 0, 0, qk_ready[0])
            load_stack(qs[0], 0, TERMS_Q, 0, 0, qk_ready[0])
            load_w1(0)
            load_stack(ks[1], 1, TERMS_K, 0, 1, qk_ready[1])
            load_stack(qs[1], 0, TERMS_Q, 0, 1, qk_ready[1])
            sp.wait_ge(v_stored, 16 + 16 * 4 * 2 * B)
            sp.wait_ge(x_ready[0], 16 * (B + 1))
            sp.wait_ge(s_accx, 16 * B)
            for i in range(2):
                sp.wait_ge(scat[i], 16 + 128 * B)
            sp.sem_inc(phase, 1)
            sp.wait_ge(phase, 5)

            def store_max(u, h, g):
                sp.wait_ge(mp_ready, 1 + 2 * u + h + 1)
                for r in range(PARTS):
                    sp.dma_start(qs[g][KR + r:KR + r + 1, h, :, :]
                                 .rearrange("a j (t q) -> a (j t) q", q=P),
                                 mparts[h][:, r, :]).then_inc(m_rows[h], 16)

            def pack(b, g, c):
                u = NG * b + g
                sp.wait_ge(att_done, 2 + 2 * u + c + 1)
                sp.sem_inc(sp_passed, 1)
                sp.wait_ge(att_split, att_value(b - 1, g // 2, c))
                for j in range(HG):
                    row = DH * (HG * (g % 2) + j)
                    sp.dma_start(attc[row:row + DH, g // 2, 512 * c:512 * (c + 1)], att[c][32 * j:32 * j + DH, :]
                                 ).then_inc(att_moved[c], 16)

            load_v(0, 0, 0)
            load_disp(0, 0)
            store_max(0, 0, 0)
            sp.wait_ge(w1_split, 4)
            load_w2(0)
            with sp.Fori(0, B) as b:
                for g in range(NG):
                    u = NG * b + g
                    sp.wait_ge(av_done, 2 + NS * u)
                    load_v((b + (g + 1) // NG) % B, (g + 1) % NG, (g + 1) % 2)
                    g2 = (g + 2) % NG
                    b2 = (b + (g + 2) // NG) % B
                    store_max(u, 1, g)
                    if g:
                        pack(b, g - 1, 1)
                    load_stack(ks[g2], 1, TERMS_K, b2, g2, qk_ready[g2])
                    load_stack(qs[g2], 0, TERMS_Q, b2, g2, qk_ready[g2])
                    s, v = f_end(b, USE[(g - 1, "T")]) if g else f_end(b - 1, USE[(NG - 1, "T")])
                    sp.wait_ge(s, v)
                    load_disp((u + 1) % U, (g + 1) % 2)
                    if g == 0:
                        s, v = f_end(b - 1, USE[(NG - 1, "S1")])
                        sp.wait_ge(s, v)
                        sp.dma_start(eb2b[:, :], eb2[b, :].rearrange("(a n) -> a n", a=1).to_broadcast([P, C])
                                     ).then_inc(eb2_ld, 16)
                    if g == 1:
                        sp.wait_ge(w2_split, 4 * (b + 1))
                        load_w1((b + 1) % E)
                    pack(b, g, 0)
                    store_max(u + 1, 0, (g + 1) % NG)
                    if g == NG - 1:
                        sp.wait_ge(w1_split, 4 * (b + 2))
                        load_w2((b + 1) % E)
                        pack(b, g, 1)
            sp.wait_ge(added, 16 + 16 * (NA * B + 4))
            outf = out.rearrange("b t d -> (b t) d")
            for b in range(B):
                sp.dma_start(outf[T * b:T * (b + 1), :], acc[T * b:T * (b + 1), :]).then_inc(s_out, 16)
            sp.wait_ge(s_out, 16 * B)
            for i in range(4):
                sp.wait_ge(qk_ready[i], 192 * (B + (1 if i < 2 else 0)))
            sp.wait_ge(v_ready[0], 16 * (2 * B + 1))
            sp.wait_ge(xd_ready[0], 16 * (2 * B + 1))
            sp.wait_ge(w2_ld, 16 * (B + 1))
            sp.wait_ge(m_rows[0], 48 * (U + 2))
            for c in range(2):
                sp.wait_ge(att_moved[c], 64 * (U + 1))

        @block.gpsimd
        def _(pool):
            pool.sem_inc(split_done, 4)
            fi = fill[:, :, :].bitcast(I32)
            nc.gpsimd.memset(fill[:, :, :], 0.0).then_inc(c_pool, 1)
            pool.wait_ge(c_pool, 1)
            nc.gpsimd.iota(fi[:, :, TOKC:TOKC + 1], pattern=[[0, 8], [0, 1]], base=N, channel_multiplier=1
                           ).then_inc(c_pool, 1)
            nc.gpsimd.memset(ident[:, :], 0.0)
            nc.gpsimd.memset(identb[:, :], 0.0)
            nc.gpsimd.memset(mask_qk[:, :], 0.0)
            nc.gpsimd.memset(mask_kq[:, :], 0.0)
            nc.gpsimd.memset(before[:, :], 1.0)
            nc.gpsimd.memset(onesb[:, :], 1.0)
            nc.gpsimd.memset(sum4[:, :], 0.0)
            nc.gpsimd.memset(minus_half[:, :], -0.5)
            nc.gpsimd.iota(small["iota8"][:, :, :], pattern=[[0, TB], [1, E]], base=-E, channel_multiplier=0,
                           allow_small_or_imprecise_dtypes=True)
            nc.gpsimd.iota(small["slotbase"][:, :, :], pattern=[[0, TB], [CAP, E]], base=0, channel_multiplier=0,
                           allow_small_or_imprecise_dtypes=True)
            nc.gpsimd.iota(one["tokf"][:, :], pattern=[[P, TB]], base=0, channel_multiplier=1,
                           allow_small_or_imprecise_dtypes=True).then_inc(c_pool, 1)
            pool.wait_ge(c_pool, 3)
            for t in (ident, identb):
                nc.gpsimd.affine_select(out=t[:, :], in_=t[:, :], compare_op=ALU.not_equal, fill=1.0, base=0,
                                        pattern=[[-1, P]], channel_multiplier=1)
            nc.gpsimd.affine_select(out=mask_qk[:, :], in_=mask_qk[:, :], compare_op=ALU.is_ge, fill=-BIG, base=0,
                                    pattern=[[-1, P]], channel_multiplier=1)
            nc.gpsimd.affine_select(out=mask_kq[:, :], in_=mask_kq[:, :], compare_op=ALU.is_ge, fill=-BIG, base=0,
                                    pattern=[[1, P]], channel_multiplier=-1)
            nc.gpsimd.affine_select(out=before[:, :], in_=before[:, :], compare_op=ALU.is_gt, fill=0.0, base=0,
                                    pattern=[[1, P]], channel_multiplier=-1)
            for j in range(4):
                nc.gpsimd.affine_select(out=sum4[:, :], in_=sum4[:, :], compare_op=ALU.not_equal, fill=1.0,
                                        base=-32 * j, pattern=[[-1, E]], channel_multiplier=1).then_inc(sum4_step, 1)
                pool.wait_ge(sum4_step, j + 1)
            pool.sem_inc(c_pool, 1)
            pool.wait_ge(c_pool, 4)

            def inverse_deviation(n):
                pool.wait_ge(var_ready, n + 1)
                nc.gpsimd.tensor_tensor(rstd[:, :], veps[:, :], minus_half[:, :], ALU.pow).then_inc(rstd_ready, 1)

            for a, (lo, hi) in zip((scat[0], scat[1], added), ((0, 32), (32, 64), (64, 128))):
                pool.dma_start(acc[N + lo:N + hi, :], fill[lo:hi, 0, 0:C]).then_inc(a, 16)
            inverse_deviation(0)
            for i in range(4):
                o = nc.gpsimd.memset(ks[i][:, :, :, :], 1.0)
            o.then_inc(k_ones, 1)
            pool.wait_ge(s_fill, 16 * E)
            def settled():
                pool.sem_inc(pool_passed, 1)

            with pool.Fori(0, B) as i:
                for p in range(2):
                    n = 2 * i + p
                    inverse_deviation(n + 1)
                    for k in range(4):
                        pool.wait_ge(b2_done, 4 * n + k + 1)
                        nc.gpsimd.tensor_tensor(qst[k][:, 2, :], res[k][:, :], qst[k][:, 1, :],
                                                ALU.subtract).then_inc(split_done, 1)
                    pool.wait_ge(slot_ready, n + 1)
                    settled()
                    for k in range(2):
                        for t in range(TB):
                            nc.gpsimd.indirect_dma_start(
                                out=disp, out_offset=bass.IndirectOffsetOnAxis(
                                    ap=slots[p][:, TB * k + t:TB * k + t + 1], axis=0),
                                in_=xn[p][:, t, :], in_offset=None,
                                bounds_check=E * CAP - 1, oob_is_err=False).then_inc(scat[p], 16)
            for i in range(2):
                pool.wait_ge(scat[i], 16 + 128 * B)
            pool.wait_ge(added, 16)
            pool.drain().then_inc(phase, 1)
            pool.wait_ge(phase, 5)

            pool.sem_inc(mp_ready, 1)
            pool.sem_inc(h_split, 2)
            for h in range(2):
                pool.sem_inc(m_rows[h], 48)

            def low_w(e, i, hi_sem, done, wh, wl):
                pool.wait_ge(hi_sem, 4 * e + i + 1)
                q = slice(512 * i, 512 * (i + 1))
                nc.gpsimd.tensor_tensor(wl[:, q], wstage[:, q], wh[:, q].bitcast(F32), ALU.subtract).then_inc(done, 1)

            def low_att(b, gg, c):
                pool.wait_ge(att_hi, att_value(b, gg, c) - 4)
                q = slice(512 * c, 512 * (c + 1))
                nc.gpsimd.tensor_tensor(attl[:, gg, q], attc[:, gg, q], atth[:, gg, q].bitcast(F32), ALU.subtract
                                        ).then_inc(att_split, 1)

            def add_wo(b, r, prev):
                pool.wait_ge(added, prev)
                settled()
                pool.dma_start(acc[0:N, :].rearrange("(b k t p) c -> b k p t c", k=4, t=2, p=P)[b, r, :, :, :],
                               wob[r % 2][:, :, :], accum_op=ALU.add).then_inc(added, 16)

            def max_parts(u, h):
                M = 2 * u + h
                pool.wait_ge(m_rows[h], 48 * (u + 1))
                settled()
                nc.gpsimd.tensor_copy(mparts[h][:, 0, :], nm[:, :]).then_inc(mp_step, 1)
                pool.wait_ge(mp_step, 3 * M + 1)
                nc.gpsimd.tensor_tensor(nmr[:, :], nm[:, :], mparts[h][:, 0, :], ALU.subtract).then_inc(mp_step, 1)
                pool.wait_ge(mp_step, 3 * M + 2)
                settled()
                nc.gpsimd.tensor_copy(mparts[h][:, 1, :], nmr[:, :]).then_inc(mp_step, 1)
                pool.wait_ge(mp_step, 3 * M + 3)
                nc.gpsimd.tensor_tensor(mparts[h][:, 2, :], nmr[:, :], mparts[h][:, 1, :], ALU.subtract
                                        ).then_inc(mp_ready, 1)

            def part(b, g, k):
                u = NG * b + g
                if k[0] == "M":
                    pool.wait_ge(mn_ready, 2 * u + (2 if k == "M1" else 3))
                    if k == "M1":
                        max_parts(u, 1)
                    else:
                        max_parts(u + 1, 0)
                if k[0] == "H":
                    r = int(k[1])
                    pool.wait_ge(h_hi, 4 * u + r + 1)
                    nc.gpsimd.tensor_tensor(hl[:, 2 * r:2 * r + 2, :], hf[r % 2][:, :, :],
                                            hh[:, 2 * r:2 * r + 2, :].bitcast(F32), ALU.subtract).then_inc(h_split, 1)
                if k[0] == "S":
                    pool.wait_ge(added, add_done(b, ADD[(g, k)] - 1))
                    r = int(k[1])
                    pool.wait_ge(eo_ready, 2 * u + r + 1)
                    settled()
                    nc.gpsimd.indirect_dma_start(
                        out=acc, out_offset=bass.IndirectOffsetOnAxis(ap=tok[g % 2][:, r:r + 1], axis=0),
                        in_=eo[r][:, :], in_offset=None, bounds_check=N + P - 1, oob_is_err=True,
                        compute_op=ALU.add).then_inc(added, 16)
                if k[0] == "W":
                    r = int(k[1])
                    s, v = f_end(b, USE[(g, k)])
                    pool.wait_ge(s, v)
                    settled()
                    add_wo((b + B - 1) % B, r, add_done(b, ADD[(g, k)] - 1))

            pool.wait_ge(mn_ready, 1)
            max_parts(0, 0)
            for i in range(4):
                low_w(0, i, w1_hi, w1_split, w1h, w1l)
            for t in (attc, atth, attl):
                o = nc.gpsimd.memset(t[:, :, :].bitcast(F32), 0.0)
            o.then_inc(att_zero, 1)
            pool.sem_inc(att_split, 4)
            with pool.Fori(0, B) as b:
                for g in range(NG):
                    u = NG * b + g
                    part(b, g, "M1")
                    part(b, g, "H0")
                    if g == 0:
                        low_w(b, 0, w2_hi, w2_split, w2h, w2l)
                        low_w(b, 1, w2_hi, w2_split, w2h, w2l)
                    part(b, g, "H1")
                    if g == 0:
                        low_w(b, 2, w2_hi, w2_split, w2h, w2l)
                        low_w(b, 3, w2_hi, w2_split, w2h, w2l)
                    part(b, g, "H2")
                    part(b, g, "H3")
                    part(b, g, "M0")
                    if g % 2 == 0:
                        low_att(b if g else b - 1, 0 if g else 1, 1)
                    if g < 2:
                        part(b, g, f"W{2 * g}")
                        part(b, g, f"W{2 * g + 1}")
                    if g % 2:
                        low_att(b, g // 2, 0)
                    if g == NG - 1:
                        for i in range(4):
                            low_w(b + 1, i, w1_hi, w1_split, w1h, w1l)
                    part(b, g, "S0")
                    part(b, g, "S1")
            low_att(B - 1, 1, 1)
            for r in range(4):
                pool.wait_ge(f_act, (B + 1) * FA + r + 1)
                add_wo(B - 1, r, add_done(B, r - 1))
            pool.wait_ge(added, add_done(B, 3))

        @block.scalar
        def _(act):
            act.sem_inc(g_act, 2 * GA)

            def high(k, n, q):
                act.wait_ge(xT_ready, n + 1)
                nc.scalar.activation(xTh[q][:, k, :], bT[k][:, :], ACT.Copy).then_inc(hi_done, 1)

            act.wait_ge(c_bias, 2)
            act.wait_ge(c_dve, 2)
            for k in range(KC):
                high(k, 0, 0)
            with act.Fori(0, B) as i:
                for p in range(2):
                    n = 2 * i + p
                    q, iq = next_blk(i, p)
                    for m in range(0, 8, 2):
                        act.wait_ge(g_ready, 14 * n + m + 1)
                        nc.scalar.activation(hT[:, m, :], ringG[(14 * p + m) % 4][:, :], ACT.Relu,
                                             bias=biasT[:, RB + m:RB + m + 1]).then_inc(g_act, 1)
                    act.wait_ge(v_stored, 16 + 64 * n)
                    for k in range(2):
                        act.wait_ge(g_ready, 14 * n + 8 + k + 1)
                        nc.scalar.activation(vst[:, 2 * k:2 * k + 2, :, 0:DH],
                                             ringG[(14 * p + 8 + k) % 4][:, :].rearrange("p (t h d) -> p t h d", t=2, d=DH),
                                             ACT.Copy).then_inc(g_act, 1)
                    def second(k):
                        s, v = g_value(n, 10 + k)
                        act.wait_ge(s, v)
                        nc.scalar.activation(qst[k][:, 1, :], res[k][:, :], ACT.Copy).then_inc(b2_done, 1)

                    for k in range(4):
                        if k == 2:
                            for c in range(KC):
                                high(c, n + 1, q)
                            second(0)
                            second(1)
                            act.wait_ge(gap_ready, n + 1)
                            nc.scalar.activation(one["egap"][:, :], one["gap"][:, :], ACT.Exp).then_inc(e_done, 1)
                        act.wait_ge(q_stored[k], 16 * (n + 1))
                        act.wait_ge(g_ready, 14 * n + 10 + k + 1)
                        nc.scalar.activation(qst[k][:, 0, :], ringG[(14 * p + 10 + k) % 4][:, :], ACT.Copy
                                             ).then_inc(b1_done, 1)
                    second(2)
                    second(3)
            act.drain().then_inc(phase, 1)
            act.wait_ge(phase, 5)

            act.sem_inc(f_act, FA)
            act.sem_inc(exp_done, 2)
            RS = 1.0 / float(C) ** 0.5

            def exps(u, s, j):
                c, kt = STEP2[s]
                nq = 512 * (c + 1) - max(P * kt, 512 * c)
                if j == 0:
                    act.wait_ge(av_done, NS * u + s + 1)
                act.wait_ge(s2_ready, 48 * u + 4 * s + j + 1)
                nc.scalar.activation(pt[s % 2][:, j, 0:nq], bS2[j % 2][:, 0:nq], ACT.Exp, scale=RS
                                     ).then_inc(exp_done, 1)

            def high_chunk(bank):
                nc.scalar.activation(dTh[:, :, :], bank[:, :].rearrange("p (k n) -> p k n", k=KC), ACT.Copy
                                     ).then_inc(dhi_done, 1)

            def part(b, g, k):
                u = NG * b + g
                if k == "T":
                    act.wait_ge(f_ready, f_full(b, g, k))
                    high_chunk(f_bank(g, k))
                if k[0] == "H":
                    r = int(k[1])
                    act.wait_ge(eb_ready, b + 1)
                    act.wait_ge(h_split, 4 * u + r + 1)
                    act.wait_ge(f_ready, f_full(b, g, k))
                    for m in range(2):
                        o = nc.scalar.activation(hf[r % 2][:, m, :], f_bank(g, k)[:, CH * m:CH * (m + 1)], ACT.Relu,
                                                 bias=ebias[:, 2 * r + m:2 * r + m + 1])
                    o.then_inc(f_act, 1)
                if k[0] == "W":
                    r = int(k[1])
                    act.wait_ge(added, add_done(b, ADD[(0, f"W{r - 2}")]) if r >= 2 else add_done(b, -1))
                    act.wait_ge(f_ready, f_full(b, g, k))
                    nc.scalar.activation(wob[r % 2][:, :, :], f_bank(g, k)[:, :].rearrange("p (t c) -> p t c", t=2),
                                         ACT.Copy).then_inc(f_act, 1)

            def high_att(b, gg, c, moved):
                act.wait_ge(att_moved[c], moved)
                q = slice(512 * c, 512 * (c + 1))
                nc.scalar.activation(atth[:, gg, q], attc[:, gg, q], ACT.Copy).then_inc(att_hi, 1)

            def high_h(b, g, k):
                r = int(k[1])
                s, v = f_end(b, USE[(g, k)])
                act.wait_ge(s, v)
                nc.scalar.activation(hh[:, 2 * r:2 * r + 2, :], hf[r % 2][:, :, :], ACT.Copy).then_inc(h_hi, 1)

            def high_w(e, i, ld, hi_sem, wh):
                act.wait_ge(ld, 16 * (e + 1))
                nc.scalar.activation(wh[:, 512 * i:512 * (i + 1)], wstage[:, 512 * i:512 * (i + 1)], ACT.Copy
                                     ).then_inc(hi_sem, 1)

            for i in range(4):
                high_w(0, i, w1_ld, w1_hi, w1h)
            act.wait_ge(t_ready, 1)
            high_chunk(bAV[1])
            act.wait_ge(att_zero, 1)
            with act.Fori(0, B) as b:
                for g in range(NG):
                    for slot in range(NS * HG):
                        exps(NG * b + g, slot // HG, slot % HG)
                        for k in after(g, slot, "THW", 1):
                            part(b, g, k)
                        for k in after(g, slot, "H", 2):
                            high_h(b, g, k)
                        if g == NG - 1 and 29 <= slot < 33:
                            if slot == 29:
                                act.wait_ge(f_ready, f_full(b, g, "H3"))
                            high_w(b + 1, slot - 29, w1_ld, w1_hi, w1h)
                        if g == 0 and 4 <= slot < 8:
                            high_w(b, slot - 4, w2_ld, w2_hi, w2h)
                        if g % 2 == 0 and slot == 25:
                            if g == 2:
                                act.wait_ge(f_ready, f_full(b, 1, "W3"))
                            high_att(b if g else b - 1, 0 if g else 1, 1, 64 + 64 * (NG * b + g))
                        if g % 2 and slot == 34:
                            high_att(b, g // 2, 0, 64 + 64 * (NG * b + g + 1))
            high_att(B - 1, 1, 1, 64 + 64 * U)
            for r in range(4):
                act.wait_ge(added, add_done(B, r - 2) if r >= 2 else add_done(B, -1))
                act.wait_ge(f_ready, B * FU + r + 1)
                nc.scalar.activation(wob[r % 2][:, :, :], ringF[r % 2][:, :].rearrange("p (t c) -> p t c", t=2),
                                     ACT.Copy).then_inc(f_act, 1)

        @block.vector
        def _(dve):
            chain = {"base": 0, "n": 0}

            def link(ins):
                chain["n"] += 1
                ins.then_inc(dstep, 1)
                dve.wait_ge(dstep, chain["base"] + chain["n"])

            dve.sem_inc(g_dve, 2 * GD)
            dve.sem_inc(ln_done, 1)
            dve.sem_inc(lt_done, 1)
            dve.sem_inc(p_read, 1)
            nc.vector.memset(rw2p[:, :, :], 0.0).then_inc(c_dve, 1)
            nc.vector.memset(vst[:, :, :, :], 1.0)
            nc.vector.memset(carry[:, :], 0.0)
            for i in range(2):
                nc.vector.memset(xn[i][:, :, C:ROW], 0.0)
            dve.wait_ge(s_rw1, 16)
            link(nc.vector.tensor_copy(rw1h[:, :, :], stage[:, :, :]))
            nc.vector.tensor_tensor(rw1l[:, :, :], stage[:, :, :], rw1h[:, :, :].bitcast(F32), ALU.subtract
                                    ).then_inc(c_dve, 2)

            def layer_norm(n, q, iq):
                dve.wait_ge(x_ready[q], 16 * (iq + 1))
                for t in range(TB):
                    o = nc.vector.bn_stats(stats[:, t, :], xb[q][:, t, :])
                link(o)
                dve.sem_inc(dve_passed, 1)
                for t in range(TB):
                    o = nc.vector.bn_aggr(mv[:, t, :], stats[:, t, :])
                link(o)
                nc.vector.tensor_scalar(veps[:, :], mv[:, :, 1], EPS, None, ALU.add).then_inc(var_ready, 1)
                dve.wait_ge(rstd_ready, n + 1)
                dve.wait_ge(scat[q], 16 + 128 * iq)
                for t in range(TB):
                    o = nc.vector.tensor_scalar(xn[q][:, t, 0:C], xb[q][:, t, :], mv[:, t, 0:1], rstd[:, t:t + 1],
                                                ALU.subtract, ALU.mult)
                o.then_inc(ln_done, 1)

            def low(k, n, q):
                dve.wait_ge(hi_done, 2 * n + k + 1)
                nc.vector.tensor_tensor(xTl[q][:, k, :], bT[k][:, :], xTh[q][:, k, :].bitcast(F32), ALU.subtract
                                        ).then_inc(lo_done, 1)

            layer_norm(0, 0, 0)
            dve.wait_ge(c_bias, 1)
            nc.vector.tensor_copy(biasT[:, :], bL[:, 0:9 * MH]).then_inc(c_bias, 1)
            dve.wait_ge(s_wq, 16)
            dve.wait_ge(c_pool, 4)
            for k in range(KC):
                src = wqs[:, k, :].rearrange("p (g j s d) -> p s g d j", s=3, d=DH, j=HG)
                dh = wqh[:, k, 0:2 * C].rearrange("p (s g d j) -> p s g d j", s=2, d=DH, j=HG)
                dl = wql[:, k, 0:2 * C].rearrange("p (s g d j) -> p s g d j", s=2, d=DH, j=HG)
                vsrc = wqs[:, k, :].rearrange("p (h s d) -> p h s d", s=3, d=DH)[:, :, 2, :]
                vdh = wqh[:, k, 2 * C:3 * C].rearrange("p (h d) -> p h d", d=DH)
                vdl = wql[:, k, 2 * C:3 * C].rearrange("p (h d) -> p h d", d=DH)
                for s in range(2):
                    for g in range(NG):
                        nc.vector.tensor_copy(dh[:, s, g, :, :], src[:, s, g, :, :])
                link(nc.vector.tensor_copy(vdh, vsrc))
                for s in range(2):
                    for g in range(NG):
                        nc.vector.tensor_tensor(dl[:, s, g, :, :], src[:, s, g, :, :],
                                                dh[:, s, g, :, :].bitcast(F32), ALU.subtract)
                o = nc.vector.tensor_tensor(vdl, vsrc, vdh.bitcast(F32), ALU.subtract)
            o.then_inc(c_dve, 1)
            for k in range(KC):
                low(k, 0, 0)
            dve.wait_ge(s_load, 16 * 5)
            link(nc.vector.tensor_copy(woh[:, :, :], wos[:, :, :]))
            nc.vector.tensor_tensor(wol[:, :, :], wos[:, :, :], woh[:, :, :].bitcast(F32), ALU.subtract
                                    ).then_inc(c_dve, 1)
            start = chain["n"]

            def bc(ap):
                return ap.rearrange("p (t a) -> p t a", a=1).to_broadcast([P, TB, E])

            with dve.Fori(0, B) as i:
                S_ = small
                chain["base"] = start + i * CHAIN1
                chain["n"] = 0
                for p in range(2):
                    n = 2 * i + p
                    q, iq = next_blk(i, p)
                    for m in range(1, 8, 2):
                        dve.wait_ge(g_ready, 14 * n + m + 1)
                        nc.vector.tensor_scalar(hT[:, m, :], ringG[(14 * p + m) % 4][:, :],
                                                biasT[:, RB + m:RB + m + 1], 0.0, ALU.add, ALU.max).then_inc(g_dve, 1)
                    layer_norm(n + 1, q, iq)
                    dve.wait_ge(l_ready, n + 1)
                    nc.vector.tensor_copy(ltp[:, :], bL[:, :]).then_inc(lt_done, 1)

                    def rest(k):
                        dve.wait_ge(b1_done, 4 * n + k + 1)
                        dve.wait_ge(split_done, 4 * n + k + 1)
                        nc.vector.tensor_tensor(res[k][:, :], ringG[(14 * p + 10 + k) % 4][:, :],
                                                qst[k][:, 0, :], ALU.subtract).then_inc(g_dve, 1)

                    rest(0)
                    rest(1)
                    dve.wait_ge(s_ready, n + 1)
                    link(nc.vector.tensor_tensor(S_["lg"][:, :, :], bR[:, 0:TB * E].rearrange("p (t e) -> p t e", e=E),
                                                 rb2b[:, :].rearrange("p (a e) -> p a e", a=1).to_broadcast([P, TB, E]),
                                                 ALU.add))
                    for k, (lg, top, f, oh) in enumerate((("lg", "top0", "f0", "oh0"), ("lg2", "top1", "f1", "oh1"))):
                        if k == 1:
                            for c in range(KC):
                                low(c, n + 1, q)
                            link(nc.vector.scalar_tensor_tensor(S_["lg2"][:, :, :], S_["oh0"][:, :, :], -3.0e38,
                                                                S_["lg"][:, :, :], ALU.mult, ALU.add))
                        link(nc.vector.tensor_reduce(one[top][:, :], S_[lg][:, :, :], AX, ALU.max))
                        link(nc.vector.tensor_tensor(S_["eq"][:, :, :], S_[lg][:, :, :], bc(one[top][:, :]), ALU.is_equal))
                        link(nc.vector.tensor_tensor(S_["cand"][:, :, :], S_["eq"][:, :, :], S_["iota8"][:, :, :], ALU.mult))
                        link(nc.vector.tensor_reduce(one[f][:, :], S_["cand"][:, :, :], AX, ALU.min))
                        link(nc.vector.tensor_tensor(S_[oh][:, :, :], S_["iota8"][:, :, :], bc(one[f][:, :]), ALU.is_equal))
                    nc.vector.tensor_tensor(m8[:, :, :], S_["oh0"][:, :, :], S_["oh1"][:, :, :], ALU.add
                                            ).then_inc(m_ready, 1)
                    nc.vector.tensor_tensor(one["gap"][:, :], one["top1"][:, :], one["top0"][:, :], ALU.subtract
                                            ).then_inc(gap_ready, 1)
                    rest(2)
                    rest(3)
                    dve.wait_ge(e_done, n + 1)
                    link(nc.vector.tensor_scalar(one["den2"][:, :], one["egap"][:, :], 1.0, None, ALU.add))
                    link(nc.vector.reciprocal(one["w0"][:, :], one["den2"][:, :]))
                    nc.vector.tensor_tensor(S_["pv0"][:, :, :], S_["oh0"][:, :, :], bc(one["w0"][:, :]), ALU.mult)
                    link(nc.vector.tensor_tensor(one["w1"][:, :], one["w0"][:, :], one["egap"][:, :], ALU.mult))
                    link(nc.vector.tensor_tensor(S_["pv1"][:, :, :], S_["oh1"][:, :, :], bc(one["w1"][:, :]), ALU.mult))
                    nc.vector.tensor_tensor(xn[p][:, :, PVC:PVC + E], S_["pv0"][:, :, :], S_["pv1"][:, :, :], ALU.add)
                    link(nc.vector.tensor_copy(xn[p][:, :, TOKC:TOKC + 1].bitcast(U32),
                                               one["tokf"][:, :].rearrange("p (t a) -> p t a", a=1)))
                    link(nc.vector.tensor_scalar(one["tokf"][:, :], one["tokf"][:, :], float(BLK), None, ALU.add))
                    dve.wait_ge(p_ready, n + 1)
                    pos = bR[:, 64:64 + TB * E].rearrange("p (t e) -> p t e", e=E)
                    link(nc.vector.tensor_reduce(msum[:, :], m8[:, :, :].rearrange("p t e -> p e t"), AX, ALU.add))
                    nc.vector.tensor_tensor(carry[:, :], carry[:, :], msum[:, :], ALU.add)
                    nc.vector.tensor_scalar(S_["over"][:, :, :], pos, float(CAP), float(1 << 20), ALU.is_ge, ALU.mult)
                    link(nc.vector.tensor_tensor(S_["place"][:, :, :], pos, S_["slotbase"][:, :, :], ALU.add))
                    nc.vector.tensor_tensor(S_["cand"][:, :, :], S_["place"][:, :, :], S_["over"][:, :, :], ALU.add
                                            ).then_inc(p_read, 1)
                    dve.wait_ge(p_read, n + 2)
                    for k in range(2):
                        o = nc.vector.tensor_tensor(S_[f"sel{k}"][:, :, :], S_[f"oh{k}"][:, :, :], S_["cand"][:, :, :], ALU.mult)
                        if k == 1:
                            link(o)
                    for k in range(2):
                        o = nc.vector.tensor_reduce(slotf[p][:, k, :], S_[f"sel{k}"][:, :, :], AX, ALU.add)
                    link(o)
                    nc.vector.tensor_copy(slots[p][:, :], slotf[p][:, :, :].rearrange("p k t -> p (k t)")
                                          ).then_inc(slot_ready, 1)
                assert chain["n"] == CHAIN1, chain["n"]
            dve.drain().then_inc(phase, 1)

            dve.sem_inc(f_dve, FD)
            dve.sem_inc(s1_max, APART + 2)
            dve.sem_inc(att_done, 2)
            for c in range(2):
                dve.sem_inc(att_moved[c], 64)

            def reduce(u, s, j, par):
                qt, kc = STEP1[s]
                nk = 512 if kc < qt // 4 else P * (qt % 4 + 1)
                dve.wait_ge(s1_ready, 48 * u + 4 * s + j + 1)
                dst = mxA[par][:, j, qt:qt + 1] if qt < 4 else mxB[par][:, j, qt - 4, kc:kc + 1]
                nc.vector.tensor_reduce(dst, bS1[j % 2][:, 0:nk], AX, ALU.max).then_inc(s1_max, 1)

            def late_max(u, par):
                dve.wait_ge(s1_max, APART + 2 + 48 * (u + 1))
                nc.vector.tensor_reduce(mxBr[:, :], mxB[par][:, :, :, :].rearrange("p j t k -> p (j t) k"), AX, ALU.max
                                        ).then_inc(mb_ready, 1)

            def attend(u, g, c, stage):
                D = 3 * (2 * u + c)
                if stage == 0:
                    dve.wait_ge(av_done, 2 + NS * u + (4 if c == 0 else 12))
                    dve.wait_ge(att_done, 2 * u + c + 2)
                    nc.vector.transpose(den[:, :], bAV[c][:, :]).then_inc(den_ready, 1)
                if stage == 1:
                    dve.wait_ge(den_ready, D + 1)
                    nc.vector.reciprocal(rsum[:, :], den[:, :].rearrange("p (n r) -> p n r", r=32)[:, :, DH]
                                         ).then_inc(den_ready, 1)
                if stage == 2:
                    dve.wait_ge(den_ready, D + 2)
                    nc.vector.transpose(rden[:, :].rearrange("p (n r) -> p n r", r=32),
                                        rsum[:, :].rearrange("p (n a) -> p n a", a=1).to_broadcast([P, 16, 32])
                                        ).then_inc(den_ready, 1)
                if stage == 3:
                    dve.wait_ge(den_ready, D + 3)
                    dve.wait_ge(att_moved[c], 64 + 64 * u)
                    nc.vector.tensor_tensor(att[c][:, :], bAV[c][:, :], rden[:, :], ALU.mult
                                            ).then_inc(att_done, 1)

            def chunk_rows(i, e):
                nc.vector.tensor_copy(tok[i][:, :], xd[i][:, :, TOKC].bitcast(U32))
                nc.vector.tensor_copy(wgt[i][:, :].rearrange("p (s a) -> p s a", a=1), xd[i][:, :, bass.ds(e + PVC, 1)]
                                      ).then_inc(tok_done, 1)

            def low_chunk(bank):
                return nc.vector.tensor_tensor(dTl[:, :, :], bank[:, :].rearrange("p (k n) -> p k n", k=KC),
                                               dTh[:, :, :].bitcast(F32), ALU.subtract)

            def part(b, g, k):
                u = NG * b + g
                if k == "T":
                    dve.wait_ge(added, add_done(b, ADD[(g - 1, "S1")]) if g else add_done(b, -1))
                    dve.wait_ge(xd_ready[(g + 1) % 2], 16 * (2 * b + (g + 1) // 2 + 1))
                    chunk_rows((g + 1) % 2, b + (g + 1) // NG)
                    dve.wait_ge(dhi_done, u + 2)
                    low_chunk(f_bank(g, k)).then_inc(f_dve, 1)
                if k[0] == "M":
                    M = 2 * u + (1 if k == "M1" else 2)
                    dve.wait_ge(mp_ready, M + 1)
                    dve.wait_ge(mt_ready, M + 1)
                    nc.vector.tensor_scalar(nm[:, :], bAV[0][0:16, 0:P], -1.0, None, ALU.mult
                                            ).then_inc(mn_ready, 1)
                if k[0] == "S":
                    r = int(k[1])
                    n = ADD[(g, k)]
                    dve.wait_ge(added, add_done(b, ADD[(g - 1, k)]) if g else add_done(b, -1))
                    dve.wait_ge(eb2_ld, 16 * (b + 1))
                    dve.wait_ge(f_ready, f_full(b, g, k))
                    nc.vector.tensor_tensor(eo[r][:, :], f_bank(g, k)[:, 0:C], eb2b[:, :], ALU.add).then_inc(f_dve, 1)
                    s, v = f_end(b, USE[(g, k)])
                    dve.wait_ge(s, v)
                    nc.vector.tensor_scalar(eo[r][:, :], eo[r][:, :], wgt[g % 2][:, r:r + 1], None, ALU.mult
                                            ).then_inc(eo_ready, 1)

            for s in range(NS):
                for j in range(HG):
                    reduce(0, s, j, 0)
                if s == 6:
                    dve.wait_ge(mt_ready, 1)
                    nc.vector.tensor_scalar(nm[:, :], bAV[0][0:16, 0:P], -1.0, None, ALU.mult).then_inc(mn_ready, 1)
            late_max(0, 0)
            dve.wait_ge(phase, 5)
            dve.wait_ge(xd_ready[0], 16)
            chunk_rows(0, 0)
            dve.wait_ge(dhi_done, 1)
            low_chunk(bAV[1]).then_inc(t_done, 1)
            with dve.Fori(0, B) as b:
                for g in range(NG):
                    u = NG * b + g
                    if g == 0:
                        nc.vector.tensor_copy(ebias[:, :], biasT[:, bass.ds(b * MH, MH)]).then_inc(eb_ready, 1)
                        dve.wait_ge(eb_ready, b + 1)
                    for slot in range(NS * HG):
                        reduce(u + 1, slot // HG, slot % HG, (g + 1) % 2)
                        for k in after(g, slot, "TSM", 1):
                            part(b, g, k)
                        if 19 <= slot <= 22:
                            attend(u, g, 0, slot - 19)
                        if g and slot in (1, 2, 4, 5):
                            attend(u - 1, g - 1, 1, (1, 2, 4, 5).index(slot))
                    if g < NG - 1:
                        part(b, g, "S1")
                    dve.wait_ge(mt_ready, 2 * u + 2)
                    late_max(u + 1, (g + 1) % 2)
                    if g == NG - 1:
                        for st in range(4):
                            attend(u, g, 1, st)
                        part(b, g, "S1")

        @block.tensor
        def _(pe):
            mm = nc.tensor.matmul

            def pass3(dst, ah, al, bh, bl, t, first, last):
                a, b = ((ah, bh), (ah, bl), (al, bh))[t]
                return mm(dst, a, b, start=(first and t == 0), stop=(last and t == 2))

            def mm3(dst, ah, al, bh, bl, first, last):
                mm(dst, ah, bh, start=first, stop=False)
                mm(dst, ah, bl, start=False, stop=False)
                return mm(dst, al, bh, start=False, stop=last)

            pe.wait_ge(c_pool, 4)
            pe.wait_ge(s_load, 16 * 5)
            pe.wait_ge(c_dve, 1)
            nc.tensor.transpose(bL[:, 0:9 * MH], brow[:, :], ident[0:9 * MH, 0:9 * MH]).then_inc(c_bias, 1)
            pe.wait_ge(c_bias, 2)

            def transposes(n, q):
                pe.wait_ge(ln_done, n + 2)
                for k in range(KC):
                    for t in range(TB):
                        o = nc.tensor.transpose(bT[k][:, P * t:P * (t + 1)], xn[q][:, t, P * k:P * (k + 1)], ident[:, :])
                o.then_inc(xT_ready, 1)

            transposes(0, 0)
            pe.wait_ge(c_dve, 4)
            with pe.Fori(0, B) as i:
                for p in range(2):
                    n = 2 * i + p
                    q, iq = next_blk(i, p)
                    xh, xl = xTh[p], xTl[p]

                    def free(g):
                        s, v = g_value(n, g - 4)
                        pe.wait_ge(s, v)
                        return ringG[(14 * p + g) % 4]

                    pe.wait_ge(lo_done, 2 * n + 2)
                    for m in range(MH):
                        dst = free(m)
                        for k in range(KC):
                            o = mm3(dst[:, :], rw1h[:, k, P * m:P * (m + 1)], rw1l[:, k, P * m:P * (m + 1)],
                                    xh[:, k, :], xl[:, k, :], k == 0, k == KC - 1)
                        o.then_inc(g_ready, 1)
                    for h in range(2):
                        dst = free(8 + h)
                        for t in range(2):
                            ts = slice(P * (2 * h + t), P * (2 * h + t + 1))
                            for k in range(KC):
                                o = mm3(dst[:, C * t:C * (t + 1)], xh[:, k, ts], xl[:, k, ts],
                                        wqh[:, k, 2 * C:3 * C], wql[:, k, 2 * C:3 * C], k == 0, k == KC - 1)
                        o.then_inc(g_ready, 1)
                    for g in (6, 7):
                        s, v = g_value(n, g)
                        pe.wait_ge(s, v)
                    pe.wait_ge(lt_done, n + 1)
                    for r in range(2):
                        for j in range(4):
                            o = mm(bL[32 * j:32 * j + 32, :], rw2p[:, 4 * r + j, :], hT[:, 4 * r + j, :],
                                   start=(r == 0), stop=(r == 1), tile_position=(0, 32 * j), skip_group_check=True)
                    o.then_inc(l_ready, 1)

                    def qk_tile(k):
                        dst = free(10 + k)
                        for c in range(KC):
                            o = mm3(dst[:, :], wqh[:, c, P * k:P * (k + 1)], wql[:, c, P * k:P * (k + 1)],
                                    xh[:, c, :], xl[:, c, :], c == 0, c == KC - 1)
                        o.then_inc(g_ready, 1)

                    qk_tile(0)
                    qk_tile(1)
                    pe.wait_ge(lt_done, n + 2)
                    pe.wait_ge(p_read, n + 1)
                    for t in range(TB):
                        o = mm(bR[:, E * t:E * (t + 1)], ltp[:, P * t:P * (t + 1)], sum4[:, :], start=True, stop=True)
                    o.then_inc(s_ready, 1)
                    transposes(n + 1, q)
                    qk_tile(2)
                    qk_tile(3)
                    pe.wait_ge(m_ready, n + 1)
                    pos = bR[:, 64:64 + TB * E]
                    for t in range(TB):
                        d = pos[:, E * t:E * (t + 1)]
                        mm(d, before[:, :], m8[:, t, :], start=True, stop=False)
                        for tt in range(t):
                            mm(d, onesb[:, :], m8[:, tt, :], start=False, stop=False)
                        o = mm(d, onesb[:, :], carry[:, :], start=False, stop=True)
                    o.then_inc(p_ready, 1)
            pe.drain().then_inc(phase, 1)

            pe.sem_inc(av_done, 2)

            def s1_chunk(u, s, j, g):
                qt, kc = STEP1[s]
                diag = kc == qt // 4
                nk = P * (qt % 4 + 1) if diag else 512
                pe.wait_ge(s1_max, APART + 48 * u + 4 * s + j + 1)
                bank = bS1[j % 2]
                o = mm(bank[:, 0:nk], qs[g][0:KR, qt // 4, j, P * (qt % 4):P * (qt % 4 + 1)], ks[g][0:KR, kc, j, 0:nk],
                       start=True, stop=True)
                if diag:
                    o = mm(bank[:, nk - P:nk], identb[:, :], mask_qk[:, :], start=False, stop=True, skip_group_check=True)
                o.then_inc(s1_ready, 1)

            def s2_chunk(u, s, j, g):
                c, kt = STEP2[s]
                q0 = max(P * kt, 512 * c)
                nq = 512 * (c + 1) - q0
                diag = P * kt >= 512 * c
                pe.wait_ge(exp_done, 48 * u + 4 * s + j + 1)
                bank = bS2[j % 2]
                o = mm(bank[:, 0:nq], ks[g][0:KR + PARTS, kt // 4, j, P * (kt % 4):P * (kt % 4 + 1)],
                       qs[g][0:KR + PARTS, c, j, q0 - 512 * c:512],
                       start=True, stop=True)
                if diag:
                    o = mm(bank[:, 0:P], identb[:, :], mask_kq[:, :], start=False, stop=True, skip_group_check=True)
                o.then_inc(s2_ready, 1)

            def av_step(u, s, g):
                c, kt = STEP2[s]
                q0 = max(P * kt, 512 * c)
                nq = 512 * (c + 1) - q0
                pe.wait_ge(exp_done, 2 + 48 * u + 4 * s + 4)
                if kt == 0:
                    if c == 0:
                        pe.wait_ge(mn_ready, 2 * u + 2)
                    else:
                        pe.wait_ge(att_done, 2 * u + 2)
                for j in range(HG):
                    o = mm(bAV[c][32 * j:32 * j + 32, q0 - 512 * c:512], vh[g % 2][:, kt, j, :], pt[s % 2][:, j, 0:nq],
                           start=(kt == 0), stop=True, tile_position=(0, 32 * j), skip_group_check=True)
                o.then_inc(av_done, 1)

            def chunk_transpose(dst, buf, i):
                c, st = i // 2, i % 2
                return nc.tensor.transpose(dst[:, CH * c + P * st:CH * c + P * (st + 1)],
                                           xd[buf][:, st, P * c:P * (c + 1)], ident[:, :])

            def wo_pass(dst, r, i):
                t, gg, n = i // 6, i // 3 % 2, i % 3
                ts = slice(P * (2 * r + t), P * (2 * r + t + 1))
                return pass3(dst[:, C * t:C * (t + 1)], atth[:, gg, ts], attl[:, gg, ts], woh[:, gg, :], wol[:, gg, :],
                             n, gg == 0, gg == KC - 1)

            def part(b, g, k, lo, hi):
                u = NG * b + g
                dst = bAV[0] if k[0] == "M" else f_bank(g, k)
                r = int(k[1]) if len(k) > 1 else 0
                if lo == 0:
                    if k == "T":
                        pe.wait_ge(xd_ready[(g + 1) % 2], 16 * (2 * b + (g + 1) // 2 + 1))
                    if k[0] == "M":
                        pe.wait_ge(att_done, 2 * u + (3 if k == "M0" else 1))
                        if k == "M1":
                            pe.wait_ge(mn_ready, 2 * u + 1)
                    if k == "M0":
                        pe.wait_ge(s1_max, APART + 2 + 48 * (u + 1) + 16)
                    if k == "M1":
                        pe.wait_ge(mb_ready, u + 1)
                    if k == "H0":
                        if g == 0:
                            pe.wait_ge(w1_split, 4 * (b + 1))
                        s, v = f_end(b, USE[(g - 1, "T")]) if g else f_end(b - 1, USE[(NG - 1, "T")])
                        pe.wait_ge(s, v)
                    if k == "S0" and g == 0:
                        pe.wait_ge(w2_split, 4 * (b + 1))
                    if k in ("W0", "W2"):
                        pe.wait_ge(att_split, att_value(b - 1, 1, r // 2))
                    if k[0] != "M":
                        s, v = f_end(b, USE[(g, k)] - 2)
                        pe.wait_ge(s, v)
                for i in range(lo, hi):
                    if k == "T":
                        o = chunk_transpose(dst, (g + 1) % 2, i)
                    elif k == "M0":
                        o = nc.tensor.transpose(dst[0:16, 0:P], mxA[(g + 1) % 2][:, :, :].rearrange("p j t -> p (j t)"),
                                                ident[:, :])
                    elif k == "M1":
                        o = nc.tensor.transpose(dst[0:16, 0:P], mxBr[:, :], ident[:, :])
                    elif k[0] == "H":
                        h, c, t = i // 6, i // 3 % 2, i % 3
                        m = 2 * r + h
                        w = slice(H * c + P * m, H * c + P * (m + 1))
                        o = pass3(dst[:, CH * h:CH * (h + 1)], w1h[:, w], w1l[:, w], dTh[:, c, :], dTl[:, c, :],
                                  t, c == 0, c == KC - 1)
                    elif k[0] == "S":
                        m, t = i // 3, i % 3
                        if k == "S0" and i % 6 == 0:
                            pe.wait_ge(h_split, 2 + 4 * u + m // 2 + 1)
                        ss = slice(P * r, P * (r + 1))
                        w = slice(C * m, C * (m + 1))
                        o = pass3(dst[:, 0:C], hh[:, m, ss], hl[:, m, ss], w2h[:, w], w2l[:, w], t, m == 0, m == MH - 1)
                    else:
                        o = wo_pass(dst, r, i)
                if hi == WORK[k[0]]:
                    o.then_inc(mt_ready if k[0] == "M" else f_ready, 1)

            pe.wait_ge(g_act, (2 * B + 2) * GA)
            pe.wait_ge(g_dve, (2 * B + 2) * GD)
            pe.wait_ge(lo_done, 2 * (2 * B + 1))
            pe.wait_ge(qk_ready[0], 192)
            for s in range(NS):
                for j in range(HG):
                    s1_chunk(0, s, j, 0)
                if s == 5:
                    pe.wait_ge(s1_max, APART + 2 + 16)
                    nc.tensor.transpose(bAV[0][0:16, 0:P], mxA[0][:, :, :].rearrange("p j t -> p (j t)"), ident[:, :]
                                        ).then_inc(mt_ready, 1)
            pe.wait_ge(phase, 5)
            pe.wait_ge(xd_ready[0], 16)
            for i in range(WORK["T"]):
                o = chunk_transpose(bAV[1], 0, i)
            o.then_inc(t_ready, 1)
            pe.wait_ge(t_done, 1)
            with pe.Fori(0, B) as b:
                for g in range(NG):
                    u = NG * b + g
                    g1 = (g + 1) % NG
                    pe.wait_ge(qk_ready[g1], 192 * (b + 1 + (g + 1) // NG))
                    pe.wait_ge(v_ready[g % 2], 16 * (2 * b + g // 2 + 1))
                    pe.wait_ge(m_rows[0], 48 * (u + 2))
                    for slot in range(NS * HG):
                        s, j = slot // HG, slot % HG
                        if slot == 4 * HG:
                            pe.wait_ge(m_rows[1], 48 * (u + 2))
                        s2_chunk(u, s, j, g)
                        s1_chunk(u + 1, s, j, g1)
                        if j == 1 and s > 0:
                            av_step(u, s - 1, g)
                        for k, lo, hi in slices(g, slot):
                            part(b, g, k, lo, hi)
                    if g == NG - 1:
                        part(b, g, "S1", 0, 6)
                    av_step(u, NS - 1, g)
                    if g == NG - 1:
                        part(b, g, "S1", 6, WORK["S"])
            pe.wait_ge(att_split, att_value(B - 1, 1, 1))
            for r in range(4):
                s, v = f_end(B - 1, FU - 2 + r) if r < 2 else (f_act, (B + 1) * FA + r - 1)
                pe.wait_ge(s, v)
                for i in range(WORK["W"]):
                    o = wo_pass(ringF[r % 2], r, i)
                o.then_inc(f_ready, 1)


CHAIN1 = 48

_INS = ['L0_attn_x', 'L0_attn_w_qkv', 'L0_attn_w_o', 'L0_ffn_rw1', 'L0_ffn_rb1', 'L0_ffn_rw2', 'L0_ffn_rb2',
        'L0_ffn_ew1', 'L0_ffn_eb1', 'L0_ffn_ew2', 'L0_ffn_eb2']
_OUTS = [((8, 1024, 256), 'float32')]


def kernel(**inputs):
    import numpy as _np
    import concourse.bacc as _bacc
    from concourse import mybir as _mybir
    from concourse.bass_utils import run_bass_kernel_spmd as _run

    nc = _bacc.Bacc("TRN2", target_bir_lowering=False, num_devices=1)
    arrays, args = {}, []
    for name in _INS:
        a = _np.ascontiguousarray(inputs[name])
        arrays[f"in_{name}_dram"] = a
        args.append(nc.dram_tensor(f"in_{name}_dram", a.shape, _mybir.dt.from_np(a.dtype), kind="ExternalInput").ap())
    for i, (shape, dtype) in enumerate(_OUTS):
        dt = _mybir.dt.from_np(_np.dtype(dtype))
        args.append(nc.dram_tensor(f"out_{i}_dram", shape, dt, kind="ExternalOutput").ap())
    layer_kernel(nc, *args)
    r = _run(nc, [arrays], core_ids=[0])
    got = tuple(r.results[0][f"out_{i}_dram"] for i in range(len(_OUTS)))
    return got[0]
```

```python
from contextlib import ExitStack

import concourse.bass as bass
from concourse import mybir

F32 = mybir.dt.float32
F32R = mybir.dt.float32r
BF16 = mybir.dt.bfloat16
U32 = mybir.dt.uint32
I32 = mybir.dt.int32
ALU = mybir.AluOpType
ACT = mybir.ActivationFunctionType
AX = mybir.AxisListType.X

P = 128
BIG = 1.0e30
LOWEST = -3.4028234663852886e38
EPS = 1e-5
PARTS = 3
TERMS_Q = (0, 0, 0, 1, 1, 2)
TERMS_K = (0, 1, 2, 0, 1, 0)


def layer_kernel(nc, x, w_qkv, w_o, rw1, rb1, rw2, rb2, ew1, eb1, ew2, eb2, out):
    B, T, C = x.shape
    N = B * T
    H = rw1.shape[1]
    E = rw2.shape[1]
    CAP = 1024
    NH, DH = 16, 16
    KC = C // P
    MH = H // P
    BLK = 512
    TB = BLK // P
    HG = 4
    NG = NH // HG
    U = B * NG
    KT = T // P
    NT = len(TERMS_Q)
    KR = NT * DH
    ROW = 272
    TOKC, PVC = C, C + 4
    CH = 256
    assert (C, H, E, T, B) == (256, 1024, 8, 1024, 8) and N // BLK == 2 * B

    spare = nc.dram_tensor("spare", (P, C), F32).ap()
    disp = nc.dram_tensor("disp", (E * CAP, ROW), F32).ap()
    qkd = nc.dram_tensor("qk_parts", (B, 2, PARTS, 2, C, 512), BF16).ap()
    vhd = nc.dram_tensor("v_ones", (B, NG, P, KT, HG * 32), F32).ap()

    outf = out.rearrange("b t d -> (b t) d")

    ctx = ExitStack()
    with ctx:
        def sb(name, shape, dt=F32, stack=ctx):
            return stack.enter_context(nc.sbuf_tensor(name, shape, dt))

        def sem(name):
            return ctx.enter_context(nc.semaphore(name))

        ident = sb("ident", [P, P])
        causal = sb("causal", [P, 512], BF16)
        before = sb("before", [P, P], BF16)
        onesb = sb("onesb", [P, P], BF16)
        sum4 = sb("sum4", [P, E])
        woh = sb("woh", [P, KC, C], F32R)
        wol = sb("wol", [P, KC, C], F32R)
        biasT = sb("biasT", [P, 9 * MH])
        RB = 8 * MH
        phase = sem("phase")
        qs = [sb(f"qs{i}", [P, 2, HG, 512], BF16) for i in range(2)]
        ks = [sb(f"ks{i}", [P, 2, HG, 512], BF16) for i in range(4)]
        wstage = sb("wstage", [P, 2048])
        mxA = [sb(f"mxA{i}", [P, HG, 4]) for i in range(2)]
        mxB = [sb(f"mxB{i}", [P, HG, 4, 2]) for i in range(2)]
        mxBr = sb("mxBr", [P, HG * 4])
        nm = sb("nm", [16, P])
        nmr = sb("nmr", [16, P])
        mparts = [sb(f"mparts{i}", [16, PARTS, P], BF16) for i in range(2)]

        banks = [ctx.enter_context(nc.psum_tensor(f"bank{i}", [P, 512], F32)) for i in range(8)]

        p1 = ExitStack()
        stage = sb("stage", [P, KC, H], stack=p1)
        wqs = sb("wqs", [P, KC, 3 * C], stack=p1)
        wos = sb("wos", [P, KC, C], stack=p1)
        brow = sb("brow", [9 * MH, P], stack=p1)
        rw1h = sb("rw1h", [P, KC, H], F32R, p1)
        rw1l = sb("rw1l", [P, KC, H], F32R, p1)
        wqh = sb("wqh", [P, KC, 3 * C], F32R, p1)
        wql = sb("wql", [P, KC, 3 * C], F32R, p1)
        rw2p = sb("rw2p", [P, MH, 32], F32, p1)
        rb2b = sb("rb2b", [P, E], F32, p1)
        fill = sb("fill", [P, 8, ROW], F32, p1)
        xb = [sb(f"xb{i}", [P, TB, C], F32, p1) for i in range(2)]
        xn = [sb(f"xn{i}", [P, TB, ROW], F32, p1) for i in range(2)]
        xTh = [sb(f"xTh{i}", [P, KC, BLK], F32R, p1) for i in range(2)]
        xTl = [sb(f"xTl{i}", [P, KC, BLK], F32R, p1) for i in range(2)]
        hT = sb("hT", [P, MH, BLK], F32, p1)
        ltp = sb("ltp", [P, BLK], F32, p1)
        qst = [sb(f"qst{i}", [P, PARTS, BLK], BF16, p1) for i in range(4)]
        res = [sb(f"res{i}", [P, BLK], F32, p1) for i in range(4)]
        vst = sb("vst", [P, TB, NH, 32], F32, p1)
        stats = sb("stats", [P, TB, 6], F32, p1)
        mv = sb("mv", [P, TB, 2], F32, p1)
        veps = sb("veps", [P, TB], F32, p1)
        rstd = sb("rstd", [P, TB], F32, p1)
        minus_half = sb("minus_half", [P, TB], F32, p1)
        small = {n: sb(n, [P, TB, E], F32, p1) for n in
                 ("lg", "lg2", "eq", "oh0", "oh1", "cand", "pv0", "pv1", "iota8", "slotbase", "place", "over", "sel0", "sel1")}
        one = {n: sb(n, [P, TB], F32, p1) for n in
               ("top0", "top1", "f0", "f1", "gap", "egap", "den2", "w0", "w1", "tokf")}
        m8 = sb("m8", [P, TB, E], BF16, p1)
        msum = sb("msum", [P, E], F32, p1)
        carry = sb("carry", [P, E], BF16, p1)
        slotf = [sb(f"slotf{i}", [P, 2, TB], F32, p1) for i in range(2)]
        slots = [sb(f"slot{i}", [P, 2 * TB], U32, p1) for i in range(2)]
        p1.close()

        p2 = ctx
        qs += [sb(f"qs{i}", [P, 2, HG, 512], BF16, p2) for i in (2, 3)]
        vh = [sb(f"vh{i}", [P, KT, HG, 32], F32, p2) for i in range(2)]
        pt = [sb(f"pt{i}", [P, HG, 512], F32, p2) for i in range(2)]
        att = [sb(f"att{i}", [P, 512], F32, p2) for i in range(2)]
        attc = sb("attc", [P, KC, T], F32, p2)
        atth = sb("atth", [P, KC, T], F32R, p2)
        attl = sb("attl", [P, KC, T], F32R, p2)
        den = sb("den", [P, 512], F32, p2)
        rden = sb("rden", [P, 512], F32, p2)
        rsum = sb("rsum", [P, 16], F32, p2)
        w1h = sb("w1h", [P, 2048], F32R, p2)
        w1l = sb("w1l", [P, 2048], F32R, p2)
        w2h = sb("w2h", [P, 2048], F32R, p2)
        w2l = sb("w2l", [P, 2048], F32R, p2)
        ebias = sb("ebias", [P, MH], F32, p2)
        eb2b = sb("eb2b", [P, C], F32, p2)
        xd = [sb(f"xd{i}", [P, 2, ROW], F32, p2) for i in range(2)]
        dTh = sb("dTh", [P, KC, CH], F32R, p2)
        dTl = sb("dTl", [P, KC, CH], F32R, p2)
        hf = [sb(f"hf{i}", [P, 2, CH], F32, p2) for i in range(2)]
        hh = sb("hh", [P, MH, CH], F32R, p2)
        hl = sb("hl", [P, MH, CH], F32R, p2)
        eo = [sb(f"eo{i}", [P, C], F32, p2) for i in range(2)]
        wob = [sb(f"wob{i}", [P, 2, C], F32, p2) for i in range(2)]
        tok = [sb(f"tok{i}", [P, 2], U32, p2) for i in range(2)]
        wgt = [sb(f"wgt{i}", [P, 2], F32, p2) for i in range(2)]

        s_load = sem("small_loads")
        s_rw1 = sem("rw1_loaded")
        s_wq = sem("wqkv_loaded")
        s_outx = sem("out_holds_x")
        s_fill = sem("disp_filled")
        c_pool = sem("constants_by_pool")
        sum4_step = sem("sum4_step")
        k_ones = sem("ones_rows_of_k")
        c_dve = sem("constants_by_dve")
        c_bias = sem("bias_transposed")
        x_ready = [sem(f"x_ready{i}") for i in range(2)]
        var_ready = sem("variance_ready")
        rstd_ready = sem("rstd_ready")
        ln_done = sem("ln_done")
        xT_ready = sem("xT_ready")
        hi_done = sem("hi_done")
        lo_done = sem("lo_done")
        g_ready = sem("g_ready")
        g_act = sem("g_act")
        g_dve = sem("g_dve")
        b1_done = sem("first_part_done")
        b2_done = sem("second_part_done")
        split_done = sem("parts_done")
        q_stored = [sem(f"q_stored{i}") for i in range(4)]
        v_stored = sem("v_stored")
        l_ready = sem("logit_parts_ready")
        lt_done = sem("logit_parts_read")
        s_ready = sem("logits_ready")
        m_ready = sem("choice_ready")
        p_ready = sem("places_ready")
        p_read = sem("places_read")
        gap_ready = sem("gap_ready")
        e_done = sem("gap_exp_done")
        slot_ready = sem("slot_ready")
        scat = [sem(f"scattered{i}") for i in range(2)]
        dstep = sem("dve_step")
        pool_passed, dve_passed, sp_passed = sem("pool_passed"), sem("dve_passed"), sem("sp_passed")
        qk_ready = [sem(f"qk_ready{i}") for i in range(4)]
        v_ready = [sem(f"v_ready{i}") for i in range(2)]
        s1_ready = sem("s1_ready")
        s1_max = sem("s1_max")
        mb_ready = sem("max_of_late_queries")
        mt_ready = sem("max_transposed")
        mn_ready = sem("max_negated")
        mp_step = sem("max_parts_step")
        mp_ready = sem("max_parts_ready")
        m_rows = [sem("max_rows_early"), sem("max_rows_late")]
        s2_ready = sem("s2_ready")
        exp_done = sem("exp_done")
        masked = sem("exps_masked")
        av_done = sem("av_done")
        den_ready = sem("den_ready")
        att_done = sem("att_done")
        att_moved = [sem(f"att_moved{i}") for i in range(2)]
        att_zero = sem("att_zeroed")
        att_hi = sem("att_hi")
        att_split = sem("att_split")
        f_ready = sem("f_ready")
        f_act = sem("f_act")
        f_dve = sem("f_dve")
        t_ready = sem("first_chunk_transposed")
        t_done = sem("first_chunk_split")
        dhi_done = sem("dispatched_hi_done")
        tok_done = sem("token_rows_copied")
        h_hi = sem("h_hi_done")
        h_split = sem("h_split")
        w1_ld, w2_ld = sem("w1_loaded"), sem("w2_loaded")
        w1_hi, w2_hi = sem("w1_hi"), sem("w2_hi")
        w1_split, w2_split = sem("w1_split"), sem("w2_split")
        eb_ready = sem("expert_bias_ready")
        eb2_ld = sem("eb2_loaded")
        xd_ready = [sem(f"xd_ready{i}") for i in range(2)]
        eo_ready = sem("expert_rows_ready")
        added = sem("rows_added")

        ringG = banks[0:4]
        bT = banks[4:6]
        bL, bR = banks[6], banks[7]
        GA, GD = 6, 8

        def g_end(g):
            if g < 8:
                return ("A", g // 2) if g % 2 == 0 else ("D", g // 2)
            return ("A", 4 + g - 8) if g < 10 else ("D", 4 + g - 10)

        def g_value(n, g):
            if g < 0:
                n, g = n - 1, g + 14
            who, k = g_end(g)
            return (g_act, (n + 2) * GA + k + 1) if who == "A" else (g_dve, (n + 2) * GD + k + 1)

        WO_AT = [["W0"], ["W1", "W2"], ["W3"], []]
        USES = []
        for g in range(NG):
            USES += [(g, "H0", "A"), (g, "H1", "A"), (g, "H2", "A"), (g, "H3", "A")]
            USES += [(g, k, "A") for k in WO_AT[g]]
            USES += [(g, "S0", "D"), (g, "T", "D"), (g, "S1", "D")]
        FU = len(USES)
        FA = sum(e == "A" for _, _, e in USES)
        FD = FU - FA
        USE = {(g, k): n for n, (g, k, _) in enumerate(USES)}
        assert FU % 2 == 0

        def f_end(b, n):
            if n < 0:
                b, n = b - 1, n + FU
            who = USES[n][2]
            k = sum(USES[i][2] == who for i in range(n))
            return (f_act, (b + 1) * FA + k + 1) if who == "A" else (f_dve, (b + 1) * FD + k + 1)

        def f_full(b, g, k):
            return b * FU + USE[(g, k)] + 1

        ringF = banks[6:8]
        bS1 = banks[0:2]
        bS2 = banks[2:4]
        bAV = banks[4:6]

        def f_bank(g, k):
            return ringF[USE[(g, k)] % 2]

        ADDS = [(g, k) for g, k, _ in USES if k[0] in "SW"]
        ADD = {gk: n for n, gk in enumerate(ADDS)}
        NA = len(ADDS)

        def add_done(b, n):
            return 16 + b * NA * 16 + 16 * (n + 1)

        STEP2 = [(0, k) for k in range(4)] + [(1, k) for k in range(8)]
        STEP1 = [(q, 0) for q in range(4)] + [(4, 0), (4, 1), (5, 0), (6, 0), (7, 1), (7, 0), (6, 1), (5, 1)]
        NS = 12
        DIAG = [s for s, (c, kt) in enumerate(STEP2) if P * kt >= 512 * c]
        APART = 1000
        WORK = {"T": 4, "M": 1, "H": 12, "S": 24, "W": 12}

        def widths(slot):
            s, j = slot // HG, slot % HG
            qt, kc = STEP1[s]
            n2 = [512 * (c_ + 1) - max(P * k_, 512 * c_) for c_, k_ in STEP2]
            return n2[s], 512 if kc < qt // 4 else P * (qt % 4 + 1), n2[s - 1] if s and j == HG - 1 else 0

        ATT0, ATT1 = 20, 4

        M_AT = {"M1": 1, "M0": 25}

        def plan(g):
            parts = [k for gg, k, _ in USES if gg == g and not (g == NG - 1 and k == "S1")]
            total = sum(WORK[k[0]] for k in parts)
            own, others = [], []
            for slot in range(NS * HG):
                n2, n1, av = widths(slot)
                own.append((n2 + n1 + 4 * av) / 256)
                vec = 0.5 + 2.9 * n1 / 256 + (4.5 if ATT0 <= slot < ATT0 + 4 or (g and ATT1 <= slot < ATT1 + 4) else 0)
                others.append(max(vec, 0.8 + 2.2 * n2 / 256))
            level = 0.0
            while True:
                fill = [max(0, round(max(o, level) - w)) for o, w in zip(others, own)]
                if sum(fill) >= total:
                    break
                level += 0.02
            extra = sum(fill) - total
            for slot in reversed(range(NS * HG)):
                cut = min(extra, fill[slot], 1)
                fill[slot] -= cut
                extra -= cut
            return parts, fill

        def schedule(g):
            parts, fill = plan(g)
            slots, ends, k, done = [], dict(M_AT), 0, 0
            for slot, room in enumerate(fill):
                got = [(m, 0, 1) for m, a in M_AT.items() if a == slot]
                while room and k < len(parts):
                    n = min(room, WORK[parts[k][0]] - done)
                    got.append((parts[k], done, done + n))
                    done += n
                    room -= n
                    if done == WORK[parts[k][0]]:
                        ends[parts[k]] = slot
                        k, done = k + 1, 0
                slots.append(got)
            assert k == len(parts)
            return slots, ends

        SCHEDULE = [schedule(g) for g in range(NG)]

        def slices(g, slot):
            return SCHEDULE[g][0][slot]

        def after(g, slot, kinds, lag):
            return [k for k, z in SCHEDULE[g][1].items() if k[0] in kinds and slot == z + lag]

        def unended(g, kinds, lag):
            return [k for k, z in SCHEDULE[g][1].items() if k[0] in kinds and NS * HG <= z + lag]

        def att_value(b, gg, c):
            return 4 + 4 * b + {(0, 0): 2, (0, 1): 3, (1, 0): 4, (1, 1): 5}[gg, c]

        def next_blk(i, p):
            return (1, i) if p == 0 else (0, i + 1)

        block = ctx.enter_context(nc.Block())

        @block.sync
        def _(sp):
            for i in range(4):
                sp.sem_inc(q_stored[i], 16)
            sp.sem_inc(v_stored, 16)
            x_blk = x.rearrange("b (c t p) d -> (b c) p t d", t=TB, p=P)

            def load_x(blk, p):
                sp.dma_start(xb[p][:, :, :], x_blk[blk, :, :, :]).then_inc(x_ready[p], 16)

            load_x(0, 0)
            sp.dma_start(stage[:, :, :], rw1.rearrange("(k p) n -> p k n", p=P)).then_inc(s_rw1, 16)
            sp.dma_start(wqs[:, :, :], w_qkv.rearrange("(k p) n -> p k n", p=P)).then_inc(s_wq, 16)
            sp.dma_start(brow[0:8 * MH, :], eb1.rearrange("e (m p) -> (e m) p", p=P)).then_inc(s_load, 16)
            sp.dma_start(brow[8 * MH:9 * MH, :], rb1.rearrange("(m p) -> m p", p=P)).then_inc(s_load, 16)
            sp.dma_start(rb2b[:, :], rb2.rearrange("(a e) -> a e", a=1).to_broadcast([P, E])).then_inc(s_load, 16)
            sp.wait_ge(c_dve, 1)
            sp.dma_start(rw2p[:, :, 0:E], rw2.rearrange("(m p) e -> p m e", p=P)).then_inc(s_load, 16)
            sp.dma_start(wos[:, :, :], w_o.rearrange("(k p) n -> p k n", p=P)).then_inc(s_load, 16)
            for i in range(2):
                sp.wait_ge(scat[i], 16)
            sp.wait_ge(c_pool, 2)
            for a in range(E):
                sp.dma_start(disp[a * CAP:(a + 1) * CAP, :].rearrange("(n p) r -> p n r", p=P),
                             fill[:, :, :]).then_inc(s_fill, 16)
            def load_stack(dst, which, terms, b, g, ready):
                for t, part in enumerate(terms):
                    sp.dma_start(dst[DH * t:DH * (t + 1), :, :, :].rearrange("r c j t -> r c (j t)"),
                                 qkd[b, which, part, :, HG * DH * g:HG * DH * (g + 1), :]
                                 .rearrange("c (d j) t -> d c (j t)", d=DH)).then_inc(ready, 16)

            def load_v(b, g, buf):
                sp.dma_start(vh[buf][:, :, :, :], vhd[b, g, :, :, :]).then_inc(v_ready[buf], 16)

            def load_disp(c, buf):
                sp.dma_start(xd[buf][:, :, :], disp.rearrange("(c s p) r -> c p s r", s=2, p=P)[c, :, :, :]
                             ).then_inc(xd_ready[buf], 16)

            def load_w1(e):
                sp.dma_start(wstage[:, :].rearrange("p (k n) -> p k n", k=KC),
                             ew1.rearrange("e (k p) n -> e p k n", p=P)[e, :, :, :]).then_inc(w1_ld, 16)

            def load_w2(e):
                sp.dma_start(wstage[:, :].rearrange("p (m n) -> p m n", m=MH),
                             ew2.rearrange("e (m p) n -> e p m n", p=P)[e, :, :, :]).then_inc(w2_ld, 16)

            def loads(i, p):
                n = 2 * i + p
                q, iq = next_blk(i, p)
                sp.wait_ge(ln_done, n + 1)
                load_x((n + 1) % (2 * B), q)
                if p == 0:
                    sp.dma_start(out[i, :, :], x[i, :, :]).then_inc(s_outx, 16)

            def stores(i, p):
                n = 2 * i + p
                s, v = g_value(n, 9)
                sp.wait_ge(s, v)
                for g in range(NG):
                    sp.dma_start(vhd[i, g, :, TB * p:TB * (p + 1), :],
                                 vst[:, :, HG * g:HG * (g + 1), :].rearrange("p t j e -> p t (j e)")
                                 ).then_inc(v_stored, 16)
                for k in range(4):
                    sp.wait_ge(split_done, 4 + 4 * n + k + 1)
                    sp.dma_start(qkd[i, k // 2, :, p, P * (k % 2):P * (k % 2 + 1), :]
                                 .rearrange("a r t -> r a t"), qst[k][:, :, :]).then_inc(q_stored[k], 16)

            with sp.Fori(0, B - 1) as i:
                for p in range(2):
                    loads(i, p)
                    stores(i, p)
            loads(B - 1, 0)
            stores(B - 1, 0)
            loads(B - 1, 1)
            for k in range(4):
                sp.wait_ge(q_stored[k], 16 + 16 * (2 * B - 2))
            sp.wait_ge(k_ones, 1)
            load_stack(ks[0], 1, TERMS_K, 0, 0, qk_ready[0])
            load_stack(qs[0], 0, TERMS_Q, 0, 0, qk_ready[0])
            stores(B - 1, 1)
            load_w1(0)
            load_stack(ks[1], 1, TERMS_K, 0, 1, qk_ready[1])
            load_stack(qs[1], 0, TERMS_Q, 0, 1, qk_ready[1])
            for k in range(4):
                sp.wait_ge(q_stored[k], 16 + 16 * 2 * B)
            sp.wait_ge(v_stored, 16 + 16 * 4 * 2 * B)
            sp.wait_ge(x_ready[0], 16 * (B + 1))
            sp.wait_ge(s_outx, 16 * B)
            for i in range(2):
                sp.wait_ge(scat[i], 16 + 128 * B)
            sp.sem_inc(phase, 1)
            sp.wait_ge(phase, 5)

            def store_max(u, h, g):
                sp.wait_ge(mp_ready, 1 + 2 * u + h + 1)
                for r in range(PARTS):
                    sp.dma_start(qs[g][KR + r:KR + r + 1, h, :, :]
                                 .rearrange("a j (t q) -> a (j t) q", q=P),
                                 mparts[h][:, r, :]).then_inc(m_rows[h], 16)

            def pack(b, g, c):
                u = NG * b + g
                sp.wait_ge(att_done, 2 + 2 * u + c + 1)
                sp.sem_inc(sp_passed, 1)
                sp.wait_ge(att_split, att_value(b - 1, g // 2, c))
                for j in range(HG):
                    row = DH * (HG * (g % 2) + j)
                    sp.dma_start(attc[row:row + DH, g // 2, 512 * c:512 * (c + 1)], att[c][32 * j:32 * j + DH, :]
                                 ).then_inc(att_moved[c], 16)

            load_v(0, 0, 0)
            load_disp(0, 0)
            store_max(0, 0, 0)
            sp.wait_ge(w1_split, 4)
            load_w2(0)
            with sp.Fori(0, B) as b:
                for g in range(NG):
                    u = NG * b + g
                    sp.wait_ge(av_done, 2 + NS * u)
                    load_v((b + (g + 1) // NG) % B, (g + 1) % NG, (g + 1) % 2)
                    g2 = (g + 2) % NG
                    b2 = (b + (g + 2) // NG) % B
                    store_max(u, 1, g)
                    if g:
                        pack(b, g - 1, 1)
                    load_stack(ks[g2], 1, TERMS_K, b2, g2, qk_ready[g2])
                    load_stack(qs[g2], 0, TERMS_Q, b2, g2, qk_ready[g2])
                    s, v = f_end(b, USE[(g - 1, "T")]) if g else f_end(b - 1, USE[(NG - 1, "T")])
                    sp.wait_ge(s, v)
                    load_disp((u + 1) % U, (g + 1) % 2)
                    if g == 0:
                        s, v = f_end(b - 1, USE[(NG - 1, "S1")])
                        sp.wait_ge(s, v)
                        sp.dma_start(eb2b[:, :], eb2[b, :].rearrange("(a n) -> a n", a=1).to_broadcast([P, C])
                                     ).then_inc(eb2_ld, 16)
                    if g == 1:
                        sp.wait_ge(w2_split, 4 * (b + 1))
                        load_w1((b + 1) % E)
                    pack(b, g, 0)
                    store_max(u + 1, 0, (g + 1) % NG)
                    if g == NG - 1:
                        sp.wait_ge(w1_split, 4 * (b + 2))
                        load_w2((b + 1) % E)
                        pack(b, g, 1)
            sp.wait_ge(added, 16 + 16 * (NA * B + 4))
            for i in range(4):
                sp.wait_ge(qk_ready[i], 192 * (B + (1 if i < 2 else 0)))
            sp.wait_ge(v_ready[0], 16 * (2 * B + 1))
            sp.wait_ge(xd_ready[0], 16 * (2 * B + 1))
            sp.wait_ge(w2_ld, 16 * (B + 1))
            sp.wait_ge(m_rows[0], 48 * (U + 2))
            for c in range(2):
                sp.wait_ge(att_moved[c], 64 * (U + 1))

        @block.gpsimd
        def _(pool):
            pool.sem_inc(split_done, 4)
            fi = fill[:, :, :].bitcast(I32)
            nc.gpsimd.memset(fill[:, :, :], 0.0).then_inc(c_pool, 1)
            pool.wait_ge(c_pool, 1)
            nc.gpsimd.iota(fi[:, :, TOKC:TOKC + 1], pattern=[[0, 8], [0, 1]], base=N, channel_multiplier=1
                           ).then_inc(c_pool, 1)
            nc.gpsimd.memset(ident[:, :], 0.0)
            nc.gpsimd.memset(causal[:, :], 0.0)
            nc.gpsimd.memset(before[:, :], 1.0)
            nc.gpsimd.memset(onesb[:, :], 1.0)
            nc.gpsimd.memset(sum4[:, :], 0.0)
            nc.gpsimd.memset(minus_half[:, :], -0.5)
            nc.gpsimd.iota(small["iota8"][:, :, :], pattern=[[0, TB], [1, E]], base=-E, channel_multiplier=0,
                           allow_small_or_imprecise_dtypes=True)
            nc.gpsimd.iota(small["slotbase"][:, :, :], pattern=[[0, TB], [CAP, E]], base=0, channel_multiplier=0,
                           allow_small_or_imprecise_dtypes=True)
            nc.gpsimd.iota(one["tokf"][:, :], pattern=[[P, TB]], base=0, channel_multiplier=1,
                           allow_small_or_imprecise_dtypes=True).then_inc(c_pool, 1)
            pool.wait_ge(c_pool, 3)
            nc.gpsimd.affine_select(out=ident[:, :], in_=ident[:, :], compare_op=ALU.not_equal, fill=1.0, base=0,
                                    pattern=[[-1, P]], channel_multiplier=1)
            nc.gpsimd.affine_select(out=causal[:, 512 - P:512], in_=causal[:, 512 - P:512], compare_op=ALU.is_ge,
                                    fill=-BIG, base=0, pattern=[[-1, P]], channel_multiplier=1)
            nc.gpsimd.affine_select(out=before[:, :], in_=before[:, :], compare_op=ALU.is_gt, fill=0.0, base=0,
                                    pattern=[[1, P]], channel_multiplier=-1)
            for j in range(4):
                nc.gpsimd.affine_select(out=sum4[:, :], in_=sum4[:, :], compare_op=ALU.not_equal, fill=1.0,
                                        base=-32 * j, pattern=[[-1, E]], channel_multiplier=1).then_inc(sum4_step, 1)
                pool.wait_ge(sum4_step, j + 1)
            pool.sem_inc(c_pool, 1)
            pool.wait_ge(c_pool, 4)

            def inverse_deviation(n):
                pool.wait_ge(var_ready, n + 1)
                nc.gpsimd.tensor_tensor(rstd[:, :], veps[:, :], minus_half[:, :], ALU.pow).then_inc(rstd_ready, 1)

            for a, (lo, hi) in zip((scat[0], scat[1], added), ((0, 32), (32, 64), (64, 128))):
                pool.dma_start(spare[lo:hi, :], fill[lo:hi, 0, 0:C]).then_inc(a, 16)
            inverse_deviation(0)
            for i in range(4):
                o = nc.gpsimd.memset(ks[i][:, :, :, :], 1.0)
            o.then_inc(k_ones, 1)
            pool.wait_ge(s_fill, 16 * E)
            def settled():
                pool.sem_inc(pool_passed, 1)

            with pool.Fori(0, B) as i:
                for p in range(2):
                    n = 2 * i + p
                    inverse_deviation(n + 1)
                    for k in range(4):
                        pool.wait_ge(b2_done, 4 * n + k + 1)
                        nc.gpsimd.tensor_tensor(qst[k][:, 2, :], res[k][:, :], qst[k][:, 1, :],
                                                ALU.subtract).then_inc(split_done, 1)
                    pool.wait_ge(slot_ready, n + 1)
                    settled()
                    for k in range(2):
                        for t in range(TB):
                            nc.gpsimd.indirect_dma_start(
                                out=disp, out_offset=bass.IndirectOffsetOnAxis(
                                    ap=slots[p][:, TB * k + t:TB * k + t + 1], axis=0),
                                in_=xn[p][:, t, :], in_offset=None,
                                bounds_check=E * CAP - 1, oob_is_err=False).then_inc(scat[p], 16)
            for i in range(2):
                pool.wait_ge(scat[i], 16 + 128 * B)
            pool.wait_ge(added, 16)
            pool.drain().then_inc(phase, 1)
            pool.wait_ge(phase, 5)

            pool.sem_inc(h_split, 2)

            def low_w(e, i, hi_sem, done, wh, wl):
                pool.wait_ge(hi_sem, 4 * e + i + 1)
                q = slice(512 * i, 512 * (i + 1))
                nc.gpsimd.tensor_tensor(wl[:, q], wstage[:, q], wh[:, q].bitcast(F32), ALU.subtract).then_inc(done, 1)

            def mask(u, s):
                pool.wait_ge(exp_done, 2 + 48 * u + 4 * s + 4)
                settled()
                nc.gpsimd.affine_select(out=pt[s % 2][:, :, 0:P], in_=pt[s % 2][:, :, 0:P], compare_op=ALU.is_ge,
                                        fill=0.0, base=0, pattern=[[0, HG], [1, P]], channel_multiplier=-1
                                        ).then_inc(masked, 1)

            def low_att(b, gg, c):
                pool.wait_ge(att_hi, att_value(b, gg, c) - 4)
                q = slice(512 * c, 512 * (c + 1))
                nc.gpsimd.tensor_tensor(attl[:, gg, q], attc[:, gg, q], atth[:, gg, q].bitcast(F32), ALU.subtract
                                        ).then_inc(att_split, 1)

            def add_wo(b, r, prev):
                pool.wait_ge(added, prev)
                settled()
                pool.dma_start(outf.rearrange("(b k t p) c -> b k p t c", k=4, t=2, p=P)[b, r, :, :, :],
                               wob[r % 2][:, :, :], accum_op=ALU.add).then_inc(added, 16)

            def part(b, g, k):
                u = NG * b + g
                if k[0] == "H":
                    r = int(k[1])
                    pool.wait_ge(h_hi, 4 * u + r + 1)
                    nc.gpsimd.tensor_tensor(hl[:, 2 * r:2 * r + 2, :], hf[r % 2][:, :, :],
                                            hh[:, 2 * r:2 * r + 2, :].bitcast(F32), ALU.subtract).then_inc(h_split, 1)
                if k[0] == "S":
                    pool.wait_ge(added, add_done(b, ADD[(g, k)] - 1))
                    r = int(k[1])
                    pool.wait_ge(eo_ready, 2 * u + r + 1)
                    settled()
                    nc.gpsimd.indirect_dma_start(
                        out=outf, out_offset=bass.IndirectOffsetOnAxis(ap=tok[g % 2][:, r:r + 1], axis=0),
                        in_=eo[r][:, :], in_offset=None, bounds_check=N - 1, oob_is_err=False,
                        compute_op=ALU.add).then_inc(added, 16)
                if k[0] == "W":
                    r = int(k[1])
                    s, v = f_end(b, USE[(g, k)])
                    pool.wait_ge(s, v)
                    settled()
                    add_wo((b + B - 1) % B, r, add_done(b, ADD[(g, k)] - 1))

            for i in range(4):
                low_w(0, i, w1_hi, w1_split, w1h, w1l)
            for t in (attc, atth, attl):
                o = nc.gpsimd.memset(t[:, :, :].bitcast(F32), 0.0)
            o.then_inc(att_zero, 1)
            pool.sem_inc(att_split, 4)
            with pool.Fori(0, B) as b:
                for g in range(NG):
                    u = NG * b + g
                    mask(u, 0)
                    if g == 0:
                        low_w(b, 0, w2_hi, w2_split, w2h, w2l)
                        low_w(b, 1, w2_hi, w2_split, w2h, w2l)
                    mask(u, 1)
                    part(b, g, "H0")
                    if g == 0:
                        low_w(b, 2, w2_hi, w2_split, w2h, w2l)
                    mask(u, 2)
                    part(b, g, "H1")
                    if g == 0:
                        low_w(b, 3, w2_hi, w2_split, w2h, w2l)
                    mask(u, 3)
                    part(b, g, "H2")
                    part(b, g, "H3")
                    if g == 0:
                        low_att(b - 1, 1, 1)
                    for k in WO_AT[g]:
                        part(b, g, k)
                    if g:
                        low_att(b, (g - 1) // 2, 1 - g % 2)
                    if g == NG - 1:
                        low_w(b + 1, 0, w1_hi, w1_split, w1h, w1l)
                    mask(u, 8)
                    if g == NG - 1:
                        low_w(b + 1, 1, w1_hi, w1_split, w1h, w1l)
                    mask(u, 9)
                    if g == NG - 1:
                        low_w(b + 1, 2, w1_hi, w1_split, w1h, w1l)
                    else:
                        part(b, g, "S0")
                    mask(u, 10)
                    if g == NG - 1:
                        low_w(b + 1, 3, w1_hi, w1_split, w1h, w1l)
                    mask(u, 11)
                    if g == NG - 1:
                        part(b, g, "S0")
                    part(b, g, "S1")
            for r in range(4):
                if r == 2:
                    low_att(B - 1, 1, 1)
                pool.wait_ge(f_act, (B + 1) * FA + r + 1)
                add_wo(B - 1, r, add_done(B, r - 1))
            pool.wait_ge(added, add_done(B, 3))

        @block.scalar
        def _(act):
            act.sem_inc(g_act, 2 * GA)

            def high(k, n, q):
                act.wait_ge(xT_ready, n + 1)
                nc.scalar.activation(xTh[q][:, k, :], bT[k][:, :], ACT.Copy).then_inc(hi_done, 1)

            act.wait_ge(c_bias, 2)
            act.wait_ge(c_dve, 2)
            for k in range(KC):
                high(k, 0, 0)
            with act.Fori(0, B) as i:
                for p in range(2):
                    n = 2 * i + p
                    q, iq = next_blk(i, p)
                    for m in range(0, 8, 2):
                        act.wait_ge(g_ready, 14 * n + m + 1)
                        nc.scalar.activation(hT[:, m, :], ringG[(14 * p + m) % 4][:, :], ACT.Relu,
                                             bias=biasT[:, RB + m:RB + m + 1]).then_inc(g_act, 1)
                    act.wait_ge(v_stored, 16 + 64 * n)
                    for k in range(2):
                        act.wait_ge(g_ready, 14 * n + 8 + k + 1)
                        nc.scalar.activation(vst[:, 2 * k:2 * k + 2, :, 0:DH],
                                             ringG[(14 * p + 8 + k) % 4][:, :].rearrange("p (t h d) -> p t h d", t=2, d=DH),
                                             ACT.Copy).then_inc(g_act, 1)
                    def second(k):
                        s, v = g_value(n, 10 + k)
                        act.wait_ge(s, v)
                        nc.scalar.activation(qst[k][:, 1, :], res[k][:, :], ACT.Copy).then_inc(b2_done, 1)

                    for k in range(4):
                        if k == 2:
                            for c in range(KC):
                                high(c, n + 1, q)
                            second(0)
                            second(1)
                            act.wait_ge(gap_ready, n + 1)
                            nc.scalar.activation(one["egap"][:, :], one["gap"][:, :], ACT.Exp).then_inc(e_done, 1)
                        act.wait_ge(q_stored[k], 16 * (n + 1))
                        act.wait_ge(g_ready, 14 * n + 10 + k + 1)
                        nc.scalar.activation(qst[k][:, 0, :], ringG[(14 * p + 10 + k) % 4][:, :], ACT.Copy
                                             ).then_inc(b1_done, 1)
                    second(2)
                    second(3)
            act.drain().then_inc(phase, 1)
            act.wait_ge(phase, 5)

            act.sem_inc(f_act, FA)
            act.sem_inc(exp_done, 2)
            RS = 1.0 / float(C) ** 0.5

            def exps(u, s, j):
                c, kt = STEP2[s]
                nq = 512 * (c + 1) - max(P * kt, 512 * c)
                if j == 0:
                    act.wait_ge(av_done, NS * u + s + 1)
                act.wait_ge(s2_ready, 48 * u + 4 * s + j + 1)
                nc.scalar.activation(pt[s % 2][:, j, 0:nq], bS2[j % 2][:, 0:nq], ACT.Exp, scale=RS
                                     ).then_inc(exp_done, 1)

            def high_chunk(bank):
                nc.scalar.activation(dTh[:, :, :], bank[:, :].rearrange("p (k n) -> p k n", k=KC), ACT.Copy
                                     ).then_inc(dhi_done, 1)

            def part(b, g, k):
                u = NG * b + g
                if k == "T":
                    act.wait_ge(f_ready, f_full(b, g, k))
                    high_chunk(f_bank(g, k))
                if k[0] == "H":
                    r = int(k[1])
                    act.wait_ge(eb_ready, b + 1)
                    act.wait_ge(h_split, 4 * u + r + 1)
                    act.wait_ge(f_ready, f_full(b, g, k))
                    for m in range(2):
                        o = nc.scalar.activation(hf[r % 2][:, m, :], f_bank(g, k)[:, CH * m:CH * (m + 1)], ACT.Relu,
                                                 bias=ebias[:, 2 * r + m:2 * r + m + 1])
                    o.then_inc(f_act, 1)
                if k[0] == "W":
                    r = int(k[1])
                    act.wait_ge(added, add_done(b, ADD[(r - 2, f"W{r - 2}")]) if r >= 2 else add_done(b, -1))
                    act.wait_ge(f_ready, f_full(b, g, k))
                    nc.scalar.activation(wob[r % 2][:, :, :], f_bank(g, k)[:, :].rearrange("p (t c) -> p t c", t=2),
                                         ACT.Copy).then_inc(f_act, 1)

            def high_att(b, gg, c, moved):
                act.wait_ge(att_moved[c], moved)
                q = slice(512 * c, 512 * (c + 1))
                nc.scalar.activation(atth[:, gg, q], attc[:, gg, q], ACT.Copy).then_inc(att_hi, 1)

            def high_h(b, g, k):
                r = int(k[1])
                s, v = f_end(b, USE[(g, k)])
                act.wait_ge(s, v)
                nc.scalar.activation(hh[:, 2 * r:2 * r + 2, :], hf[r % 2][:, :, :], ACT.Copy).then_inc(h_hi, 1)

            def high_w(e, i, ld, hi_sem, wh):
                act.wait_ge(ld, 16 * (e + 1))
                nc.scalar.activation(wh[:, 512 * i:512 * (i + 1)], wstage[:, 512 * i:512 * (i + 1)], ACT.Copy
                                     ).then_inc(hi_sem, 1)

            for i in range(4):
                high_w(0, i, w1_ld, w1_hi, w1h)
            act.wait_ge(t_ready, 1)
            high_chunk(bAV[1])
            act.wait_ge(att_zero, 1)
            with act.Fori(0, B) as b:
                for g in range(NG):
                    for slot in range(NS * HG):
                        exps(NG * b + g, slot // HG, slot % HG)
                        for k in after(g, slot, "THW", 1):
                            part(b, g, k)
                        for k in after(g, slot, "H", 2):
                            high_h(b, g, k)
                        w = slot - SCHEDULE[g][1]["H3"] - 3
                        if g == NG - 1 and 0 <= w < 4:
                            if w == 0:
                                act.wait_ge(f_ready, f_full(b, g, "H3"))
                            high_w(b + 1, w, w1_ld, w1_hi, w1h)
                        if g == 0 and 4 <= slot < 8:
                            high_w(b, slot - 4, w2_ld, w2_hi, w2h)
                        if g == 0 and slot == 25:
                            high_att(b - 1, 1, 1, 64 + 64 * (NG * b))
                        if g and slot == 33:
                            if g < 3:
                                act.wait_ge(f_ready, f_full(b, g, ("W1", "W3")[g - 1]))
                            high_att(b, (g - 1) // 2, 1 - g % 2, 64 + 64 * (NG * b + g + g % 2))
            for r in range(4):
                if r == 2:
                    high_att(B - 1, 1, 1, 64 + 64 * U)
                act.wait_ge(added, add_done(B, r - 2) if r >= 2 else add_done(B, -1))
                act.wait_ge(f_ready, B * FU + r + 1)
                nc.scalar.activation(wob[r % 2][:, :, :], ringF[r % 2][:, :].rearrange("p (t c) -> p t c", t=2),
                                     ACT.Copy).then_inc(f_act, 1)

        @block.vector
        def _(dve):
            chain = {"base": 0, "n": 0}

            def link(ins):
                chain["n"] += 1
                ins.then_inc(dstep, 1)
                dve.wait_ge(dstep, chain["base"] + chain["n"])

            dve.sem_inc(g_dve, 2 * GD)
            dve.sem_inc(ln_done, 1)
            dve.sem_inc(lt_done, 1)
            dve.sem_inc(p_read, 1)
            nc.vector.memset(rw2p[:, :, :], 0.0).then_inc(c_dve, 1)
            nc.vector.memset(vst[:, :, :, :], 1.0)
            nc.vector.memset(carry[:, :], 0.0)
            for i in range(2):
                nc.vector.memset(xn[i][:, :, C:ROW], 0.0)
            dve.wait_ge(s_rw1, 16)
            link(nc.vector.tensor_copy(rw1h[:, :, :], stage[:, :, :]))
            nc.vector.tensor_tensor(rw1l[:, :, :], stage[:, :, :], rw1h[:, :, :].bitcast(F32), ALU.subtract
                                    ).then_inc(c_dve, 2)

            def layer_norm(n, q, iq):
                dve.wait_ge(x_ready[q], 16 * (iq + 1))
                for t in range(TB):
                    o = nc.vector.bn_stats(stats[:, t, :], xb[q][:, t, :])
                link(o)
                dve.sem_inc(dve_passed, 1)
                for t in range(TB):
                    o = nc.vector.bn_aggr(mv[:, t, :], stats[:, t, :])
                link(o)
                nc.vector.tensor_scalar(veps[:, :], mv[:, :, 1], EPS, None, ALU.add).then_inc(var_ready, 1)
                dve.wait_ge(rstd_ready, n + 1)
                dve.wait_ge(scat[q], 16 + 128 * iq)
                for t in range(TB):
                    o = nc.vector.tensor_scalar(xn[q][:, t, 0:C], xb[q][:, t, :], mv[:, t, 0:1], rstd[:, t:t + 1],
                                                ALU.subtract, ALU.mult)
                o.then_inc(ln_done, 1)

            def low(k, n, q):
                dve.wait_ge(hi_done, 2 * n + k + 1)
                nc.vector.tensor_tensor(xTl[q][:, k, :], bT[k][:, :], xTh[q][:, k, :].bitcast(F32), ALU.subtract
                                        ).then_inc(lo_done, 1)

            layer_norm(0, 0, 0)
            dve.wait_ge(c_bias, 1)
            nc.vector.tensor_copy(biasT[:, :], bL[:, 0:9 * MH]).then_inc(c_bias, 1)
            dve.wait_ge(s_wq, 16)
            dve.wait_ge(c_pool, 4)
            for k in range(KC):
                src = wqs[:, k, :].rearrange("p (g j s d) -> p s g d j", s=3, d=DH, j=HG)
                dh = wqh[:, k, 0:2 * C].rearrange("p (s g d j) -> p s g d j", s=2, d=DH, j=HG)
                dl = wql[:, k, 0:2 * C].rearrange("p (s g d j) -> p s g d j", s=2, d=DH, j=HG)
                vsrc = wqs[:, k, :].rearrange("p (h s d) -> p h s d", s=3, d=DH)[:, :, 2, :]
                vdh = wqh[:, k, 2 * C:3 * C].rearrange("p (h d) -> p h d", d=DH)
                vdl = wql[:, k, 2 * C:3 * C].rearrange("p (h d) -> p h d", d=DH)
                for s in range(2):
                    for g in range(NG):
                        nc.vector.tensor_copy(dh[:, s, g, :, :], src[:, s, g, :, :])
                link(nc.vector.tensor_copy(vdh, vsrc))
                for s in range(2):
                    for g in range(NG):
                        nc.vector.tensor_tensor(dl[:, s, g, :, :], src[:, s, g, :, :],
                                                dh[:, s, g, :, :].bitcast(F32), ALU.subtract)
                o = nc.vector.tensor_tensor(vdl, vsrc, vdh.bitcast(F32), ALU.subtract)
            o.then_inc(c_dve, 1)
            for k in range(KC):
                low(k, 0, 0)
            dve.wait_ge(s_load, 16 * 5)
            link(nc.vector.tensor_copy(woh[:, :, :], wos[:, :, :]))
            nc.vector.tensor_tensor(wol[:, :, :], wos[:, :, :], woh[:, :, :].bitcast(F32), ALU.subtract
                                    ).then_inc(c_dve, 1)
            start = chain["n"]

            def bc(ap):
                return ap.rearrange("p (t a) -> p t a", a=1).to_broadcast([P, TB, E])

            with dve.Fori(0, B) as i:
                S_ = small
                chain["base"] = start + i * CHAIN1
                chain["n"] = 0
                for p in range(2):
                    n = 2 * i + p
                    q, iq = next_blk(i, p)
                    for m in range(1, 8, 2):
                        dve.wait_ge(g_ready, 14 * n + m + 1)
                        nc.vector.tensor_scalar(hT[:, m, :], ringG[(14 * p + m) % 4][:, :],
                                                biasT[:, RB + m:RB + m + 1], 0.0, ALU.add, ALU.max).then_inc(g_dve, 1)
                    layer_norm(n + 1, q, iq)
                    dve.wait_ge(l_ready, n + 1)
                    nc.vector.tensor_copy(ltp[:, :], bL[:, :]).then_inc(lt_done, 1)

                    def rest(k):
                        dve.wait_ge(b1_done, 4 * n + k + 1)
                        dve.wait_ge(split_done, 4 * n + k + 1)
                        nc.vector.tensor_tensor(res[k][:, :], ringG[(14 * p + 10 + k) % 4][:, :],
                                                qst[k][:, 0, :], ALU.subtract).then_inc(g_dve, 1)

                    rest(0)
                    dve.wait_ge(s_ready, n + 1)
                    link(nc.vector.tensor_tensor(S_["lg"][:, :, :], bR[:, 0:TB * E].rearrange("p (t e) -> p t e", e=E),
                                                 rb2b[:, :].rearrange("p (a e) -> p a e", a=1).to_broadcast([P, TB, E]),
                                                 ALU.add))
                    for k, (lg, top, f, oh) in enumerate((("lg", "top0", "f0", "oh0"), ("lg2", "top1", "f1", "oh1"))):
                        if k == 1:
                            rest(1)
                            link(nc.vector.scalar_tensor_tensor(S_["lg2"][:, :, :], S_["oh0"][:, :, :], -3.0e38,
                                                                S_["lg"][:, :, :], ALU.mult, ALU.add))
                        link(nc.vector.tensor_reduce(one[top][:, :], S_[lg][:, :, :], AX, ALU.max))
                        link(nc.vector.tensor_tensor(S_["eq"][:, :, :], S_[lg][:, :, :], bc(one[top][:, :]), ALU.is_equal))
                        link(nc.vector.tensor_tensor(S_["cand"][:, :, :], S_["eq"][:, :, :], S_["iota8"][:, :, :], ALU.mult))
                        link(nc.vector.tensor_reduce(one[f][:, :], S_["cand"][:, :, :], AX, ALU.min))
                        link(nc.vector.tensor_tensor(S_[oh][:, :, :], S_["iota8"][:, :, :], bc(one[f][:, :]), ALU.is_equal))
                    nc.vector.tensor_tensor(m8[:, :, :], S_["oh0"][:, :, :], S_["oh1"][:, :, :], ALU.add
                                            ).then_inc(m_ready, 1)
                    nc.vector.tensor_tensor(one["gap"][:, :], one["top1"][:, :], one["top0"][:, :], ALU.subtract
                                            ).then_inc(gap_ready, 1)
                    for c in range(KC):
                        low(c, n + 1, q)
                    rest(2)
                    rest(3)
                    dve.wait_ge(e_done, n + 1)
                    link(nc.vector.tensor_scalar(one["den2"][:, :], one["egap"][:, :], 1.0, None, ALU.add))
                    link(nc.vector.reciprocal(one["w0"][:, :], one["den2"][:, :]))
                    nc.vector.tensor_tensor(S_["pv0"][:, :, :], S_["oh0"][:, :, :], bc(one["w0"][:, :]), ALU.mult)
                    link(nc.vector.tensor_tensor(one["w1"][:, :], one["w0"][:, :], one["egap"][:, :], ALU.mult))
                    link(nc.vector.tensor_tensor(S_["pv1"][:, :, :], S_["oh1"][:, :, :], bc(one["w1"][:, :]), ALU.mult))
                    nc.vector.tensor_tensor(xn[p][:, :, PVC:PVC + E], S_["pv0"][:, :, :], S_["pv1"][:, :, :], ALU.add)
                    link(nc.vector.tensor_copy(xn[p][:, :, TOKC:TOKC + 1].bitcast(U32),
                                               one["tokf"][:, :].rearrange("p (t a) -> p t a", a=1)))
                    link(nc.vector.tensor_scalar(one["tokf"][:, :], one["tokf"][:, :], float(BLK), None, ALU.add))
                    dve.wait_ge(p_ready, n + 1)
                    pos = bR[:, 64:64 + TB * E].rearrange("p (t e) -> p t e", e=E)
                    link(nc.vector.tensor_reduce(msum[:, :], m8[:, :, :].rearrange("p t e -> p e t"), AX, ALU.add))
                    nc.vector.tensor_tensor(carry[:, :], carry[:, :], msum[:, :], ALU.add)
                    nc.vector.tensor_scalar(S_["over"][:, :, :], pos, float(CAP), float(1 << 20), ALU.is_ge, ALU.mult)
                    link(nc.vector.tensor_tensor(S_["place"][:, :, :], pos, S_["slotbase"][:, :, :], ALU.add))
                    nc.vector.tensor_tensor(S_["cand"][:, :, :], S_["place"][:, :, :], S_["over"][:, :, :], ALU.add
                                            ).then_inc(p_read, 1)
                    dve.wait_ge(p_read, n + 2)
                    for k in range(2):
                        o = nc.vector.tensor_tensor(S_[f"sel{k}"][:, :, :], S_[f"oh{k}"][:, :, :], S_["cand"][:, :, :], ALU.mult)
                        if k == 1:
                            link(o)
                    for k in range(2):
                        o = nc.vector.tensor_reduce(slotf[p][:, k, :], S_[f"sel{k}"][:, :, :], AX, ALU.add)
                    link(o)
                    nc.vector.tensor_copy(slots[p][:, :], slotf[p][:, :, :].rearrange("p k t -> p (k t)")
                                          ).then_inc(slot_ready, 1)
                assert chain["n"] == CHAIN1, chain["n"]
            dve.drain().then_inc(phase, 1)

            dve.sem_inc(f_dve, FD)
            dve.sem_inc(s1_max, APART + 2)
            dve.sem_inc(att_done, 2)
            dve.sem_inc(mp_ready, 1)
            for h in range(2):
                dve.sem_inc(m_rows[h], 48)
            for c in range(2):
                dve.sem_inc(att_moved[c], 64)

            def reduce(u, s, j, par):
                qt, kc = STEP1[s]
                nk = 512 if kc < qt // 4 else P * (qt % 4 + 1)
                dve.wait_ge(s1_ready, 48 * u + 4 * s + j + 1)
                dst = mxA[par][:, j, qt:qt + 1] if qt < 4 else mxB[par][:, j, qt - 4, kc:kc + 1]
                bank = bS1[j % 2][:, 0:nk]
                if kc == qt // 4:
                    dve.sem_inc(dve_passed, 1)
                    nc.vector.tensor_tensor_reduce(bank, bank, causal[:, 512 - nk:512], 1.0, LOWEST, ALU.add, ALU.max,
                                                   accum_out=dst).then_inc(s1_max, 1)
                else:
                    nc.vector.tensor_reduce(dst, bank, AX, ALU.max).then_inc(s1_max, 1)

            def max_parts(u, h):
                M = 2 * u + h
                dve.wait_ge(mt_ready, M + 1)
                dve.wait_ge(m_rows[h], 48 * (u + 1))
                nc.vector.tensor_scalar(mparts[h][:, 0, :], bAV[0][0:16, 0:P], -1.0, None, ALU.mult)
                nc.vector.tensor_scalar(nm[:, :], bAV[0][0:16, 0:P], -1.0, None, ALU.mult).then_inc(mn_ready, 1)
                dve.wait_ge(mn_ready, M + 1)
                nc.vector.tensor_tensor(nmr[:, :], nm[:, :], mparts[h][:, 0, :], ALU.subtract).then_inc(mp_step, 1)
                dve.wait_ge(mp_step, 2 * M + 1)
                nc.vector.tensor_copy(mparts[h][:, 1, :], nmr[:, :]).then_inc(mp_step, 1)
                dve.wait_ge(mp_step, 2 * M + 2)
                nc.vector.tensor_tensor(mparts[h][:, 2, :], nmr[:, :], mparts[h][:, 1, :], ALU.subtract
                                        ).then_inc(mp_ready, 1)

            def late_max(u, par):
                dve.wait_ge(s1_max, APART + 2 + 48 * (u + 1))
                nc.vector.tensor_reduce(mxBr[:, :], mxB[par][:, :, :, :].rearrange("p j t k -> p (j t) k"), AX, ALU.max
                                        ).then_inc(mb_ready, 1)

            def attend(u, g, c, stage):
                D = 3 * (2 * u + c)
                if stage == 0:
                    dve.wait_ge(av_done, 2 + NS * u + (4 if c == 0 else 12))
                    dve.wait_ge(att_done, 2 * u + c + 2)
                    nc.vector.transpose(den[:, :], bAV[c][:, :]).then_inc(den_ready, 1)
                if stage == 1:
                    dve.wait_ge(den_ready, D + 1)
                    nc.vector.reciprocal(rsum[:, :], den[:, :].rearrange("p (n r) -> p n r", r=32)[:, :, DH]
                                         ).then_inc(den_ready, 1)
                if stage == 2:
                    dve.wait_ge(den_ready, D + 2)
                    nc.vector.transpose(rden[:, :].rearrange("p (n r) -> p n r", r=32),
                                        rsum[:, :].rearrange("p (n a) -> p n a", a=1).to_broadcast([P, 16, 32])
                                        ).then_inc(den_ready, 1)
                if stage == 3:
                    dve.wait_ge(den_ready, D + 3)
                    dve.wait_ge(att_moved[c], 64 + 64 * u)
                    nc.vector.tensor_tensor(att[c][:, :], bAV[c][:, :], rden[:, :], ALU.mult
                                            ).then_inc(att_done, 1)

            def chunk_rows(i, e):
                nc.vector.tensor_copy(tok[i][:, :], xd[i][:, :, TOKC].bitcast(U32))
                nc.vector.tensor_copy(wgt[i][:, :].rearrange("p (s a) -> p s a", a=1), xd[i][:, :, bass.ds(e + PVC, 1)]
                                      ).then_inc(tok_done, 1)

            def low_chunk(bank):
                return nc.vector.tensor_tensor(dTl[:, :, :], bank[:, :].rearrange("p (k n) -> p k n", k=KC),
                                               dTh[:, :, :].bitcast(F32), ALU.subtract)

            def part(b, g, k):
                u = NG * b + g
                if k == "T":
                    dve.wait_ge(added, add_done(b, ADD[(g - 1, "S1")]) if g else add_done(b, -1))
                    dve.wait_ge(xd_ready[(g + 1) % 2], 16 * (2 * b + (g + 1) // 2 + 1))
                    chunk_rows((g + 1) % 2, b + (g + 1) // NG)
                    dve.wait_ge(dhi_done, u + 2)
                    low_chunk(f_bank(g, k)).then_inc(f_dve, 1)
                if k[0] == "M":
                    max_parts(u if k == "M1" else u + 1, k == "M1")
                if k[0] == "S":
                    r = int(k[1])
                    n = ADD[(g, k)]
                    dve.wait_ge(added, add_done(b, ADD[(g - 1, k)]) if g else add_done(b, -1))
                    dve.wait_ge(eb2_ld, 16 * (b + 1))
                    dve.wait_ge(f_ready, f_full(b, g, k))
                    nc.vector.tensor_tensor(eo[r][:, :], f_bank(g, k)[:, 0:C], eb2b[:, :], ALU.add).then_inc(f_dve, 1)
                    s, v = f_end(b, USE[(g, k)])
                    dve.wait_ge(s, v)
                    nc.vector.tensor_scalar(eo[r][:, :], eo[r][:, :], wgt[g % 2][:, r:r + 1], None, ALU.mult
                                            ).then_inc(eo_ready, 1)

            for s in range(NS):
                for j in range(HG):
                    reduce(0, s, j, 0)
                if s == 6:
                    max_parts(0, 0)
            late_max(0, 0)
            dve.wait_ge(phase, 5)
            dve.wait_ge(xd_ready[0], 16)
            chunk_rows(0, 0)
            dve.wait_ge(dhi_done, 1)
            low_chunk(bAV[1]).then_inc(t_done, 1)
            with dve.Fori(0, B) as b:
                for g in range(NG):
                    u = NG * b + g
                    if g == 0:
                        nc.vector.tensor_copy(ebias[:, :], biasT[:, bass.ds(b * MH, MH)]).then_inc(eb_ready, 1)
                        dve.wait_ge(eb_ready, b + 1)
                    for slot in range(NS * HG):
                        reduce(u + 1, slot // HG, slot % HG, (g + 1) % 2)
                        for k in after(g, slot, "TSM", 1):
                            part(b, g, k)
                        if ATT0 <= slot < ATT0 + 4:
                            attend(u, g, 0, slot - ATT0)
                        if g and ATT1 <= slot < ATT1 + 4:
                            attend(u - 1, g - 1, 1, slot - ATT1)
                    for k in unended(g, "TS", 1):
                        part(b, g, k)
                    dve.wait_ge(mt_ready, 2 * u + 2)
                    late_max(u + 1, (g + 1) % 2)
                    if g == NG - 1:
                        for st in range(4):
                            attend(u, g, 1, st)
                        part(b, g, "S1")

        @block.tensor
        def _(pe):
            mm = nc.tensor.matmul

            def pass3(dst, ah, al, bh, bl, t, first, last):
                a, b = ((ah, bh), (ah, bl), (al, bh))[t]
                return mm(dst, a, b, start=(first and t == 0), stop=(last and t == 2))

            def mm3(dst, ah, al, bh, bl, first, last):
                mm(dst, ah, bh, start=first, stop=False)
                mm(dst, ah, bl, start=False, stop=False)
                return mm(dst, al, bh, start=False, stop=last)

            pe.wait_ge(c_pool, 4)
            pe.wait_ge(s_load, 16 * 5)
            pe.wait_ge(c_dve, 1)
            nc.tensor.transpose(bL[:, 0:9 * MH], brow[:, :], ident[0:9 * MH, 0:9 * MH]).then_inc(c_bias, 1)
            pe.wait_ge(c_bias, 2)

            def transposes(n, q):
                pe.wait_ge(ln_done, n + 2)
                for k in range(KC):
                    for t in range(TB):
                        o = nc.tensor.transpose(bT[k][:, P * t:P * (t + 1)], xn[q][:, t, P * k:P * (k + 1)], ident[:, :])
                o.then_inc(xT_ready, 1)

            transposes(0, 0)
            pe.wait_ge(c_dve, 4)
            with pe.Fori(0, B) as i:
                for p in range(2):
                    n = 2 * i + p
                    q, iq = next_blk(i, p)
                    xh, xl = xTh[p], xTl[p]

                    def free(g):
                        s, v = g_value(n, g - 4)
                        pe.wait_ge(s, v)
                        return ringG[(14 * p + g) % 4]

                    pe.wait_ge(lo_done, 2 * n + 2)
                    for m in range(MH):
                        dst = free(m)
                        for k in range(KC):
                            o = mm3(dst[:, :], rw1h[:, k, P * m:P * (m + 1)], rw1l[:, k, P * m:P * (m + 1)],
                                    xh[:, k, :], xl[:, k, :], k == 0, k == KC - 1)
                        o.then_inc(g_ready, 1)
                    for h in range(2):
                        dst = free(8 + h)
                        for t in range(2):
                            ts = slice(P * (2 * h + t), P * (2 * h + t + 1))
                            for k in range(KC):
                                o = mm3(dst[:, C * t:C * (t + 1)], xh[:, k, ts], xl[:, k, ts],
                                        wqh[:, k, 2 * C:3 * C], wql[:, k, 2 * C:3 * C], k == 0, k == KC - 1)
                        o.then_inc(g_ready, 1)
                    for g in (6, 7):
                        s, v = g_value(n, g)
                        pe.wait_ge(s, v)
                    pe.wait_ge(lt_done, n + 1)
                    for r in range(2):
                        for j in range(4):
                            o = mm(bL[32 * j:32 * j + 32, :], rw2p[:, 4 * r + j, :], hT[:, 4 * r + j, :],
                                   start=(r == 0), stop=(r == 1), tile_position=(0, 32 * j), skip_group_check=True)
                    o.then_inc(l_ready, 1)

                    def qk_tile(k):
                        dst = free(10 + k)
                        for c in range(KC):
                            o = mm3(dst[:, :], wqh[:, c, P * k:P * (k + 1)], wql[:, c, P * k:P * (k + 1)],
                                    xh[:, c, :], xl[:, c, :], c == 0, c == KC - 1)
                        o.then_inc(g_ready, 1)

                    qk_tile(0)
                    pe.wait_ge(lt_done, n + 2)
                    pe.wait_ge(p_read, n + 1)
                    for t in range(TB):
                        o = mm(bR[:, E * t:E * (t + 1)], ltp[:, P * t:P * (t + 1)], sum4[:, :], start=True, stop=True)
                    o.then_inc(s_ready, 1)
                    qk_tile(1)
                    transposes(n + 1, q)
                    qk_tile(2)
                    qk_tile(3)
                    pe.wait_ge(m_ready, n + 1)
                    pos = bR[:, 64:64 + TB * E]
                    for t in range(TB):
                        d = pos[:, E * t:E * (t + 1)]
                        mm(d, before[:, :], m8[:, t, :], start=True, stop=False)
                        for tt in range(t):
                            mm(d, onesb[:, :], m8[:, tt, :], start=False, stop=False)
                        o = mm(d, onesb[:, :], carry[:, :], start=False, stop=True)
                    o.then_inc(p_ready, 1)
            pe.drain().then_inc(phase, 1)

            pe.sem_inc(av_done, 2)

            def s1_chunk(u, s, j, g):
                qt, kc = STEP1[s]
                nk = P * (qt % 4 + 1) if kc == qt // 4 else 512
                pe.wait_ge(s1_max, APART + 48 * u + 4 * s + j + 1)
                bank = bS1[j % 2]
                o = mm(bank[:, 0:nk], qs[g][0:KR, qt // 4, j, P * (qt % 4):P * (qt % 4 + 1)], ks[g][0:KR, kc, j, 0:nk],
                       start=True, stop=True)
                o.then_inc(s1_ready, 1)

            def s2_chunk(u, s, j, g):
                c, kt = STEP2[s]
                q0 = max(P * kt, 512 * c)
                nq = 512 * (c + 1) - q0
                pe.wait_ge(exp_done, 48 * u + 4 * s + j + 1)
                bank = bS2[j % 2]
                o = mm(bank[:, 0:nq], ks[g][0:KR + PARTS, kt // 4, j, P * (kt % 4):P * (kt % 4 + 1)],
                       qs[g][0:KR + PARTS, c, j, q0 - 512 * c:512],
                       start=True, stop=True)
                o.then_inc(s2_ready, 1)

            def av_step(u, s, g):
                c, kt = STEP2[s]
                q0 = max(P * kt, 512 * c)
                nq = 512 * (c + 1) - q0
                if s in DIAG:
                    pe.wait_ge(masked, len(DIAG) * u + DIAG.index(s) + 1)
                else:
                    pe.wait_ge(exp_done, 2 + 48 * u + 4 * s + 4)
                if kt == 0:
                    if c == 0:
                        pe.wait_ge(mn_ready, 2 * u + 2)
                    else:
                        pe.wait_ge(att_done, 2 * u + 2)
                for j in range(HG):
                    o = mm(bAV[c][32 * j:32 * j + 32, q0 - 512 * c:512], vh[g % 2][:, kt, j, :], pt[s % 2][:, j, 0:nq],
                           start=(kt == 0), stop=True, tile_position=(0, 32 * j), skip_group_check=True)
                o.then_inc(av_done, 1)

            def chunk_transpose(dst, buf, i):
                c, st = i // 2, i % 2
                return nc.tensor.transpose(dst[:, CH * c + P * st:CH * c + P * (st + 1)],
                                           xd[buf][:, st, P * c:P * (c + 1)], ident[:, :])

            def wo_pass(dst, r, i):
                t, gg, n = i // 6, i // 3 % 2, i % 3
                ts = slice(P * (2 * r + t), P * (2 * r + t + 1))
                return pass3(dst[:, C * t:C * (t + 1)], atth[:, gg, ts], attl[:, gg, ts], woh[:, gg, :], wol[:, gg, :],
                             n, gg == 0, gg == KC - 1)

            def part(b, g, k, lo, hi):
                u = NG * b + g
                dst = bAV[0] if k[0] == "M" else f_bank(g, k)
                r = int(k[1]) if len(k) > 1 else 0
                if lo == 0:
                    if k == "T":
                        pe.wait_ge(xd_ready[(g + 1) % 2], 16 * (2 * b + (g + 1) // 2 + 1))
                    if k[0] == "M":
                        pe.wait_ge(att_done, 2 * u + (3 if k == "M0" else 1))
                        if k == "M1":
                            pe.wait_ge(mn_ready, 2 * u + 1)
                    if k == "M0":
                        pe.wait_ge(s1_max, APART + 2 + 48 * (u + 1) + 16)
                    if k == "M1":
                        pe.wait_ge(mb_ready, u + 1)
                    if k == "H0":
                        if g == 0:
                            pe.wait_ge(w1_split, 4 * (b + 1))
                        s, v = f_end(b, USE[(g - 1, "T")]) if g else f_end(b - 1, USE[(NG - 1, "T")])
                        pe.wait_ge(s, v)
                    if k == "S0" and g == 0:
                        pe.wait_ge(w2_split, 4 * (b + 1))
                    if k in ("W0", "W2"):
                        pe.wait_ge(att_split, att_value(b - 1, 1, r // 2))
                    if k[0] != "M":
                        s, v = f_end(b, USE[(g, k)] - 2)
                        pe.wait_ge(s, v)
                for i in range(lo, hi):
                    if k == "T":
                        o = chunk_transpose(dst, (g + 1) % 2, i)
                    elif k == "M0":
                        o = nc.tensor.transpose(dst[0:16, 0:P], mxA[(g + 1) % 2][:, :, :].rearrange("p j t -> p (j t)"),
                                                ident[:, :])
                    elif k == "M1":
                        o = nc.tensor.transpose(dst[0:16, 0:P], mxBr[:, :], ident[:, :])
                    elif k[0] == "H":
                        h, c, t = i // 6, i // 3 % 2, i % 3
                        m = 2 * r + h
                        w = slice(H * c + P * m, H * c + P * (m + 1))
                        o = pass3(dst[:, CH * h:CH * (h + 1)], w1h[:, w], w1l[:, w], dTh[:, c, :], dTl[:, c, :],
                                  t, c == 0, c == KC - 1)
                    elif k[0] == "S":
                        m, t = i // 3, i % 3
                        if k == "S0" and i % 6 == 0:
                            pe.wait_ge(h_split, 2 + 4 * u + m // 2 + 1)
                        ss = slice(P * r, P * (r + 1))
                        w = slice(C * m, C * (m + 1))
                        o = pass3(dst[:, 0:C], hh[:, m, ss], hl[:, m, ss], w2h[:, w], w2l[:, w], t, m == 0, m == MH - 1)
                    else:
                        o = wo_pass(dst, r, i)
                if hi == WORK[k[0]]:
                    o.then_inc(mt_ready if k[0] == "M" else f_ready, 1)

            pe.wait_ge(g_act, (2 * B + 2) * GA)
            pe.wait_ge(g_dve, (2 * B + 2) * GD)
            pe.wait_ge(lo_done, 2 * (2 * B + 1))
            pe.wait_ge(qk_ready[0], 192)
            for s in range(NS):
                for j in range(HG):
                    s1_chunk(0, s, j, 0)
                if s == 5:
                    pe.wait_ge(s1_max, APART + 2 + 16)
                    nc.tensor.transpose(bAV[0][0:16, 0:P], mxA[0][:, :, :].rearrange("p j t -> p (j t)"), ident[:, :]
                                        ).then_inc(mt_ready, 1)
            pe.wait_ge(phase, 5)
            pe.wait_ge(xd_ready[0], 16)
            for i in range(WORK["T"]):
                o = chunk_transpose(bAV[1], 0, i)
            o.then_inc(t_ready, 1)
            pe.wait_ge(t_done, 1)
            with pe.Fori(0, B) as b:
                for g in range(NG):
                    u = NG * b + g
                    g1 = (g + 1) % NG
                    pe.wait_ge(qk_ready[g1], 192 * (b + 1 + (g + 1) // NG))
                    pe.wait_ge(v_ready[g % 2], 16 * (2 * b + g // 2 + 1))
                    pe.wait_ge(m_rows[0], 48 * (u + 2))
                    for slot in range(NS * HG):
                        s, j = slot // HG, slot % HG
                        if slot == 4 * HG:
                            pe.wait_ge(m_rows[1], 48 * (u + 2))
                        s2_chunk(u, s, j, g)
                        s1_chunk(u + 1, s, j, g1)
                        if j == 3 and s > 0:
                            av_step(u, s - 1, g)
                        if slot == 1 and g:
                            av_step(u - 1, NS - 1, g - 1)
                        for k, lo, hi in slices(g, slot):
                            part(b, g, k, lo, hi)
                    if g == NG - 1:
                        part(b, g, "S1", 0, 4)
                        av_step(u, NS - 1, g)
                        part(b, g, "S1", 4, WORK["S"])
            for r in range(4):
                pe.wait_ge(att_split, att_value(B - 1, 1, r // 2))
                s, v = f_end(B - 1, FU - 2 + r) if r < 2 else (f_act, (B + 1) * FA + r - 1)
                pe.wait_ge(s, v)
                for i in range(WORK["W"]):
                    o = wo_pass(ringF[r % 2], r, i)
                o.then_inc(f_ready, 1)


CHAIN1 = 48

_INS = ['L0_attn_x', 'L0_attn_w_qkv', 'L0_attn_w_o', 'L0_ffn_rw1', 'L0_ffn_rb1', 'L0_ffn_rw2', 'L0_ffn_rb2',
        'L0_ffn_ew1', 'L0_ffn_eb1', 'L0_ffn_ew2', 'L0_ffn_eb2']
_OUTS = [((8, 1024, 256), 'float32')]


def kernel(**inputs):
    import numpy as _np
    import concourse.bacc as _bacc
    from concourse import mybir as _mybir
    from concourse.bass_utils import run_bass_kernel_spmd as _run

    nc = _bacc.Bacc("TRN2", target_bir_lowering=False, num_devices=1)
    arrays, args = {}, []
    for name in _INS:
        a = _np.ascontiguousarray(inputs[name])
        arrays[f"in_{name}_dram"] = a
        args.append(nc.dram_tensor(f"in_{name}_dram", a.shape, _mybir.dt.from_np(a.dtype), kind="ExternalInput").ap())
    for i, (shape, dtype) in enumerate(_OUTS):
        dt = _mybir.dt.from_np(_np.dtype(dtype))
        args.append(nc.dram_tensor(f"out_{i}_dram", shape, dt, kind="ExternalOutput").ap())
    layer_kernel(nc, *args)
    r = _run(nc, [arrays], core_ids=[0])
    got = tuple(r.results[0][f"out_{i}_dram"] for i in range(len(_OUTS)))
    return got[0]
```
